# Optimizing a Trainium2 kernel written in Bass

```python
import numpy as np
import jax
import jax.numpy as jnp

def _softmax(x, axis=-1):
    return jax.nn.softmax(x, axis=axis)

def _gelu(x):
    return jax.nn.gelu(x, approximate=True)

def _silu(x):
    return jax.nn.silu(x)

def _sigmoid(x):
    return jax.nn.sigmoid(x)

def _layernorm(x, axis=-1, eps=1e-05):
    m = jnp.mean(x, axis=axis, keepdims=True)
    v = jnp.var(x, axis=axis, keepdims=True)
    return (x - m) / jnp.sqrt(v + eps)

def _scatter_add(tgt, idx, src, axis=0):
    return tgt.at[idx].add(src)

def _segment_sum(src, seg, n):
    return jax.ops.segment_sum(src, seg, n)
kernel_name = 'mk_gps_d1_gnn_r8_841c73'

def setup_inputs(seed: int=0):
    np.random.seed(seed)
    _w = jnp.asarray

    def _rec_inputs():
        import jax
        import jax.numpy as jnp
        _gk = jax.random.key(seed)
        x = -0.0006008 + 1.001 * jax.random.normal(jax.random.fold_in(_gk, 1), (6250, 256), jnp.float32)
        src = jax.random.randint(jax.random.fold_in(_gk, 2), (100000,), 0, 6250, jnp.int32)
        dst = jax.random.randint(jax.random.fold_in(_gk, 3), (100000,), 0, 6250, jnp.int32)
        _o = jnp.argsort(dst, stable=True)
        src = src[_o]
        dst = dst[_o]
        return (x, src, dst)
    x, src, dst = _rec_inputs()

    def _L0_gnn_setup():
        import jax, jax.numpy as jnp
        import numpy as np
        N_NODES = 1250
        N_EDGES = 40000
        D_IN = 256
        D_OUT = 256
        NEG_SLOPE = 0.2
        key = jax.random.key(seed)
        ks = jax.random.split(key, 8)
        feature = jax.random.normal(ks[0], (N_NODES, D_IN), dtype=jnp.float32)
        src = jax.random.randint(ks[1], (N_EDGES,), 0, N_NODES, dtype=jnp.int32)
        dst = jax.random.randint(ks[2], (N_EDGES,), 0, N_NODES, dtype=jnp.int32)
        s = 1.0 / np.sqrt(D_IN)
        W_s = jax.random.normal(ks[3], (D_OUT, D_IN), dtype=jnp.float32) * s
        W_t = jax.random.normal(ks[4], (D_OUT, D_IN), dtype=jnp.float32) * s
        W_attn = jax.random.normal(ks[5], (1, D_OUT), dtype=jnp.float32) * (1.0 / np.sqrt(D_OUT))
        W_fc = jax.random.normal(ks[6], (D_OUT, D_IN), dtype=jnp.float32) * s
        b_fc = jnp.zeros((D_OUT,), dtype=jnp.float32)
        return {'feature': feature, 'src': src, 'dst': dst, 'W_s': W_s, 'W_t': W_t, 'W_attn': W_attn, 'W_fc': W_fc, 'b_fc': b_fc}
    _L0_gnn_all = _L0_gnn_setup()
    _L0_gnn_in = {k: v for k, v in _L0_gnn_all.items() if k in ('W_s', 'W_t', 'W_attn', 'W_fc', 'b_fc')}
    del _L0_gnn_all

    def _L0_mix_setup():
        import jax, jax.numpy as jnp
        import numpy as np
        HEADS, DIM_HEAD = (8, 64)
        EPS = 1e-05

        def instance_norm(t):
            mu = jnp.mean(t, axis=-1, keepdims=True)
            var = jnp.mean((t - mu) ** 2, axis=-1, keepdims=True)
            return (t - mu) * jax.lax.rsqrt(var + EPS)
        key = jax.random.key(seed)
        k1, k2, k3, k4 = jax.random.split(key, 4)
        B, N, D = (8, 1024, 256)
        inner = HEADS * DIM_HEAD
        x = jax.random.normal(k1, (B, N, D), jnp.float32)
        w_qkv = jax.random.normal(k2, (3 * inner, D), jnp.float32) / np.sqrt(D).astype(np.float32)
        w_out = jax.random.normal(k3, (D, inner), jnp.float32) / np.sqrt(inner).astype(np.float32)
        b_out = 0.01 * jax.random.normal(k4, (D,), jnp.float32)
        return {'x': x, 'w_qkv': w_qkv, 'w_out': w_out, 'b_out': b_out}
    _L0_mix_all = _L0_mix_setup()
    _L0_mix_in = {k: v for k, v in _L0_mix_all.items() if k in ('w_qkv', 'w_out', 'b_out')}
    del _L0_mix_all

    def _L0_ffn_setup():
        import math
        import jax, jax.numpy as jnp
        import numpy as np
        CAPACITY_FACTOR = 1.25
        key = jax.random.key(seed)
        ks = jax.random.split(key, 5)
        B, L, D, F, E = (8, 1024, 256, 1024, 8)
        h = jax.random.normal(ks[0], (B, L, D), dtype=jnp.float32)
        gate_w = jax.random.normal(ks[1], (D, E), dtype=jnp.float32) * 0.02
        gate_b = jnp.zeros((E,), dtype=jnp.float32)
        w1 = jax.random.normal(ks[2], (E, D, F), dtype=jnp.float32) * (1.0 / math.sqrt(D))
        b1 = jnp.zeros((E, F), dtype=jnp.float32)
        w2 = jax.random.normal(ks[3], (E, F, D), dtype=jnp.float32) * (1.0 / math.sqrt(F))
        b2 = jnp.zeros((E, D), dtype=jnp.float32)
        return {'h': h, 'gate_w': gate_w, 'gate_b': gate_b, 'w1': w1, 'b1': b1, 'w2': w2, 'b2': b2}
    _L0_ffn_all = _L0_ffn_setup()
    _L0_ffn_in = {k: v for k, v in _L0_ffn_all.items() if k in ('gate_w', 'gate_b', 'w1', 'b1', 'w2', 'b2')}
    del _L0_ffn_all
    return {'x': x, 'src': src, 'dst': dst, 'L0_gnn_W_s': _L0_gnn_in['W_s'], 'L0_gnn_W_t': _L0_gnn_in['W_t'], 'L0_gnn_W_attn': _L0_gnn_in['W_attn'], 'L0_gnn_W_fc': _L0_gnn_in['W_fc'], 'L0_gnn_b_fc': _L0_gnn_in['b_fc'], 'L0_mix_w_qkv': _L0_mix_in['w_qkv'], 'L0_mix_w_out': _L0_mix_in['w_out'], 'L0_mix_b_out': _L0_mix_in['b_out'], 'L0_ffn_gate_w': _L0_ffn_in['gate_w'], 'L0_ffn_gate_b': _L0_ffn_in['gate_b'], 'L0_ffn_w1': _L0_ffn_in['w1'], 'L0_ffn_b1': _L0_ffn_in['b1'], 'L0_ffn_w2': _L0_ffn_in['w2'], 'L0_ffn_b2': _L0_ffn_in['b2']}

def reference(x, src, dst, L0_gnn_W_s, L0_gnn_W_t, L0_gnn_W_attn, L0_gnn_W_fc, L0_gnn_b_fc, L0_mix_w_qkv, L0_mix_w_out, L0_mix_b_out, L0_ffn_gate_w, L0_ffn_gate_b, L0_ffn_w1, L0_ffn_b1, L0_ffn_w2, L0_ffn_b2):
    import jax
    import jax.numpy as jnp

    def _L0_gnn_ref(feature, src, dst, W_s, W_t, W_attn, W_fc, b_fc):
        import jax, jax.numpy as jnp
        import numpy as np
        N_NODES = 1250
        N_EDGES = 40000
        D_IN = 256
        D_OUT = 256
        NEG_SLOPE = 0.2
        n = feature.shape[0]
        proj_s = feature @ W_s.T
        proj_t = feature @ W_t.T
        z = proj_s[src] + proj_t[dst]
        z = jnp.where(z >= 0, z, NEG_SLOPE * z)
        e = (z @ W_attn.T)[:, 0]
        m = jax.ops.segment_max(e, src, num_segments=n)
        m = jnp.where(jnp.isfinite(m), m, 0.0)
        e_exp = jnp.exp(e - m[src])
        denom = jax.ops.segment_sum(e_exp, src, num_segments=n)
        alpha = e_exp / denom[src]
        msg = feature[src] * alpha[:, None]
        agg = jax.ops.segment_sum(msg, dst, num_segments=n)
        return agg @ W_fc.T + b_fc

    def _L0_mix_ref(x, w_qkv, w_out, b_out):
        import jax, jax.numpy as jnp
        import numpy as np
        HEADS, DIM_HEAD = (8, 64)
        EPS = 1e-05

        def instance_norm(t):
            mu = jnp.mean(t, axis=-1, keepdims=True)
            var = jnp.mean((t - mu) ** 2, axis=-1, keepdims=True)
            return (t - mu) * jax.lax.rsqrt(var + EPS)
        B, N, _ = x.shape
        H, Dh = (HEADS, DIM_HEAD)
        qkv = jnp.einsum('bnd,ed->bne', x, w_qkv)
        q, k, v = jnp.split(qkv, 3, axis=-1)

        def to_heads(t):
            return t.reshape(B, N, H, Dh).transpose(0, 2, 1, 3)
        q, k, v = (to_heads(q), to_heads(k), to_heads(v))
        k = instance_norm(k)
        v = instance_norm(v)
        dots = jnp.einsum('bhnd,bhne->bhde', k, v)
        out = jnp.einsum('bhnd,bhde->bhne', q, dots) / N
        out = out.transpose(0, 2, 1, 3).reshape(B, N, H * Dh)
        return jnp.einsum('bne,de->bnd', out, w_out) + b_out

    def _L0_ffn_ref(h, gate_w, gate_b, w1, b1, w2, b2):
        import math
        import jax, jax.numpy as jnp
        import numpy as np
        CAPACITY_FACTOR = 1.25
        B, L, D = h.shape
        E = gate_w.shape[1]
        T = B * L
        C = max(1, math.ceil(CAPACITY_FACTOR * T / E))
        x = h.reshape(T, D)
        logits = x @ gate_w + gate_b
        probs = jax.nn.softmax(logits, axis=-1)
        idx = jnp.argmax(probs, axis=-1)
        prb = jnp.take_along_axis(probs, idx[:, None], axis=1)[:, 0]
        one_hot = jax.nn.one_hot(idx, E, dtype=jnp.float32)
        pos = (jnp.cumsum(one_hot, axis=0) * one_hot).sum(-1).astype(jnp.int32) - 1
        kept = pos < C
        pos_safe = jnp.where(kept, pos, C)
        buf = jnp.zeros((E, C, D), dtype=h.dtype).at[idx, pos_safe].set(x, mode='drop')
        hmid = jax.nn.relu(jnp.einsum('ecd,edf->ecf', buf, w1) + b1[:, None, :])
        ybuf = jnp.einsum('ecf,efd->ecd', hmid, w2) + b2[:, None, :]
        pos_g = jnp.minimum(pos, C - 1)
        y_tok = ybuf[idx, pos_g] * (prb * kept)[:, None]
        y = y_tok.reshape(B, L, D)
        y = jnp.nan_to_num(y, nan=0.0, posinf=10000.0, neginf=-10000.0)
        return y
    xn = _layernorm(x, axis=-1)
    x = x + _L0_gnn_ref(xn, src, dst, L0_gnn_W_s, L0_gnn_W_t, L0_gnn_W_attn, L0_gnn_W_fc, L0_gnn_b_fc) + _L0_mix_ref(xn[None], L0_mix_w_qkv, L0_mix_w_out, L0_mix_b_out)[0]
    x = x + _L0_ffn_ref(_layernorm(x, axis=-1)[None], L0_ffn_gate_w, L0_ffn_gate_b, L0_ffn_w1, L0_ffn_b1, L0_ffn_w2, L0_ffn_b2)[0]
    return x

_drawn_inputs = setup_inputs


def setup_inputs(seed=0):
    import zlib

    import numpy as np

    out = dict(_drawn_inputs(seed))
    spreads = {'L0_gnn_b_fc': (0.0, 0.1),
     'L0_ffn_gate_b': (0.0, 0.1),
     'L0_ffn_b1': (0.0, 0.723),
     'L0_ffn_b2': (0.0, 0.51)}
    factors = {'L0_mix_b_out': 4.961}
    for name, (base, spread) in spreads.items():
        noise = np.random.default_rng([zlib.crc32(name.encode()), seed]).standard_normal(out[name].shape)
        drawn = base * np.exp(spread * noise) if base else spread * noise
        out[name] = jnp.asarray(drawn.astype(out[name].dtype))
    for name, factor in factors.items():
        out[name] = (out[name] * factor).astype(out[name].dtype)
    return out
```

```python
import concourse.bass as bass
from concourse import mybir
from contextlib import ExitStack

F32 = mybir.dt.float32
I32 = mybir.dt.int32
ALU = mybir.AluOpType
ACT = mybir.ActivationFunctionType
AX = mybir.AxisListType

P = 128
FLOAT_MAX = 3.4028234663852886e38
BIG = 1.0e30
LN_EPS = 1e-5
SLOPE = 0.2


class Steps:

    def __init__(self, eng, sem):
        self.eng, self.sem, self.base, self.n = eng, sem, 0, 0

    def enter(self, i, first, per_pass):
        self.start, self.per_pass = self.base + self.n, per_pass
        self.base, self.n = self.start + (i - first) * per_pass, 0

    def leave(self, passes):
        assert self.n == self.per_pass, (self.n, self.per_pass)
        self.base, self.n = self.start + passes * self.per_pass, 0

    def done(self, ins):
        self.n += 1
        return ins.then_inc(self.sem, 1)

    def wait(self, but=0):
        self.eng.wait_ge(self.sem, self.base + self.n - but)

    def hold(self, past):
        hold(self.eng, self.sem, self.base + self.n, past)

    def then(self, ins):
        self.done(ins)
        self.wait()


def rsqrt(v, steps, out, value, scratch):
    steps.then(v.tensor_scalar(out.bitcast(I32), value.bitcast(I32), -0.5, float(0x5f3759df), ALU.mult, ALU.add))
    for _ in range(3):
        steps.then(v.tensor_tensor(scratch, out, out, ALU.mult))
        steps.then(v.scalar_tensor_tensor(out=scratch, in0=scratch, scalar=-0.5, in1=value, op0=ALU.mult, op1=ALU.mult))
        steps.then(v.scalar_tensor_tensor(out=out, in0=scratch, scalar=1.5, in1=out, op0=ALU.add, op1=ALU.mult))


RSQRT_STEPS = 10


def wait(eng, sem, value):
    if not isinstance(value, int) or value > 0:
        eng.wait_ge(sem, value)


def hold(eng, sem, value, held):
    if not isinstance(value, int) or value > 0:
        eng.wait_ge(sem, value)
        eng.sem_inc(held, 1)


def at(v, t):
    if isinstance(t, int):
        return v[:, t, :]
    return v[:, bass.ds(t, 1), :].rearrange("p a c -> p (a c)")


def span(t, n):
    return slice(t, t + n) if isinstance(t, int) else bass.ds(t, n)


def graph_transformer_kernel(nc, x, src, dst, W_s, W_t, W_attn, W_fc, b_fc, w_qkv, w_out, b_out,
                             gate_w, gate_b, w1, b1, w2, b2, out):
    N, D = x.shape
    E = src.shape[0]
    NT = (N + P - 1) // P
    NP = NT * P
    TAIL = N - (NT - 1) * P
    PAD_NODE = NP - 1
    HALF = 8
    PASS = 2 * HALF
    PASSES = (E + P * PASS - 1) // (P * PASS)
    ET = PASSES * PASS
    HALVES = 2 * PASSES
    EC = ET + PASS
    FULL_B = E // (P * P)
    FULL_T = E // P - FULL_B * P
    REST = E % P
    ZW = D + 2
    HEADS, DH = 8, 64
    INNER = HEADS * DH
    PAIRS = INNER // P
    NE, _, F = w1.shape
    FT = F // P
    CAP = max(1, -(-5 * N // (4 * NE)))
    CT = (CAP + P - 1) // P
    SLOTS = CT * P
    DC = D // P
    TABW = 3 * NT
    ROWW = D + 2
    ACCS = 4
    ACC_ROWS = NP + P
    assert DC == 2 and NT == PASSES

    proj_s = nc.dram_tensor("proj_s", (NP, ZW), F32, kind="Internal").ap()
    proj_t = nc.dram_tensor("proj_t", (NP, ZW), F32, kind="Internal").ap()
    node_rows = nc.dram_tensor("node_rows", (NP, ROWW), F32, kind="Internal").ap()
    padded = nc.dram_tensor("padded_edges", (2, ET * P), I32, kind="Internal").ap()
    acc = [nc.dram_tensor(f"acc{a}", (ACC_ROWS, D), F32, kind="Internal").ap() for a in range(ACCS)]
    moe_in = nc.dram_tensor("moe_in", (NE * SLOTS + NP, D), F32, kind="Internal").ap()
    moe_out = nc.dram_tensor("moe_out", (NE * SLOTS, D), F32, kind="Internal").ap()

    with ExitStack() as ctx:
        def sb(name, shape, dt=F32):
            return ctx.enter_context(nc.sbuf_tensor(name, shape, dt))

        def sem(name):
            return ctx.enter_context(nc.semaphore(name))

        s_held = sem("held")
        psum = ctx.enter_context(nc.psum_tensor("psum", [P, 8, 512], F32))

        x_all = sb("x_all", [P, NT, D])
        xn_all = sb("xn_all", [P, NT, D])
        edges = sb("edges", [P, 2, EC], I32)
        attr = sb("attr", [P, 3, EC])
        dst_f = sb("dst_f", [P, EC])
        score_all = sb("score_all", [P, EC])
        ident = sb("ident", [P, P])
        below = sb("below", [P, P])
        above = sb("above", [P, P])
        ones = sb("ones", [P, P])
        count_i = sb("count_i", [P, P], I32)
        count = sb("count", [P, P])
        trash_i = sb("trash_i", [P, 1], I32)
        row_id = sb("row_id", [P, 1])
        attn = sb("attn", [P, ZW])
        attn_col = sb("attn_col", [P, DC])
        win_base = sb("win_base", [P, HALVES + 2])
        win_nodes = sb("win_nodes", [P, HALVES], I32)
        win_rows = sb("win_rows", [P, HALVES], I32)
        fits = sb("fits", [P, 1], I32)
        bias_row = sb("bias_row", [1, 2, D])
        w3T = sb("w3T", [P, DC, 3 * D])
        wkvT = sb("wkvT", [P, DC, 2 * INNER])
        woutT = sb("woutT", [P, PAIRS, D])
        wq = sb("wq", [P, PAIRS, D])
        gw = sb("gw", [P, DC, NE])
        gb = sb("gb", [P, NE])
        b1T = sb("b1T", [P, NE * FT])
        tab_max = sb("tab_max", [P, NT])
        tab_sum = sb("tab_sum", [P, NT])
        max_rsum = sb("max_rsum", [P, NT, 2])
        zeros = sb("zeros", [P, 512])
        gate_prob = sb("gate_prob", [P, NT])
        slot_in = sb("slot_in", [P, NT], I32)
        slot_out = sb("slot_out", [P, NT], I32)
        pool_mem = sb("pool_mem", [P, 13800])

        def windowed(eng):
            return eng.value_load(fits[0:1, 0:1], min_val=0, max_val=1)

        class Arena:
            def __init__(self):
                self.at = 0

            def take(self, *shape):
                n = 1
                for s in shape:
                    n *= s
                v = pool_mem[:, self.at:self.at + n]
                self.at += n
                assert self.at <= 13800, self.at
                if len(shape) == 2:
                    v = v.rearrange("p (a b) -> p a b", b=shape[1])
                if len(shape) == 3:
                    v = v.rearrange("p (a b c) -> p a b c", b=shape[1], c=shape[2])
                return v

        m = Arena()
        w3_raw = m.take(3 * DC, D)
        kv_raw = m.take(2 * INNER // P, D)
        wout_raw = m.take(DC, INNER)
        b1_raw = m.take(P)
        stats = m.take(2, 6)
        mean_var = m.take(NT, 2)
        pair = m.take(2, 2)
        variance = m.take(NT)
        rstd = m.take(NT)
        scratch = m.take(NT)
        xn = m.take(2, D)
        xnT = m.take(2, D)
        proj = m.take(2, 3, ZW)
        lin_out = m.take(4, D)
        headmean = m.take(DC, 2 * HEADS)
        hi_i = m.take(EC).bitcast(I32)
        raw_e = m.take(2, FULL_B + 1, P).bitcast(I32)
        raw_f = m.take(2, FULL_B + 1, P)
        dst_range = m.take(2, HALVES)
        extremes = m.take(2)
        misfit = m.take(1)
        diagonal = m.take(HALVES)
        window_f = m.take(HALVES)

        s_fill, s_x, s_edges, s_w = sem("fills_done"), sem("x_loaded"), sem("edges_loaded"), sem("weights_loaded")
        s_const, s_pool, s_dve = sem("constants_made"), sem("pool_steps"), sem("dve_steps")
        s_wt, s_wc = sem("weights_transposed"), sem("weights_copied")
        s_xn, s_tp, s_xt = sem("xn_ready"), sem("xn_transposed"), sem("xnT_ready")
        s_pj, s_pc, s_lin = sem("proj_ready"), sem("proj_copied"), sem("linear_terms_done")
        s_st = [sem(f"proj_stored{i}") for i in range(2)]
        s_rf, s_et, s_ec = sem("raw_edges_float"), sem("edges_transposed"), sem("edges_copied")
        s_range, s_rangeT, s_ends, s_base = sem("ranges_ready"), sem("ranges_transposed"), sem("extremes_ready"), sem("bases_broadcast")
        LOADS = 12

        jobs = []
        for c in range(DC):
            for w in range(3 * DC):
                jobs.append((w3_raw[:, w, c * P:(c + 1) * P], w3T[:, c, w * P:(w + 1) * P]))
        FIRST = len(jobs)
        for c in range(DC):
            for w in range(2 * INNER // P):
                jobs.append((kv_raw[:, w, c * P:(c + 1) * P], wkvT[:, c, w * P:(w + 1) * P]))
        for g in range(PAIRS):
            for c in range(DC):
                jobs.append((wout_raw[:, c, g * P:(g + 1) * P], woutT[:, g, c * P:(c + 1) * P]))
        GROUPS = len(jobs) // 4
        dve = Steps(nc.vector, s_dve)

        with nc.Block() as block:
            @block.sync
            def _(sp):
                sp.wait_ge(s_fill, 2)
                for j, e in enumerate((src, dst)):
                    sp.dma_start(raw_e[:, j, 0:FULL_B, :], e[0:FULL_B * P * P].rearrange("(b p c) -> p b c", p=P, c=P)).then_inc(s_edges, 16)
                    sp.dma_start(raw_e[0:FULL_T, j, FULL_B, :], e[FULL_B * P * P:FULL_B * P * P + FULL_T * P].rearrange("(p c) -> p c", c=P)).then_inc(s_edges, 16)
                    sp.dma_start(raw_e[FULL_T:FULL_T + 1, j, FULL_B, 0:REST], e[E - REST:E].rearrange("(p c) -> p c", p=1)).then_inc(s_edges, 16)
                sp.dma_start(x_all[:, 0:NT - 1, :], x[0:(NT - 1) * P, :].rearrange("(t p) c -> p t c", p=P)).then_inc(s_x, 16)
                sp.dma_start(x_all[0:TAIL, NT - 1, :], x[(NT - 1) * P:N, :]).then_inc(s_x, 16)
                for i, w in enumerate((W_s, W_t, W_fc)):
                    sp.dma_start(w3_raw[:, 2 * i:2 * i + 2, :], w.rearrange("(o p) c -> p o c", p=P)).then_inc(s_w, 16)
                sp.dma_start(kv_raw, w_qkv[INNER:3 * INNER, :].rearrange("(o p) c -> p o c", p=P)).then_inc(s_w, 16)
                sp.dma_start(wout_raw, w_out.rearrange("(o p) c -> p o c", p=P)).then_inc(s_w, 16)
                sp.dma_start(b1_raw[0:NE * FT, :], b1.rearrange("e (f p) -> (e f) p", p=P)).then_inc(s_w, 16)
                sp.dma_start(wq[:, :, :], w_qkv[0:INNER, :].rearrange("(o p) c -> p o c", p=P)).then_inc(s_w, 16)
                sp.dma_start(attn[:, 0:D], W_attn[0, :].partition_broadcast(P)).then_inc(s_w, 16)
                sp.dma_start(gw[:, :, :], gate_w.rearrange("(c p) e -> p c e", p=P)).then_inc(s_w, 16)
                sp.dma_start(gb[:, :], gate_b.partition_broadcast(P)).then_inc(s_w, 16)
                sp.dma_start(bias_row[:, 0, :], b_fc.rearrange("(a c) -> a c", a=1)).then_inc(s_w, 16)
                sp.dma_start(bias_row[:, 1, :], b_out.rearrange("(a c) -> a c", a=1)).then_inc(s_w, 16)

                def store(t, slot):
                    wait(sp, s_pc, 2 * t + 2)
                    wait(sp, s_lin, 4 * t + 4)
                    rows = span(t * P, P)
                    sp.dma_start(proj_s[rows, :], proj[:, slot, 0, :]).then_inc(s_st[slot], 16)
                    sp.dma_start(proj_t[rows, :], proj[:, slot, 1, :]).then_inc(s_st[slot], 16)
                    sp.dma_start(node_rows[rows, 0:D], proj[:, slot, 2, 0:D]).then_inc(s_st[slot], 16)

                with sp.Fori(0, NT // 2) as i:
                    store(2 * i, 0)
                    store(2 * i + 1, 1)
                store(NT - 1, 0)
                for j in range(2):
                    sp.dma_start(padded[j, 0:FULL_B * P * P].rearrange("(b p c) -> p b c", p=P, c=P), raw_e[:, j, 0:FULL_B, :]).then_inc(s_edges, 16)
                    sp.dma_start(padded[j, FULL_B * P * P:ET * P].rearrange("(p c) -> p c", c=P), raw_e[0:ET - FULL_B * P, j, FULL_B, :]).then_inc(s_edges, 16)
                sp.wait_ge(s_edges, 16 * 10)
                sp.wait_ge(s_st[0], 48 * (NT // 2 + 1))
                sp.wait_ge(s_st[1], 48 * (NT // 2))

            @block.gpsimd
            def _(g):
                st = Steps(g, s_pool)
                st.done(g.memset(ident[:, :], 0.0))
                st.done(g.memset(below[:, :], 0.0))
                st.done(g.memset(above[:, :], 0.0))
                st.done(g.iota(count_i[:, :], [[1, P]], base=0, channel_multiplier=0))
                st.then(g.iota(trash_i[:, :], [[0, 1]], base=0, channel_multiplier=1))
                g.affine_select(out=ident[:, :], in_=ident[:, :], compare_op=ALU.not_equal, fill=1.0, base=0,
                                pattern=[[-1, P]], channel_multiplier=1).then_inc(s_const, 1)
                g.affine_select(out=below[:, :], in_=below[:, :], compare_op=ALU.is_ge, fill=1.0, base=0,
                                pattern=[[1, P]], channel_multiplier=-1).then_inc(s_const, 1)
                g.affine_select(out=above[:, :], in_=above[:, :], compare_op=ALU.is_ge, fill=1.0, base=0,
                                pattern=[[-1, P]], channel_multiplier=1).then_inc(s_const, 1)

            @block.vector
            def _(v):
                v.memset(x_all[96:P, NT - 1, :], 0.0).then_inc(s_fill, 1)
                v.memset(raw_e, PAD_NODE).then_inc(s_fill, 1)
                dve.done(v.memset(ones[:, :], 1.0))
                dve.done(v.memset(attn[:, D:D + 1], 1.0))
                dve.done(v.memset(attn[:, D + 1:ZW], -1.0))
                dve.done(v.memset(zeros[:, :], 0.0))
                dve.done(v.memset(score_all[:, :], 0.0))
                dve.done(v.memset(tab_max[:, :], -BIG))
                dve.done(v.memset(tab_sum[:, :], 0.0))
                v.wait_ge(s_edges, 96)
                v.tensor_copy(raw_f, raw_e).then_inc(s_rf, 1)
                v.wait_ge(s_x, 32)

                def measure(t, slot):
                    dve.done(v.bn_stats(stats[:, slot, :], at(x_all, t)))
                    dve.hold(s_held)
                    dve.then(v.bn_aggr(pair[:, slot, :], stats[:, slot, :]))
                    dve.done(v.tensor_copy(at(mean_var, t), pair[:, slot, :]))

                measure(0, 0)
                with v.Fori(0, NT // 2) as i:
                    dve.enter(i, 0, 6)
                    measure(2 * i + 1, 1)
                    measure(2 * i + 2, 0)
                dve.leave(NT // 2)
                dve.wait()
                dve.then(v.tensor_scalar(variance, mean_var[:, :, 1], LN_EPS, None, ALU.add))
                rsqrt(v, dve, rstd, variance, scratch)

                def norm(t, slot):
                    wait(v, s_tp, t - 1)
                    v.tensor_scalar(xn[:, slot, :], at(x_all, t), at(mean_var, t)[:, 0:1], rstd[:, span(t, 1)],
                                    ALU.subtract, ALU.mult).then_inc(s_xn, 1)

                def linear(t, slot):
                    wait(v, s_pc, 2 * t + 1)
                    wait(v, s_lin, 4 * t)
                    for w in range(2):
                        for k, sign in ((0, 1.0), (1, -1.0)):
                            v.tensor_tensor_reduce(lin_out[:, 2 * w + k, :], proj[:, slot, w, 0:D], attn[:, 0:D],
                                                   sign * SLOPE / (1.0 - SLOPE), 0.0, ALU.mult, ALU.add,
                                                   proj[:, slot, w, D + k:D + k + 1]).then_inc(s_lin, 1)

                norm(0, 0)
                norm(1, 1)
                norm(2, 0)
                linear(0, 0)
                norm(3, 1)
                linear(1, 1)
                with v.Fori(1, NT // 2 - 1) as i:
                    norm(2 * i + 2, 0)
                    linear(2 * i, 0)
                    norm(2 * i + 3, 1)
                    linear(2 * i + 1, 1)
                norm(NT - 1, 0)
                linear(NT - 3, 0)
                linear(NT - 2, 1)
                linear(NT - 1, 0)

                v.wait_ge(s_pool, 5)
                dve.done(v.tensor_copy(count[:, :], count_i[:, :]))
                dve.done(v.tensor_copy(row_id[:, :], trash_i[:, :]))
                dve.done(v.memset(attr[:, 0, ET:EC], PAD_NODE))
                dve.done(v.memset(dst_f[:, ET:EC], PAD_NODE))
                for b in range(FULL_B + 1):
                    n = min(P, ET - b * P)
                    v.wait_ge(s_et, b + 1)
                    dve.done(v.tensor_copy(attr[:, 0, b * P:b * P + n], psum[:, b % 2, 0:n]))
                    dve.then(v.tensor_copy(dst_f[:, b * P:b * P + n], psum[:, b % 2, P:P + n]))
                    v.sem_inc(s_ec, 1)
                dve.done(v.tensor_copy(edges[:, 0, :], attr[:, 0, :]))
                dve.then(v.tensor_copy(edges[:, 1, :], dst_f[:, :]))
                dve.then(v.tensor_scalar(hi_i, edges[:, 0, :], P.bit_length() - 1, None, ALU.arith_shift_right))
                dve.then(v.tensor_copy(attr[:, 1, :], hi_i))
                dve.then(v.scalar_tensor_tensor(out=attr[:, 2, :], in0=attr[:, 1, :], scalar=-float(P), in1=attr[:, 0, :],
                                                op0=ALU.mult, op1=ALU.add))
                by_half = dst_f[:, 0:ET].rearrange("p (k t) -> p k t", t=HALF)
                v.tensor_reduce(dst_range[:, 0, :], by_half, AX.X, ALU.min).then_inc(s_range, 1)
                v.tensor_reduce(dst_range[:, 1, :], by_half, AX.X, ALU.max).then_inc(s_range, 1)
                v.wait_ge(s_rangeT, 1)
                dve.done(v.tensor_reduce(extremes[0:HALVES, 0:1], psum[0:HALVES, 2, 0:P], AX.X, ALU.min))
                dve.then(v.tensor_reduce(extremes[0:HALVES, 1:2], psum[0:HALVES, 2, P:2 * P], AX.X, ALU.max))
                dve.then(v.tensor_tensor(misfit[0:HALVES, :], extremes[0:HALVES, 1:2], extremes[0:HALVES, 0:1], ALU.subtract))
                v.tensor_scalar(misfit[0:HALVES, :], misfit[0:HALVES, :], P - 0.5, None, ALU.is_gt).then_inc(s_ends, 1)
                v.tensor_scalar(diagonal[0:HALVES, :], ident[0:HALVES, 0:HALVES], extremes[0:HALVES, 0:1], None, ALU.mult).then_inc(s_ends, 1)
                v.wait_ge(s_base, 1)
                dve.done(v.memset(win_base[:, HALVES:], 0.0))
                dve.then(v.tensor_copy(win_base[:, 0:HALVES], psum[:, 3, 0:HALVES]))
                dve.done(v.tensor_copy(attn_col[:, :], psum[:, 3, HALVES + 1:HALVES + 1 + DC]))
                dve.done(v.tensor_scalar(fits[:, :], psum[:, 3, HALVES:HALVES + 1], 0.5, None, ALU.is_lt))
                dve.then(v.tensor_scalar(window_f, win_base[:, 0:HALVES], row_id[:, :], None, ALU.add))
                dve.done(v.tensor_copy(win_nodes[:, :], window_f))
                dve.then(v.tensor_scalar(window_f, window_f, float(NP - 1), None, ALU.min))
                dve.done(v.tensor_copy(win_rows[:, :], window_f))
                v.wait_ge(s_wc, GROUPS + 1)
                for c in range(DC):
                    w = wkvT[:, c, :].rearrange("p (h d) -> p h d", d=DH)
                    dve.then(v.tensor_reduce(headmean[:, c, :], w, AX.X, ALU.add))
                    dve.then(v.tensor_scalar(headmean[:, c, :], headmean[:, c, :], 1.0 / DH, None, ALU.mult))
                    dve.then(v.tensor_tensor(w, w, headmean[:, c, :].unsqueeze(2).to_broadcast([P, 2 * HEADS, DH]),
                                             ALU.subtract))

            @block.tensor
            def _(pe):
                pe.wait_ge(s_const, 3)
                pe.wait_ge(s_w, 16 * LOADS)

                def transposes(a, b):
                    for q in range(a, b):
                        wait(pe, s_wc, q - 1)
                        for k in range(4):
                            mm = pe.transpose(psum[:, q % 2, k * P:(k + 1) * P], jobs[4 * q + k][0], ident[:, :])
                        mm.then_inc(s_wt, 1)

                transposes(0, FIRST // 4)

                def turn(t, slot):
                    wait(pe, s_xn, t + 1)
                    wait(pe, s_xt, t - 1)
                    for c in range(DC):
                        mm = pe.transpose(psum[:, 6 + slot, c * P:(c + 1) * P], xn[:, slot, c * P:(c + 1) * P], ident[:, :])
                    mm.then_inc(s_tp, 1)

                def project(t, slot):
                    wait(pe, s_xt, t + 1)
                    wait(pe, s_pc, 2 * t - 2)
                    for a, b, bank in ((0, 512, 2 + 2 * slot), (512, 3 * D, 3 + 2 * slot)):
                        for c in range(DC):
                            mm = pe.matmul(psum[:, bank, 0:b - a], xnT[:, slot, c * P:(c + 1) * P], w3T[:, c, a:b],
                                           start=(c == 0), stop=(c == DC - 1))
                    mm.then_inc(s_pj, 1)

                pe.wait_ge(s_wc, FIRST // 4)
                turn(0, 0)
                turn(1, 1)
                project(0, 0)
                turn(2, 0)
                project(1, 1)
                with pe.Fori(1, NT // 2) as i:
                    turn(2 * i + 1, 1)
                    project(2 * i, 0)
                    turn(2 * i + 2, 0)
                    project(2 * i + 1, 1)
                project(NT - 1, 0)
                transposes(FIRST // 4, GROUPS)
                pe.wait_ge(s_wc, GROUPS - 1)
                mm = pe.transpose(psum[:, GROUPS % 2, 0:NE * FT], b1_raw[0:NE * FT, :], ident[0:NE * FT, 0:NE * FT])
                mm.then_inc(s_wt, 1)
                pe.wait_ge(s_wc, GROUPS + 1)
                pe.wait_ge(s_rf, 1)
                for b in range(FULL_B + 1):
                    n = min(P, ET - b * P)
                    wait(pe, s_ec, b - 1)
                    for j in range(2):
                        mm = pe.transpose(psum[:, b % 2, j * P:j * P + n], raw_f[0:n, j, b, :], ident[0:n, 0:n])
                    mm.then_inc(s_et, 1)
                pe.wait_ge(s_range, 2)
                for j in range(2):
                    mm = pe.transpose(psum[0:HALVES, 2, j * P:(j + 1) * P], dst_range[:, j, :], ident[:, :])
                mm.then_inc(s_rangeT, 1)
                pe.wait_ge(s_ends, 2)
                pe.matmul(psum[:, 3, 0:HALVES], ones[0:HALVES, :], diagonal[0:HALVES, :], start=True, stop=True)
                for c in range(DC):
                    pe.matmul(psum[:, 3, HALVES + 1 + c:HALVES + 2 + c], attn[0:1, c * P:(c + 1) * P], ones[0:1, 0:1], start=True, stop=True)
                pe.matmul(psum[:, 3, HALVES:HALVES + 1], ones[0:HALVES, :], misfit[0:HALVES, :], start=True, stop=True).then_inc(s_base, 1)

            @block.scalar
            def _(act):
                def copies(a, b):
                    for q in range(a, b):
                        act.wait_ge(s_wt, q + 1)
                        d0, d2 = jobs[4 * q][1], jobs[4 * q + 2][1]
                        for k in range(4):
                            ins = act.copy(jobs[4 * q + k][1], psum[:, q % 2, k * P:(k + 1) * P])
                        ins.then_inc(s_wc, 1)

                def take(t, slot):
                    wait(act, s_tp, t + 1)
                    wait(act, s_pj, t - 1)
                    act.copy(at(xn_all, t), psum[:, 6 + slot, 0:D])
                    act.copy(xnT[:, slot, :], psum[:, 6 + slot, 0:D]).then_inc(s_xt, 1)

                def give(t, slot):
                    wait(act, s_pj, t + 1)
                    wait(act, s_st[slot], 24 * t - 24 * slot)
                    act.copy(proj[:, slot, 0:2, 0:D], psum[:, 2 + 2 * slot, :].rearrange("p (w c) -> p w c", c=D)).then_inc(s_pc, 1)
                    act.copy(proj[:, slot, 2, 0:D], psum[:, 3 + 2 * slot, 0:D]).then_inc(s_pc, 1)

                copies(0, FIRST // 4)
                take(0, 0)
                take(1, 1)
                give(0, 0)
                take(2, 0)
                give(1, 1)
                with act.Fori(1, NT // 2) as i:
                    take(2 * i + 1, 1)
                    give(2 * i, 0)
                    take(2 * i + 2, 0)
                    give(2 * i + 1, 1)
                give(NT - 1, 0)
                copies(FIRST // 4, GROUPS)
                act.wait_ge(s_wt, GROUPS + 1)
                act.copy(b1T[:, :], psum[:, GROUPS % 2, 0:NE * FT]).then_inc(s_wc, 1)

        m = Arena()
        idx = [m.take(2, HALF).bitcast(I32) for _ in range(2)]
        at3 = [m.take(3, HALF) for _ in range(2)]
        z = m.take(PASS, ZW)
        lk = m.take(4, ZW)
        ttr_out = m.take(2, ZW)
        score = [m.take(HALF) for _ in range(2)]
        pen = m.take(2, P)
        top = m.take(HALF)
        expo = m.take(HALF)
        lo_hot = [m.take(HALF, P) for _ in range(2)]
        hi_hot = [m.take(HALF, TABW) for _ in range(2)]
        tabs = m.take(HALF, TABW)
        cnt = m.take(HALF, NT)
        new_max = m.take(NT)
        scale_old = m.take(NT)
        part = m.take(NT)

        s_idx, s_zin1, s_zin = sem("indices_ready"), [sem(f"proj_s_in{i}") for i in range(HALF)], [sem(f"z_in{i}") for i in range(PASS)]
        s_lk, s_sc, s_row, s_top = sem("leaky_done"), sem("score_done"), sem("rows_broadcast"), sem("top_done")
        s_dif, s_exp, s_hot = sem("top_difference"), sem("exp_done"), sem("hot_ready")
        s_tab, s_ev, s_mrg, s_df2, s_ex2 = sem("tables_ready"), sem("tables_copied"), sem("merge_done"), sem("merge_differences"), sem("merge_exps")

        s_zero = sem("zeros_stored")

        with nc.Block() as block:
            @block.gpsimd
            def _(g):
                def half(i, h):
                    k = 2 * i + h
                    hold(g, s_idx, k + 1, s_held)

                    def first(u):
                        g.indirect_dma_start(z[:, HALF * h + u, :], None, proj_s, bass.IndirectOffsetOnAxis(
                            ap=idx[h][:, 0, u:u + 1], axis=0)).then_inc(s_zin1[u], 16)

                    def second(u):
                        hold(g, s_zin1[u], 16 * (k + 1), s_held)
                        g.indirect_dma_start(z[:, HALF * h + u, :], None, proj_t, bass.IndirectOffsetOnAxis(
                            ap=idx[h][:, 1, u:u + 1], axis=0), compute_op=ALU.add).then_inc(s_zin[HALF * h + u], 16)

                    LAG = HALF // 2
                    for u in range(LAG):
                        first(u)
                    for u in range(LAG):
                        second(u)
                        first(u + LAG)
                    for u in range(LAG, HALF):
                        second(u)

                with g.Fori(0, PASSES) as i:
                    half(i, 0)
                    half(i, 1)

            @block.scalar
            def _(act):
                def leaky(i, h, u):
                    T = PASS * i + HALF * h + u
                    wait(act, s_zin[HALF * h + u], 16 * (i + 1))
                    wait(act, s_sc, T - 3)
                    act.activation(lk[:, u % 4, :], z[:, HALF * h + u, :], ACT.Relu, scale=1.0 - SLOPE).then_inc(s_lk, 1)

                def copy_tables(i, h, b):
                    k = 2 * i + h
                    wait(act, s_tab, 4 * k + b + 1)
                    wait(act, s_mrg, k)
                    act.copy(tabs[:, 2 * b:2 * b + 2, :], psum[:, 4 + b, 0:2 * TABW].rearrange("p (t c) -> p t c", c=TABW)).then_inc(s_ev, 1)

                def merge_exps(k):
                    wait(act, s_df2, k + 1)
                    act.activation(tabs[:, :, 0:NT], tabs[:, :, 0:NT], ACT.Exp).then_inc(s_ex2, 1)
                    act.activation(scale_old, scale_old, ACT.Exp).then_inc(s_ex2, 1)

                def half(i, h):
                    k = 2 * i + h
                    for u in range(6):
                        leaky(i, h, u)
                    for b in range(4):
                        copy_tables(i, h, b)
                    leaky(i, h, 6)
                    leaky(i, h, 7)
                    merge_exps(k)
                    wait(act, s_dif, k + 1)
                    act.activation(expo, expo, ACT.Exp).then_inc(s_exp, 1)

                half(0, 0)
                half(0, 1)
                with act.Fori(1, PASSES) as i:
                    half(i, 0)
                    half(i, 1)
                for b in range(4):
                    copy_tables(PASSES, 0, b)
                merge_exps(2 * PASSES)

            @block.tensor
            def _(pe):
                for b in range(4):
                    pe.matmul(psum[:, 4 + b, 0:2 * TABW], zeros[:, 0:P], zeros[:, 0:2 * TABW], start=True, stop=True).then_inc(s_tab, 1)

                def half(i, h):
                    k = 2 * i + h
                    for u in range(HALF):
                        T = HALF * k + u
                        wait(pe, s_sc, T + 1)
                        if u % 2 == 0:
                            wait(pe, s_top, T - HALF + 2)
                        row = psum[:, u // 2, (u % 2) * 2 * P:(u % 2) * 2 * P + 2 * P]
                        pe.matmul(row[:, 0:P], at3[h][:, 0, u:u + 1].to_broadcast([P, P]), ident[:, :], start=True, stop=True)
                        mm = pe.matmul(row[:, P:2 * P], score[h][:, u:u + 1].to_broadcast([P, P]), ident[:, :], start=True,
                                       stop=True)
                        if u % 2 == 1:
                            mm.then_inc(s_row, 1)
                    wait(pe, s_hot, k + 1)
                    for b in range(4):
                        wait(pe, s_ev, 4 * k + b + 1)
                        for j in range(2):
                            u = 2 * b + j
                            mm = pe.matmul(psum[:, 4 + b, j * TABW:(j + 1) * TABW], lo_hot[h][:, u, :], hi_hot[h][:, u, :],
                                           start=True, stop=True)
                        mm.then_inc(s_tab, 1)

                half(0, 0)
                half(0, 1)
                with pe.Fori(1, PASSES) as i:
                    half(i, 0)
                    half(i, 1)

            @block.vector
            def _(v):
                def prepare(i, h):
                    c = span(PASS * i + HALF * h, HALF)
                    dve.done(v.tensor_copy(at3[h], attr[:, :, c]))
                    v.tensor_copy(idx[h], edges[:, :, c]).then_inc(s_idx, 1)

                def merge(k):
                    wait(v, s_ev, 4 * k + 4)
                    cn = tabs[:, :, NT:2 * NT]
                    tm = tabs[:, :, 0:NT]
                    ts = tabs[:, :, 2 * NT:3 * NT]
                    dve.then(v.tensor_scalar(cnt, cn, 1.0, None, ALU.max))
                    dve.then(v.reciprocal(cnt, cnt))
                    dve.then(v.tensor_tensor(tm, tm, cnt, ALU.mult))
                    dve.then(v.tensor_scalar(cnt, cn, 0.5, -BIG, ALU.is_lt, ALU.mult))
                    dve.then(v.tensor_tensor(tm, tm, cnt, ALU.add))
                    dve.then(v.tensor_reduce(new_max, tm.rearrange("p t n -> p n t"), AX.X, ALU.max))
                    dve.then(v.tensor_tensor(new_max, new_max, tab_max[:, :], ALU.max))
                    dve.then(v.tensor_tensor(scale_old, tab_max[:, :], new_max, ALU.subtract))
                    v.tensor_tensor(tm, tm, new_max.unsqueeze(1).to_broadcast([P, HALF, NT]), ALU.subtract).then_inc(s_df2, 1)
                    dve.done(v.tensor_copy(tab_max[:, :], new_max))
                    wait(v, s_ex2, 2 * k + 2)
                    dve.then(v.tensor_tensor(tm, tm, ts, ALU.mult))
                    dve.then(v.tensor_reduce(part, tm.rearrange("p t n -> p n t"), AX.X, ALU.add))
                    dve.then(v.tensor_tensor(tab_sum[:, :], tab_sum[:, :], scale_old, ALU.mult))
                    v.tensor_tensor(tab_sum[:, :], tab_sum[:, :], part, ALU.add).then_inc(s_mrg, 1)
                    wait(v, s_mrg, k + 1)
                MERGE = 12

                def half(i, h):
                    k = 2 * i + h
                    for u in range(HALF):
                        T = HALF * k + u
                        wait(v, s_sc, T - 1)
                        wait(v, s_lk, T + 1)
                        v.tensor_tensor_reduce(ttr_out[:, u % 2, :], lk[:, u % 4, :], attn[:, :], 1.0, 0.0, ALU.mult, ALU.add,
                                               score[h][:, u:u + 1]).then_inc(s_sc, 1)
                    merge(k)
                    lo = at3[h][:, 2, :].unsqueeze(2).to_broadcast([P, HALF, P])
                    hi = at3[h][:, 1, :].unsqueeze(2).to_broadcast([P, HALF, NT])
                    dve.done(v.tensor_tensor(lo_hot[h], lo, count[:, :].unsqueeze(1).to_broadcast([P, HALF, P]), ALU.is_equal))
                    dve.done(v.tensor_tensor(hi_hot[h][:, :, NT:2 * NT], hi, count[:, 0:NT].unsqueeze(1).to_broadcast([P, HALF, NT]),
                                             ALU.is_equal))
                    for u in range(HALF):
                        T = HALF * k + u
                        wait(v, s_top, T - 1)
                        wait(v, s_row, HALF // 2 * k + u // 2 + 1)
                        row = psum[:, u // 2, (u % 2) * 2 * P:(u % 2) * 2 * P + 2 * P]
                        dve.done(v.tensor_scalar(pen[:, u % 2, :], row[:, 0:P], at3[h][:, 0, u:u + 1], -BIG, ALU.not_equal, ALU.mult))
                        dve.hold(s_held)
                        v.tensor_tensor_reduce(ttr_out[:, u % 2, 0:P], row[:, P:2 * P], pen[:, u % 2, :], 1.0, -3.0e38, ALU.add, ALU.max,
                                               top[:, u:u + 1]).then_inc(s_top, 1)
                    wait(v, s_top, HALF * k + HALF)
                    v.tensor_tensor(expo, score[h], top, ALU.subtract).then_inc(s_dif, 1)
                    hot = hi_hot[h][:, :, NT:2 * NT]
                    dve.done(v.tensor_tensor(hi_hot[h][:, :, 0:NT], hot, top.unsqueeze(2).to_broadcast([P, HALF, NT]), ALU.mult))
                    dve.then(v.tensor_copy(score_all[:, span(HALF * k, HALF)], score[h]))
                    wait(v, s_exp, k + 1)
                    v.tensor_tensor(hi_hot[h][:, :, 2 * NT:3 * NT], hot, expo.unsqueeze(2).to_broadcast([P, HALF, NT]),
                                    ALU.mult).then_inc(s_hot, 1)
                    wait(v, s_hot, k + 1)
                    prepare(i + 1, h)
                PER = 2 * (MERGE + 2 + HALF + 2 + 1)

                prepare(0, 0)
                prepare(0, 1)
                half(0, 0)
                half(0, 1)
                with v.Fori(1, PASSES) as i:
                    dve.enter(i, 1, PER)
                    half(i, 0)
                    half(i, 1)
                dve.leave(PASSES - 1)
                merge(2 * PASSES)
                dve.then(v.tensor_scalar(tab_sum[:, :], tab_sum[:, :], 0.5, None, ALU.max))
                dve.then(v.reciprocal(tab_sum[:, :], tab_sum[:, :]))
                dve.done(v.tensor_copy(max_rsum[:, :, 0], tab_max[:, :]))
                dve.then(v.tensor_copy(max_rsum[:, :, 1], tab_sum[:, :]))

            @block.sync
            def _(sp):
                for a in range(ACCS):
                    sp.dma_start(acc[a].rearrange("(t p) c -> p t c", p=P),
                                 zeros[:, 0:D].unsqueeze(1).to_broadcast([P, ACC_ROWS // P, D])).then_inc(s_zero, 16)
                sp.dma_start(moe_in[0:NE * SLOTS, :].rearrange("(t p) c -> p t c", p=P),
                             zeros[:, 0:D].unsqueeze(1).to_broadcast([P, NE * CT, D])).then_inc(s_zero, 16)
                sp.wait_ge(s_zero, 16 * (ACCS + 1))

        m = Arena()
        idx = [m.take(HALF).bitcast(I32) for _ in range(2)]
        dst_h = [m.take(HALF) for _ in range(2)]
        score_h = [m.take(HALF) for _ in range(2)]
        out_idx = [m.take(HALF).bitcast(I32) for _ in range(2)]
        rows = m.take(PASS, ROWW)
        msg = m.take(HALF, D)
        weight = m.take(2, 1)
        alpha = m.take(2, 1)
        picked = m.take(2, P)
        skip_out = m.take(2, P)
        earlier = m.take(HALF)
        away = m.take(HALF)
        x_tile = m.take(D)
        squares = m.take(2, INNER)
        k_sb = m.take(INNER)
        v_sb = m.take(INNER)
        var = m.take(2, HEADS)
        norm_kv = m.take(HEADS)
        inv_kv = m.take(HEADS)
        scratch = m.take(HEADS)
        trash = m.take(1)
        to_window = [m.take(1).bitcast(I32) for _ in range(2)]
        rel = [m.take(HALF) for _ in range(2)]
        wide_diff = m.take(HALF)
        wide_alpha = m.take(HALF)
        wide_picked = m.take(4, P)
        window = m.take(2, D)

        s_idx, s_mr = sem("row_indices_ready"), sem("max_rsum_stored")
        s_rows = [sem(f"rows_in{i}") for i in range(PASS)]
        s_acc = [sem(f"accumulated{a}") for a in range(ACCS)]
        s_dr, s_oi, s_w3, s_pick, s_m, s_msg = sem("dst_rows_broadcast"), sem("out_indices_ready"), sem("weights_done"), sem("picks_done"), sem("messages_ready"), sem("messages_copied")
        s_xt3, s_kv, s_sq, s_kc, s_nv, s_dots = sem("mix_x_ready"), sem("kv_ready"), sem("squares_done"), sem("keys_copied"), sem("values_ready"), sem("dots_added")
        s_red = sem("squares_summed")
        s_half = [sem(f"half_rows_in{h}") for h in range(2)]
        s_wacc = [sem(f"window_accumulated{h}") for h in range(2)]
        s_to, s_diff, s_wexp, s_win = sem("to_window_ready"), sem("differences_ready"), sem("window_weights_done"), sem("window_sums_done")
        s_gen3, s_fast3 = sem("general_steps3"), sem("window_steps3")

        with nc.Block() as block:
            @block.sync
            def _(sp):
                sp.dma_start(node_rows.rearrange("(t p) c -> p t c", p=P)[:, :, D:ROWW], max_rsum[:, :, :]).then_inc(s_mr, 16)

            @block.gpsimd
            def _(g):
                g.wait_ge(s_mr, 16)
                with g.If(windowed(g) > 0):
                    def fetch_half(k, h):
                        hold(g, s_idx, k + 1, s_held)
                        for u in range(HALF):
                            g.indirect_dma_start(rows[:, HALF * h + u, :], None, node_rows,
                                                 bass.IndirectOffsetOnAxis(ap=idx[h][:, u:u + 1], axis=0)).then_inc(s_half[h], 16)

                    def add_window(i, h):
                        k = 2 * i + h
                        hold(g, s_to, k + 1, s_held)
                        hold(g, s_msg, k + 1, s_held)
                        hold(g, s_wacc[h], 16 * i, s_held)
                        g.indirect_dma_start(acc[h], bass.IndirectOffsetOnAxis(ap=to_window[h], axis=0), window[:, h, :],
                                             None, compute_op=ALU.add).then_inc(s_wacc[h], 16)

                    def step(i):
                        fetch_half(2 * i + 1, 1)
                        add_window(i, 0)
                        fetch_half(2 * i + 2, 0)
                        add_window(i, 1)

                    fetch_half(0, 0)
                    step(0)
                    with g.Fori(1, PASSES) as i:
                        step(i)
                    for h in range(2):
                        g.wait_ge(s_wacc[h], 16 * PASSES)
                    g.wait_ge(s_half[0], 16 * HALF * (PASSES + 1))
                with g.Else():
                    def gather(k, h):
                        hold(g, s_idx, k + 1, s_held)
                        return lambda u: g.indirect_dma_start(
                            rows[:, HALF * h + u, :], None, node_rows,
                            bass.IndirectOffsetOnAxis(ap=idx[h][:, u:u + 1], axis=0)).then_inc(s_rows[HALF * h + u], 16)

                    def scatter(k, h, u):
                        a = u % ACCS
                        n = (HALF // ACCS) * k + u // ACCS
                        hold(g, s_msg, HALF * k + u + 1, s_held)
                        hold(g, s_acc[a], 16 * n, s_held)
                        g.indirect_dma_start(acc[a], bass.IndirectOffsetOnAxis(ap=out_idx[h][:, u:u + 1], axis=0), msg[:, u, :],
                                             None, compute_op=ALU.add).then_inc(s_acc[a], 16)

                    def half(i, h):
                        k = 2 * i + h
                        fetch = gather(k + 1, 1 - h)
                        hold(g, s_oi, k + 1, s_held)
                        for u in range(HALF):
                            fetch(u)
                            scatter(k, h, u)

                    fetch = gather(0, 0)
                    for u in range(HALF):
                        fetch(u)
                    half(0, 0)
                    half(0, 1)
                    with g.Fori(1, PASSES) as i:
                        half(i, 0)
                        half(i, 1)
                    for a in range(ACCS):
                        g.wait_ge(s_acc[a], 16 * (ET // ACCS))
                    for u in range(HALF):
                        g.wait_ge(s_rows[u], 16 * (PASSES + 1))

            @block.scalar
            def _(act):
                def mix(i):
                    wait(act, s_kv, i)
                    act.copy(x_tile, at(xn_all, i)).then_inc(s_xt3, 1)
                    wait(act, s_kv, i + 1)
                    wait(act, s_red, i)
                    act.activation(squares[:, 0, :], psum[:, 4, :], ACT.Square).then_inc(s_sq, 1)
                    act.activation(squares[:, 1, :], psum[:, 5, :], ACT.Square).then_inc(s_sq, 1)
                    wait(act, s_dots, i)
                    act.copy(k_sb, psum[:, 4, :]).then_inc(s_kc, 1)

                with act.If(windowed(act) > 0):
                    def step(i, h):
                        k = 2 * i + h
                        wait(act, s_diff, k + 1)
                        act.activation(wide_diff, wide_diff, ACT.Exp).then_inc(s_wexp, 1)
                        wait(act, s_win, HALF * k + HALF)
                        wait(act, s_wacc[h], 16 * i)
                        act.copy(window[:, h, :], psum[:, h, 0:D]).then_inc(s_msg, 1)

                    step(0, 0)
                    mix(0)
                    step(0, 1)
                    with act.Fori(1, PASSES) as i:
                        step(i, 0)
                        mix(i)
                        step(i, 1)
                with act.Else():
                    def half(i, h):
                        k = 2 * i + h
                        for u in range(HALF):
                            T = HALF * k + u
                            wait(act, s_rows[HALF * h + u], 16 * (i + 1))
                            wait(act, s_pick, T - 1)
                            act.activation(weight[:, u % 2, :], rows[:, HALF * h + u, D:D + 1], ACT.Exp, scale=-1.0,
                                           bias=score_h[h][:, u:u + 1]).then_inc(s_w3, 1)
                            if u >= 1:
                                give(i, h, u - 1)
                        give(i, h, HALF - 1)

                    def give(i, h, u):
                        k = 2 * i + h
                        T = HALF * k + u
                        wait(act, s_m, T + 1)
                        wait(act, s_acc[u % ACCS], 16 * ((HALF // ACCS) * (k - 1) + u // ACCS + 1))
                        act.copy(msg[:, u, :], psum[:, 2 + u % 2, 0:D]).then_inc(s_msg, 1)

                    half(0, 0)
                    mix(0)
                    half(0, 1)
                    with act.Fori(1, PASSES) as i:
                        half(i, 0)
                        mix(i)
                        half(i, 1)

            @block.tensor
            def _(pe):
                pe.matmul(psum[:, 6, :], zeros[:, 0:P], zeros[:, :], start=True, stop=True)

                def keys_values(i):
                    wait(pe, s_xt3, i + 1)
                    wait(pe, s_nv, i)
                    wait(pe, s_kc, i)
                    for half_ in range(2):
                        for c in range(DC):
                            mm = pe.matmul(psum[:, 4 + half_, :], x_tile[:, c * P:(c + 1) * P],
                                           wkvT[:, c, half_ * INNER:(half_ + 1) * INNER], start=(c == 0), stop=(c == DC - 1))
                    mm.then_inc(s_kv, 1)

                def add_dots(i):
                    wait(pe, s_kc, i + 1)
                    wait(pe, s_nv, i + 1)
                    for q in range(PAIRS):
                        mm = pe.matmul(psum[:, 6, q * P:(q + 1) * P], v_sb[:, q * P:(q + 1) * P], k_sb[:, q * P:(q + 1) * P],
                                       start=False, stop=True, skip_group_check=True)
                    mm.then_inc(s_dots, 1)

                with pe.If(windowed(pe) > 0):
                    def window_sums(i, h):
                        k = 2 * i + h
                        wait(pe, s_msg, k - 1)
                        for u in range(HALF):
                            wait(pe, s_pick, HALF * k + u + 1)
                            pe.matmul(psum[:, h, 0:D], wide_picked[:, u % 4, :], rows[:, HALF * h + u, 0:D],
                                      start=(u == 0), stop=(u == HALF - 1)).then_inc(s_win, 1)

                    def step(i):
                        window_sums(i, 0)
                        keys_values(i)
                        window_sums(i, 1)
                        add_dots(i)

                    step(0)
                    with pe.Fori(1, PASSES) as i:
                        step(i)
                with pe.Else():
                    def spread(i, h):
                        k = 2 * i + h
                        wait(pe, s_idx, k + 1)
                        wait(pe, s_pick, HALF * k)
                        for u in range(HALF):
                            mm = pe.matmul(psum[:, u // 4, (u % 4) * P:(u % 4 + 1) * P], dst_h[h][:, u:u + 1].to_broadcast([P, P]), ident[:, :],
                                           start=True, stop=True)
                        mm.then_inc(s_dr, 1)

                    def sums(i, h):
                        k = 2 * i + h
                        for u in range(HALF):
                            T = HALF * k + u
                            wait(pe, s_pick, T + 1)
                            wait(pe, s_msg, T - 1)
                            pe.matmul(psum[:, 2 + u % 2, 0:D], picked[:, u % 2, :], rows[:, HALF * h + u, 0:D],
                                      start=True, stop=True).then_inc(s_m, 1)

                    def whole(i):
                        spread(i, 0)
                        sums(i, 0)
                        keys_values(i)
                        spread(i, 1)
                        sums(i, 1)
                        add_dots(i)

                    whole(0)
                    with pe.Fori(1, PASSES) as i:
                        whole(i)

            @block.vector
            def _(v):
                def mix(i, dve):
                    wait(v, s_sq, 2 * i + 2)
                    dve.done(v.tensor_reduce(var[:, 0, :], squares[:, 0, :].rearrange("p (h d) -> p h d", d=DH), AX.X, ALU.add))
                    ins = v.tensor_reduce(var[:, 1, :], squares[:, 1, :].rearrange("p (h d) -> p h d", d=DH), AX.X, ALU.add)
                    ins.then_inc(s_red, 1)
                    wait(v, s_red, i + 1)
                    dve.wait()
                    dve.then(v.tensor_scalar(var, var, 1.0 / DH, LN_EPS, ALU.mult, ALU.add))
                    dve.then(v.tensor_tensor(norm_kv, var[:, 0, :], var[:, 1, :], ALU.mult))
                    rsqrt(v, dve, inv_kv, norm_kv, scratch)
                    wait(v, s_dots, i)
                    v.tensor_tensor(v_sb.rearrange("p (h d) -> p h d", d=DH), psum[:, 5, :].rearrange("p (h d) -> p h d", d=DH),
                                    inv_kv.unsqueeze(2).to_broadcast([P, HEADS, DH]), ALU.mult).then_inc(s_nv, 1)
                PER_MIX = 3 + RSQRT_STEPS

                with v.If(windowed(v) > 0):
                    dve = Steps(v, s_fast3)

                    def prepare(i, h):
                        c = span(PASS * i + HALF * h, HALF)
                        dve.done(v.tensor_scalar(rel[h], dst_f[:, c], win_base[:, span(2 * i + h, 1)], None, ALU.subtract))
                        dve.done(v.tensor_copy(score_h[h], score_all[:, c]))
                        v.tensor_copy(idx[h], edges[:, 0, c]).then_inc(s_idx, 1)

                    def step(i, h):
                        k = 2 * i + h
                        wait(v, s_wacc[h], 16 * i)
                        v.tensor_copy(to_window[h], win_nodes[:, span(k, 1)]).then_inc(s_to, 1)
                        wait(v, s_half[h], 16 * HALF * (i + 1))
                        row = rows[:, HALF * h:HALF * h + HALF, :]
                        v.tensor_tensor(wide_diff, score_h[h], row[:, :, D], ALU.subtract).then_inc(s_diff, 1)
                        wait(v, s_wexp, k + 1)
                        dve.then(v.tensor_tensor(wide_alpha, wide_diff, row[:, :, D + 1], ALU.mult))
                        for u in range(HALF):
                            wait(v, s_win, HALF * k + u - 3)
                            v.tensor_scalar(wide_picked[:, u % 4, :], count[:, :], rel[h][:, u:u + 1], wide_alpha[:, u:u + 1],
                                            ALU.is_equal, ALU.mult).then_inc(s_pick, 1)
                        wait(v, s_win, HALF * k + HALF)
                        prepare(i + 1, h)
                    PER_STEP = 1 + 2

                    prepare(0, 0)
                    prepare(0, 1)
                    step(0, 0)
                    mix(0, dve)
                    step(0, 1)
                    with v.Fori(1, PASSES) as i:
                        dve.enter(i, 1, 2 * PER_STEP + PER_MIX)
                        step(i, 0)
                        mix(i, dve)
                        step(i, 1)
                    dve.leave(PASSES - 1)
                with v.Else():
                    dve = Steps(v, s_gen3)

                    def prepare(i, h):
                        c = span(PASS * i + HALF * h, HALF)
                        dve.done(v.tensor_copy(dst_h[h], dst_f[:, c]))
                        dve.done(v.tensor_copy(score_h[h], score_all[:, c]))
                        v.tensor_copy(idx[h], edges[:, 0, c]).then_inc(s_idx, 1)

                    def half(i, h):
                        k = 2 * i + h
                        wait(v, s_dr, k + 1)
                        row = [psum[:, u // 4, (u % 4) * P:(u % 4 + 1) * P] for u in range(HALF)]
                        for u in range(HALF):
                            dve.wait(1)
                            dve.done(v.scalar_tensor_tensor(out=skip_out[:, u % 2, :], in0=row[u], scalar=dst_h[h][:, u:u + 1], in1=below[:, :],
                                                                  op0=ALU.is_equal, op1=ALU.mult, accum_out=earlier[:, u:u + 1]))
                        dve.wait()
                        dve.then(v.tensor_scalar(away, dst_h[h], trash, -1.0, ALU.subtract, ALU.mult))
                        dve.then(v.scalar_tensor_tensor(out=away, in0=earlier, scalar=1.0, in1=away, op0=ALU.min, op1=ALU.mult))
                        wait(v, s_acc[ACCS - 1], 16 * (HALF // ACCS) * (k - 1))
                        v.tensor_tensor(out_idx[h], away, dst_h[h], ALU.add).then_inc(s_oi, 1)
                        for u in range(HALF):
                            T = HALF * k + u
                            wait(v, s_w3, T + 1)
                            dve.then(v.tensor_tensor(alpha[:, u % 2, :], weight[:, u % 2, :], rows[:, HALF * h + u, D + 1:D + 2], ALU.mult))
                            wait(v, s_m, T - 1)
                            v.tensor_scalar(picked[:, u % 2, :], row[u], dst_h[h][:, u:u + 1], alpha[:, u % 2, :], ALU.is_equal,
                                            ALU.mult).then_inc(s_pick, 1)
                        wait(v, s_m, HALF * k + HALF)
                        wait(v, s_pick, HALF * k + HALF)
                        prepare(i + 1, h)
                    PER_HALF = HALF + 2 + HALF + 2

                    dve.then(v.tensor_scalar(trash, row_id[:, :], float(NP), None, ALU.add))
                    prepare(0, 0)
                    prepare(0, 1)
                    half(0, 0)
                    mix(0, dve)
                    half(0, 1)
                    with v.Fori(1, PASSES) as i:
                        dve.enter(i, 1, 2 * PER_HALF + PER_MIX)
                        half(i, 0)
                        mix(i, dve)
                        half(i, 1)
                    dve.leave(PASSES - 1)

        m = Arena()
        parts = m.take(2, ACCS, D)
        summed = m.take(2, 2, D)
        logits = m.take(NT, NE)
        x_tile = m.take(2, D)
        hT = m.take(2, D)
        h_sb = m.take(2, D)
        s_hs = sem("h_copied")
        stats = m.take(6)
        mean_var = m.take(NT, 2)
        pair = m.take(2, 2)
        variance = m.take(NT)
        rstd = m.take(NT)
        scratch = m.take(NT)
        dotsT = m.take(PAIRS, P)
        fold = m.take(PAIRS, D)
        mixed = m.take(DC, D)
        same_head = m.take(P)
        dots_all = m.take(PAIRS, P)
        s_fold, s_foldc = sem("fold_ready"), sem("fold_copied")
        s_pin = [sem(f"parts_in{i}") for i in range(2)]
        s_sum, s_x4, s_mm, s_xa, s_x1, s_h, s_ht, s_htc, s_lg, s_lgc = (sem("parts_summed"), sem("x_tile_ready"), sem("mixed_ready"), sem("mixed_read"),
            sem("x1_ready"), sem("h_ready"), sem("h_transposed"), sem("hT_ready"), sem("logits_ready"), sem("logits_copied"))
        s_gp = sem("sum_steps")

        with nc.Block() as block:
            @block.sync
            def _(sp):
                def load(t, slot):
                    wait(sp, s_sum, t - 1)
                    for a in range(ACCS):
                        sp.dma_start(parts[:, slot, a, :], acc[a][span(t * P, P), :]).then_inc(s_pin[slot], 16)
                load(0, 0)
                load(1, 1)
                with sp.Fori(1, NT // 2) as i:
                    load(2 * i, 0)
                    load(2 * i + 1, 1)
                load(NT - 1, 0)

            @block.gpsimd
            def _(g):
                st = Steps(g, s_gp)

                def add(t, slot):
                    wait(g, s_pin[slot], 32 * ACCS // 2 * ((t - slot) // 2 + 1) if isinstance(t, int) else 8 * ACCS * (t - slot) + 16 * ACCS)
                    wait(g, s_xa, t - 1)
                    st.done(g.tensor_tensor(summed[:, slot, 1, :], parts[:, slot, 2, :], parts[:, slot, 3, :], ALU.add))
                    st.then(g.tensor_tensor(summed[:, slot, 0, :], parts[:, slot, 0, :], parts[:, slot, 1, :], ALU.add))
                    g.tensor_tensor(summed[:, slot, 0, :], summed[:, slot, 0, :], summed[:, slot, 1, :], ALU.add).then_inc(s_sum, 1)
                add(0, 0)
                add(1, 1)
                with g.Fori(1, NT // 2) as i:
                    st.enter(i, 1, 4)
                    add(2 * i, 0)
                    add(2 * i + 1, 1)
                st.leave(NT // 2 - 1)
                add(NT - 1, 0)

            @block.tensor
            def _(pe):
                pe.wait_ge(s_foldc, 1)
                for q in range(PAIRS):
                    mm = pe.matmul(psum[:, q // 2, (q % 2) * D:(q % 2 + 1) * D], dotsT[:, q, :], woutT[:, q, :], start=True, stop=True)
                mm.then_inc(s_fold, 1)
                pe.wait_ge(s_foldc, 2)
                for c in range(DC):
                    for q in range(PAIRS):
                        mm = pe.matmul(psum[:, 2 + c, 0:D], wq[:, q, c * P:(c + 1) * P], fold[:, q, :], start=(q == 0), stop=(q == PAIRS - 1))
                mm.then_inc(s_fold, 1)
                pe.wait_ge(s_foldc, 3)

                def mix(t, slot):
                    wait(pe, s_x4, t + 1)
                    wait(pe, s_xa, t - 1)
                    for j in range(2):
                        pe.matmul(psum[:, slot, 0:D], ones[0:1, :], bias_row[:, j, :], start=(j == 0), stop=False)
                    for c in range(DC):
                        mm = pe.matmul(psum[:, slot, 0:D], x_tile[:, slot, c * P:(c + 1) * P], mixed[:, c, :], start=False, stop=(c == DC - 1))
                    mm.then_inc(s_mm, 1)

                def gate(t, slot):
                    wait(pe, s_h, t + 1)
                    wait(pe, s_htc, t - 1)
                    for c in range(DC):
                        mm = pe.transpose(psum[:, 4 + slot, c * P:(c + 1) * P], h_sb[:, slot, c * P:(c + 1) * P], ident[:, :])
                    mm.then_inc(s_ht, 1)
                    wait(pe, s_htc, t + 1)
                    wait(pe, s_lgc, t - 1)
                    for c in range(DC):
                        mm = pe.matmul(psum[:, 6 + slot, 0:NE], hT[:, slot, c * P:(c + 1) * P], gw[:, c, :], start=(c == 0), stop=(c == DC - 1))
                    mm.then_inc(s_lg, 1)

                for step in (mix, gate):
                    step(0, 0)
                    step(1, 1)
                    with pe.Fori(1, NT // 2) as i:
                        step(2 * i, 0)
                        step(2 * i + 1, 1)
                    step(NT - 1, 0)

            @block.scalar
            def _(act):
                def take(t, slot):
                    wait(act, s_mm, t - 1)
                    act.copy(x_tile[:, slot, :], at(xn_all, t)).then_inc(s_x4, 1)

                def turn(t, slot):
                    wait(act, s_h, t + 1)
                    act.copy(at(xn_all, t), h_sb[:, slot, :]).then_inc(s_hs, 1)
                    wait(act, s_ht, t + 1)
                    wait(act, s_lg, t - 1)
                    act.copy(hT[:, slot, :], psum[:, 4 + slot, 0:D]).then_inc(s_htc, 1)
                    wait(act, s_lg, t + 1)
                    act.copy(at(logits, t), psum[:, 6 + slot, 0:NE]).then_inc(s_lgc, 1)
                for step in (take, turn):
                    step(0, 0)
                    step(1, 1)
                    with act.Fori(1, NT // 2) as i:
                        step(2 * i, 0)
                        step(2 * i + 1, 1)
                    step(NT - 1, 0)

            @block.vector
            def _(v):
                dve.done(v.memset(same_head, 0.0))
                dve.wait()
                for h in range(P // DH):
                    dve.done(v.memset(same_head[h * DH:(h + 1) * DH, h * DH:(h + 1) * DH], 1.0 / N))
                dve.wait()
                v.tensor_tensor(dotsT, psum[:, 6, :].rearrange("p (q j) -> p q j", j=P), same_head.unsqueeze(1).to_broadcast([P, PAIRS, P]),
                                ALU.mult).then_inc(s_foldc, 1)
                v.wait_ge(s_fold, 1)
                dve.done(v.tensor_copy(fold[:, 0:2, :], psum[:, 0, :].rearrange("p (q j) -> p q j", j=D)))
                dve.wait()
                v.tensor_copy(fold[:, 2:4, :], psum[:, 1, :].rearrange("p (q j) -> p q j", j=D)).then_inc(s_foldc, 1)
                v.wait_ge(s_fold, 2)
                v.tensor_copy(mixed, psum[:, 2:4, 0:D]).then_inc(s_foldc, 1)

                def residual(t, slot):
                    xt = at(x_all, t)
                    wait(v, s_mm, t + 1)
                    dve.then(v.tensor_tensor(xt, xt, psum[:, slot, 0:D], ALU.add))
                    wait(v, s_sum, t + 1)
                    v.tensor_tensor(xt, xt, summed[:, slot, 0, :], ALU.add).then_inc(s_xa, 1)
                    hold(v, s_xa, t + 1, s_held)
                    dve.done(v.bn_stats(stats, xt))
                    dve.hold(s_held)
                    dve.then(v.bn_aggr(pair[:, slot, :], stats))
                    dve.done(v.tensor_copy(at(mean_var, t), pair[:, slot, :]))

                def normalise(t, slot):
                    wait(v, s_ht, t - 1)
                    wait(v, s_hs, t - 1)
                    v.tensor_scalar(h_sb[:, slot, :], at(x_all, t), at(mean_var, t)[:, 0:1], rstd[:, span(t, 1)],
                                    ALU.subtract, ALU.mult).then_inc(s_h, 1)

                residual(0, 0)
                residual(1, 1)
                with v.Fori(1, NT // 2) as i:
                    dve.enter(i, 1, 8)
                    residual(2 * i, 0)
                    residual(2 * i + 1, 1)
                dve.leave(NT // 2 - 1)
                residual(NT - 1, 0)
                dve.wait()
                dve.then(v.tensor_scalar(variance, mean_var[:, :, 1], LN_EPS, None, ALU.add))
                rsqrt(v, dve, rstd, variance, scratch)
                normalise(0, 0)
                normalise(1, 1)
                with v.Fori(1, NT // 2) as i:
                    normalise(2 * i, 0)
                    normalise(2 * i + 1, 1)
                normalise(NT - 1, 0)

        m = Arena()
        m.take(2, ACCS, D)
        m.take(2, 2, D)
        m.take(NT, NE)
        expos = m.take(NT, NE)
        probs = m.take(NT, NE)
        chosen = m.take(NT, NE)
        tmp = m.take(NT, NE)
        place_e = m.take(NT, NE)
        totals = m.take(NE, NT)
        upto = m.take(NE, NT)
        red = m.take(NT)
        prob = m.take(NT)
        expert = m.take(NT)
        pos = m.take(NT)
        kept = m.take(NT)
        trash = m.take(NT)
        s_r, s_rm, s_re, s_sent = sem("routed"), sem("ranks_ready"), sem("route_exp"), sem("rows_sent")

        with nc.Block() as block:
            @block.vector
            def _(v):
                def wide(a):
                    return a.unsqueeze(2).to_broadcast([P, NT, NE])
                ids = count[:, 0:NE].unsqueeze(1).to_broadcast([P, NT, NE])
                dve.then(v.tensor_scalar(trash, count[:, 0:NT], float(P), row_id[:, :], ALU.mult, ALU.add))
                dve.then(v.tensor_scalar(trash, trash, float(NE * SLOTS), None, ALU.add))
                dve.then(v.tensor_tensor(logits, logits, gb[:, :].unsqueeze(1).to_broadcast([P, NT, NE]), ALU.add))
                dve.then(v.tensor_reduce(red, logits, AX.X, ALU.max))
                v.tensor_tensor(expos, logits, wide(red), ALU.subtract).then_inc(s_r, 1)
                v.wait_ge(s_re, 1)
                dve.then(v.tensor_reduce(red, expos, AX.X, ALU.add))
                dve.then(v.reciprocal(red, red))
                dve.then(v.tensor_tensor(probs, expos, wide(red), ALU.mult))
                dve.then(v.tensor_reduce(prob, probs, AX.X, ALU.max))
                dve.then(v.tensor_tensor(tmp, probs, wide(prob), ALU.not_equal))
                dve.then(v.scalar_tensor_tensor(out=tmp, in0=tmp, scalar=float(NE), in1=ids, op0=ALU.mult, op1=ALU.add))
                dve.then(v.tensor_reduce(expert, tmp, AX.X, ALU.min))
                v.tensor_tensor(chosen, wide(expert), ids, ALU.is_equal).then_inc(s_r, 1)
                v.wait_ge(s_rm, 1)
                dve.then(v.tensor_copy(totals, psum[:, 1, 0:NT * NE].rearrange("p (t e) -> p e t", e=NE)))
                for e in range(NE):
                    dve.done(v.tensor_tensor_scan(upto[:, e, :], totals[:, e, :], zeros[:, 0:NT], 0.0, ALU.add, ALU.add))
                dve.wait()
                dve.then(v.tensor_tensor(upto, upto, totals, ALU.subtract))
                dve.then(v.tensor_tensor(place_e, upto.rearrange("p e t -> p t e"), psum[:, 0, 0:NT * NE].rearrange("p (t e) -> p t e", e=NE), ALU.add))
                dve.then(v.tensor_tensor(place_e, place_e, chosen, ALU.mult))
                dve.then(v.tensor_reduce(pos, place_e, AX.X, ALU.add))
                dve.then(v.tensor_scalar(kept, pos, float(CAP), None, ALU.is_lt))
                dve.then(v.tensor_tensor(gate_prob[:, :], prob, kept, ALU.mult))
                dve.then(v.tensor_scalar(expert, expert, float(SLOTS), None, ALU.mult))
                dve.then(v.scalar_tensor_tensor(out=red, in0=pos, scalar=float(CAP - 1), in1=expert, op0=ALU.min, op1=ALU.add))
                dve.done(v.tensor_copy(slot_in[:, :], red))
                dve.then(v.tensor_tensor(red, red, trash, ALU.subtract))
                dve.then(v.tensor_tensor(red, red, kept, ALU.mult))
                v.tensor_tensor(slot_out[:, :], red, trash, ALU.add).then_inc(s_r, 1)
                v.wait_ge(s_r, 3)

            @block.scalar
            def _(act):
                act.wait_ge(s_r, 1)
                act.activation(expos, expos, ACT.Exp).then_inc(s_re, 1)

            @block.tensor
            def _(pe):
                pe.wait_ge(s_r, 2)
                pe.matmul(psum[:, 0, 0:NT * NE], above[:, :], chosen.rearrange("p t e -> p (t e)"), start=True, stop=True)
                pe.matmul(psum[:, 1, 0:NT * NE], ones[:, :], chosen.rearrange("p t e -> p (t e)"), start=True, stop=True).then_inc(s_rm, 1)

            @block.gpsimd
            def _(g):
                g.wait_ge(s_r, 3)
                for t in range(NT):
                    g.indirect_dma_start(moe_in, bass.IndirectOffsetOnAxis(ap=slot_out[:, t:t + 1], axis=0), xn_all[:, t, :], None).then_inc(s_sent, 16)
                g.wait_ge(s_sent, 16 * NT)

        m = Arena()
        w1_sb = m.take(2, DC, F)
        w2_sb = m.take(2, FT * D)
        rows_in = m.take(2, CT * D)
        y_sb = m.take(2, D)
        big = xn_all[:, :, :].rearrange("p t c -> p (t c)")
        hid = big[:, 0:FT * SLOTS].rearrange("p (f s) -> p f s", s=SLOTS)
        inT = big[:, FT * SLOTS:FT * SLOTS + DC * SLOTS].rearrange("p (c s) -> p c s", s=SLOTS)
        b2_all = big[:, (FT + DC) * SLOTS:(FT + DC) * SLOTS + NE * D].rearrange("p (e c) -> p e c", c=D)
        s_win = [sem(f"expert_loaded{i}") for i in range(2)]
        s_b2, s_it, s_itc, s_hid, s_hc, s_y, s_yc = sem("b2_loaded"), sem("inputs_transposed"), sem("inputs_copied"), sem("hidden_ready"), sem("hidden_done"), sem("y_ready"), sem("y_done")
        s_ys = [sem(f"y_stored{i}") for i in range(2)]
        HG = 2 * FT
        IG = DC * CT // 4

        with nc.Block() as block:
            @block.sync
            def _(sp):
                sp.dma_start(b2_all, b2.partition_broadcast(P)).then_inc(s_b2, 16)

                def load(e, s):
                    wait(sp, s_y, CT * (e - 1))
                    ei = span(e, 1)
                    sp.dma_start(w1_sb[:, s, :, :], w1[ei, :, :].rearrange("a (c p) f -> p (a c) f", p=P)).then_inc(s_win[s], 16)
                    sp.dma_start(w2_sb[:, s, :].rearrange("p (f d) -> p f d", d=D), w2[ei, :, :].rearrange("a (f p) d -> p (a f) d", p=P)).then_inc(s_win[s], 16)
                    sp.dma_start(rows_in[:, s, :].rearrange("p (t c) -> p t c", c=D),
                                 moe_in[span(e * SLOTS, SLOTS), :].rearrange("(t p) c -> p t c", p=P)).then_inc(s_win[s], 16)

                def store(e, s):
                    for j in range(CT):
                        wait(sp, s_yc, CT * e + j + 1)
                        sp.dma_start(moe_out[span(e * SLOTS + j * P, P), :], y_sb[:, j % 2, :]).then_inc(s_ys[j % 2], 16)
                load(0, 0)
                load(1, 1)
                store(0, 0)
                with sp.Fori(1, NE // 2) as i:
                    load(2 * i, 0)
                    store(2 * i - 1, 1)
                    load(2 * i + 1, 1)
                    store(2 * i, 0)
                store(NE - 1, 1)
                for q in range(2):
                    sp.wait_ge(s_ys[q], 16 * NE * CT // 2)

            @block.tensor
            def _(pe):
                def expert_(e, s):
                    wait(pe, s_win[s], 48 * ((e - s) // 2 + 1) if isinstance(e, int) else 24 * (e - s) + 48)
                    for q in range(IG):
                        wait(pe, s_itc, IG * e + q - 1)
                        for k in range(4):
                            c, j = (4 * q + k) // CT, (4 * q + k) % CT
                            mm = pe.transpose(psum[:, q % 2, k * P:(k + 1) * P], rows_in[:, s, j * D + c * P:j * D + (c + 1) * P], ident[:, :])
                        mm.then_inc(s_it, 1)
                    wait(pe, s_itc, IG * e + IG)
                    for f in range(FT):
                        for n in range(2):
                            G = HG * e + 2 * f + n
                            bank = 2 + (2 * f + n) % 4
                            wait(pe, s_hc, G - 3)
                            for c in range(DC):
                                mm = pe.matmul(psum[:, bank, :], w1_sb[:, s, c, f * P:(f + 1) * P], inT[:, c, n * 512:(n + 1) * 512],
                                               start=(c == 0), stop=(c == DC - 1))
                            mm.then_inc(s_hid, 1)
                    wait(pe, s_hc, HG * e + HG)
                    for j in range(CT):
                        wait(pe, s_yc, CT * e + j - 1)
                        for f in range(FT):
                            mm = pe.matmul(psum[:, 6 + j % 2, 0:D], hid[:, f, j * P:(j + 1) * P], w2_sb[:, s, f * D:(f + 1) * D],
                                           start=(f == 0), stop=(f == FT - 1))
                        mm.then_inc(s_y, 1)
                expert_(0, 0)
                expert_(1, 1)
                with pe.Fori(1, NE // 2) as i:
                    expert_(2 * i, 0)
                    expert_(2 * i + 1, 1)

            @block.scalar
            def _(act):
                def expert_(e):
                    for q in range(IG):
                        wait(act, s_it, IG * e + q + 1)
                        wait(act, s_hid, HG * e)
                        c, j = 4 * q // CT, 4 * q % CT
                        act.copy(inT[:, c, j * P:(j + 4) * P], psum[:, q % 2, :]).then_inc(s_itc, 1)
                    for f in range(FT):
                        for n in range(2):
                            G = HG * e + 2 * f + n
                            bank = 2 + (2 * f + n) % 4
                            hold(act, s_hid, G + 1, s_held)
                            hold(act, s_y, CT * e, s_held)
                            act.activation(hid[:, f, n * 512:(n + 1) * 512], psum[:, bank, :], ACT.Relu,
                                           bias=b1T[:, span(e * FT + f, 1)]).then_inc(s_hc, 1)
                expert_(0)
                with act.Fori(1, NE) as i:
                    expert_(i)

            @block.vector
            def _(v):
                def expert_(e):
                    for j in range(CT):
                        wait(v, s_y, CT * e + j + 1)
                        wait(v, s_ys[j % 2], 16 * (CT // 2 * e + j // 2))
                        v.tensor_tensor(y_sb[:, j % 2, :], psum[:, 6 + j % 2, 0:D], at(b2_all, e), ALU.add).then_inc(s_yc, 1)
                v.wait_ge(s_b2, 16)
                expert_(0)
                with v.Fori(1, NE) as i:
                    expert_(i)

        RING = 7
        m = Arena()
        got = m.take(RING, D)
        y = m.take(RING, D)
        high = m.take(D)
        bad = m.take(D)
        fine = m.take(D)
        s_got = [sem(f"result_in{i}") for i in range(RING)]
        s_rd, s_o = sem("result_read"), sem("out_ready")
        s_os = [sem(f"out_stored{i}") for i in range(RING)]

        with nc.Block() as block:
            @block.gpsimd
            def _(g):
                for t in range(NT):
                    wait(g, s_rd, t - RING + 1)
                    g.indirect_dma_start(got[:, t % RING, :], None, moe_out,
                                         bass.IndirectOffsetOnAxis(ap=slot_in[:, t:t + 1], axis=0)).then_inc(s_got[t % RING], 16)

            @block.vector
            def _(v):
                def tile(i, u):
                    t = RING * i + u
                    wait(v, s_got[u], 16 * (i + 1))
                    wait(v, s_os[u], 16 * i)
                    yu = y[:, u, :]
                    v.tensor_scalar(yu, got[:, u, :], gate_prob[:, span(t, 1)], None, ALU.mult).then_inc(s_rd, 1)
                    wait(v, s_rd, t + 1)
                    dve.done(v.tensor_scalar(high, yu, FLOAT_MAX, None, ALU.is_gt))
                    dve.then(v.tensor_scalar(fine, yu, 0.0, 0.0, ALU.mult, ALU.is_equal))
                    dve.then(v.scalar_tensor_tensor(out=bad, in0=yu, scalar=-FLOAT_MAX, in1=high, op0=ALU.is_lt, op1=ALU.subtract))
                    dve.done(v.tensor_scalar(bad, bad, -1.0e4, None, ALU.mult))
                    dve.hold(s_held)
                    dve.then(v.copy_predicated(bad, fine.bitcast(I32), yu))
                    v.tensor_tensor(yu, bad, at(x_all, t), ALU.add).then_inc(s_o, 1)
                    wait(v, s_o, t + 1)
                for u in range(RING):
                    tile(0, u)
                with v.Fori(1, NT // RING) as i:
                    dve.enter(i, 1, 5 * RING)
                    for u in range(RING):
                        tile(i, u)
                dve.leave(NT // RING - 1)

            @block.sync
            def _(sp):
                def store(t, u):
                    wait(sp, s_o, t + 1)
                    sp.dma_start(out[span(t * P, P), :], y[:, u, :]).then_inc(s_os[u], 16)
                with sp.Fori(0, NT // RING - 1) as i:
                    for u in range(RING):
                        store(RING * i + u, u)
                for t in range(NT - RING, NT - 1):
                    store(t, t % RING)
                sp.wait_ge(s_o, NT)
                sp.dma_start(out[(NT - 1) * P:N, :], y[0:TAIL, RING - 1, :]).then_inc(s_os[RING - 1], 16)
                for u in range(RING):
                    sp.wait_ge(s_os[u], 16 * (NT // RING))


_INS = ['x', 'src', 'dst', 'L0_gnn_W_s', 'L0_gnn_W_t', 'L0_gnn_W_attn', 'L0_gnn_W_fc', 'L0_gnn_b_fc', 'L0_mix_w_qkv',
        'L0_mix_w_out', 'L0_mix_b_out', 'L0_ffn_gate_w', 'L0_ffn_gate_b', 'L0_ffn_w1', 'L0_ffn_b1', 'L0_ffn_w2',
        'L0_ffn_b2']


def kernel(**inputs):
    import numpy as _np
    import concourse.bacc as _bacc
    from concourse import mybir as _mybir
    from concourse.bass_utils import run_bass_kernel_spmd as _run

    nc = _bacc.Bacc("TRN2", target_bir_lowering=False, num_devices=1)
    arrays, args = {}, []
    for name in _INS:
        a = _np.ascontiguousarray(inputs[name])
        arrays[f"in_{name}_dram"] = a
        args.append(nc.dram_tensor(f"in_{name}_dram", a.shape, _mybir.dt.from_np(a.dtype), kind="ExternalInput").ap())
    args.append(nc.dram_tensor("out_0_dram", tuple(inputs['x'].shape), _mybir.dt.float32, kind="ExternalOutput").ap())
    graph_transformer_kernel(nc, *args)
    r = _run(nc, [arrays], core_ids=[0])
    return r.results[0]["out_0_dram"]
```

```python
import concourse.bass as bass
from concourse import mybir
from contextlib import ExitStack

F32 = mybir.dt.float32
I32 = mybir.dt.int32
ALU = mybir.AluOpType
ACT = mybir.ActivationFunctionType
AX = mybir.AxisListType

P = 128
FLOAT_MAX = 3.4028234663852886e38
BIG = 1.0e30
LN_EPS = 1e-5
SLOPE = 0.2


class Steps:

    def __init__(self, eng, sem):
        self.eng, self.sem, self.base, self.n = eng, sem, 0, 0

    def enter(self, i, first, per_pass):
        self.start, self.per_pass = self.base + self.n, per_pass
        self.base, self.n = self.start + (i - first) * per_pass, 0

    def leave(self, passes):
        assert self.n == self.per_pass, (self.n, self.per_pass)
        self.base, self.n = self.start + passes * self.per_pass, 0

    def done(self, ins):
        self.n += 1
        return ins.then_inc(self.sem, 1)

    def wait(self, but=0):
        self.eng.wait_ge(self.sem, self.base + self.n - but)

    def hold(self, past):
        hold(self.eng, self.sem, self.base + self.n, past)

    def then(self, ins):
        self.done(ins)
        self.wait()


def rsqrt(v, steps, out, value, scratch):
    steps.then(v.tensor_scalar(out.bitcast(I32), value.bitcast(I32), -0.5, float(0x5f3759df), ALU.mult, ALU.add))
    for _ in range(3):
        steps.then(v.tensor_tensor(scratch, out, out, ALU.mult))
        steps.then(v.scalar_tensor_tensor(out=scratch, in0=scratch, scalar=-0.5, in1=value, op0=ALU.mult, op1=ALU.mult))
        steps.then(v.scalar_tensor_tensor(out=out, in0=scratch, scalar=1.5, in1=out, op0=ALU.add, op1=ALU.mult))


RSQRT_STEPS = 10


def wait(eng, sem, value):
    if not isinstance(value, int) or value > 0:
        eng.wait_ge(sem, value)


def hold(eng, sem, value, held):
    if not isinstance(value, int) or value > 0:
        eng.wait_ge(sem, value)
        eng.sem_inc(held, 1)


def at(v, t):
    if isinstance(t, int):
        return v[:, t, :]
    return v[:, bass.ds(t, 1), :].rearrange("p a c -> p (a c)")


def span(t, n):
    return slice(t, t + n) if isinstance(t, int) else bass.ds(t, n)


def graph_transformer_kernel(nc, x, src, dst, W_s, W_t, W_attn, W_fc, b_fc, w_qkv, w_out, b_out,
                             gate_w, gate_b, w1, b1, w2, b2, out):
    N, D = x.shape
    E = src.shape[0]
    NT = (N + P - 1) // P
    NP = NT * P
    TAIL = N - (NT - 1) * P
    PAD_NODE = NP - 1
    HALF = 8
    PASS = 2 * HALF
    PASSES = (E + P * PASS - 1) // (P * PASS)
    ET = PASSES * PASS
    HALVES = 2 * PASSES
    EC = ET + PASS
    FULL_B = E // (P * P)
    FULL_T = E // P - FULL_B * P
    REST = E % P
    ZW = D + 2
    HEADS, DH = 8, 64
    INNER = HEADS * DH
    PAIRS = INNER // P
    NE, _, F = w1.shape
    FT = F // P
    CAP = max(1, -(-5 * N // (4 * NE)))
    CT = (CAP + P - 1) // P
    SLOTS = CT * P
    DC = D // P
    TABW = 3 * NT
    ROWW = D + 2
    ACCS = 4
    ACC_ROWS = NP + P
    assert DC == 2 and NT == PASSES

    proj_s = nc.dram_tensor("proj_s", (NP, ZW), F32, kind="Internal").ap()
    proj_t = nc.dram_tensor("proj_t", (NP, ZW), F32, kind="Internal").ap()
    node_rows = nc.dram_tensor("node_rows", (NP, ROWW), F32, kind="Internal").ap()
    edge_rows = nc.dram_tensor("edge_rows", (2, ET * P), F32, kind="Internal").ap()
    acc = [nc.dram_tensor(f"acc{a}", (ACC_ROWS, D), F32, kind="Internal").ap() for a in range(ACCS)]
    moe_in = nc.dram_tensor("moe_in", (NE * SLOTS + NP, D), F32, kind="Internal").ap()
    moe_out = nc.dram_tensor("moe_out", (NE * SLOTS, D), F32, kind="Internal").ap()

    with ExitStack() as ctx:
        def sb(name, shape, dt=F32):
            return ctx.enter_context(nc.sbuf_tensor(name, shape, dt))

        def sem(name):
            return ctx.enter_context(nc.semaphore(name))

        s_held = sem("held")
        psum = ctx.enter_context(nc.psum_tensor("psum", [P, 8, 512], F32))

        x_all = sb("x_all", [P, NT, D])
        xn_all = sb("xn_all", [P, NT, D])
        edges = sb("edges", [P, 2, EC], I32)
        attr = sb("attr", [P, 3, EC])
        dst_f = sb("dst_f", [P, EC])
        score_all = sb("score_all", [P, EC])
        ident = sb("ident", [P, P])
        below = sb("below", [P, P])
        above = sb("above", [P, P])
        ones = sb("ones", [P, P])
        count_i = sb("count_i", [P, P], I32)
        count = sb("count", [P, P])
        trash_i = sb("trash_i", [P, 1], I32)
        row_id = sb("row_id", [P, 1])
        attn = sb("attn", [P, ZW])
        attn_col = sb("attn_col", [P, DC])
        win_base = sb("win_base", [P, HALVES + 2])
        win_nodes = sb("win_nodes", [P, HALVES], I32)
        big = sb("big", [P, 1])
        win_rows = sb("win_rows", [P, HALVES + 2], I32)
        fits = sb("fits", [P, 1], I32)
        bias_row = sb("bias_row", [1, 2, D])
        w3T = sb("w3T", [P, DC, 3 * D])
        wkvT = sb("wkvT", [P, DC, 2 * INNER])
        woutT = sb("woutT", [P, PAIRS, D])
        wq = sb("wq", [P, PAIRS, D])
        gw = sb("gw", [P, DC, NE])
        gb = sb("gb", [P, NE])
        b1T = sb("b1T", [P, NE * FT])
        tab_max = sb("tab_max", [P, NT])
        tab_sum = sb("tab_sum", [P, NT])
        max_rsum = sb("max_rsum", [P, NT, 2])
        zeros = sb("zeros", [P, 512])
        gate_prob = sb("gate_prob", [P, NT])
        slot_in = sb("slot_in", [P, NT], I32)
        slot_out = sb("slot_out", [P, NT], I32)
        pool_mem = sb("pool_mem", [P, 13800])

        def windowed(eng):
            return eng.value_load(fits[0:1, 0:1], min_val=0, max_val=1)

        class Arena:
            def __init__(self, memory=pool_mem, size=13800):
                self.at, self.memory, self.size = 0, memory, size

            def take(self, *shape):
                n = 1
                for s in shape:
                    n *= s
                v = self.memory[:, self.at:self.at + n]
                self.at += n
                assert self.at <= self.size, self.at
                if len(shape) == 2:
                    v = v.rearrange("p (a b) -> p a b", b=shape[1])
                if len(shape) == 3:
                    v = v.rearrange("p (a b c) -> p a b c", b=shape[1], c=shape[2])
                return v

        m = Arena()
        w3_raw = m.take(3 * DC, D)
        kv_raw = m.take(2 * INNER // P, D)
        wout_raw = m.take(DC, INNER)
        b1_raw = m.take(P)
        stats = m.take(2, 6)
        mean_var = m.take(NT, 2)
        pair = m.take(2, 2)
        variance = m.take(NT)
        rstd = m.take(NT)
        scratch = m.take(NT)
        xn = m.take(2, D)
        xnT = m.take(2, D)
        proj = m.take(2, 3, ZW)
        lin_out = m.take(4, D)
        headmean = m.take(DC, 2 * HEADS)
        hi_i = m.take(EC).bitcast(I32)
        raw_e = m.take(2, FULL_B + 1, P).bitcast(I32)
        raw_f = m.take(2, FULL_B + 1, P)
        dst_range = m.take(2, HALVES)
        extremes = m.take(2)
        misfit = m.take(1)
        diagonal = m.take(HALVES)
        window_f = m.take(HALVES)

        s_fill, s_x, s_edges, s_w = sem("fills_done"), sem("x_loaded"), sem("edges_loaded"), sem("weights_loaded")
        s_const, s_pool, s_dve = sem("constants_made"), sem("pool_steps"), sem("dve_steps")
        s_wt, s_wc = sem("weights_transposed"), sem("weights_copied")
        s_xn, s_tp, s_xt = sem("xn_ready"), sem("xn_transposed"), sem("xnT_ready")
        s_pj, s_pc, s_lin = sem("proj_ready"), sem("proj_copied"), sem("linear_terms_done")
        s_st = [sem(f"proj_stored{i}") for i in range(2)]
        s_rf, s_et, s_ec = sem("raw_edges_float"), sem("edges_transposed"), sem("edges_copied")
        s_range, s_rangeT, s_ends, s_base = sem("ranges_ready"), sem("ranges_transposed"), sem("extremes_ready"), sem("bases_broadcast")
        LOADS = 12

        jobs = []
        for c in range(DC):
            for w in range(3 * DC):
                jobs.append((w3_raw[:, w, c * P:(c + 1) * P], w3T[:, c, w * P:(w + 1) * P]))
        FIRST = len(jobs)
        for c in range(DC):
            for w in range(2 * INNER // P):
                jobs.append((kv_raw[:, w, c * P:(c + 1) * P], wkvT[:, c, w * P:(w + 1) * P]))
        for g in range(PAIRS):
            for c in range(DC):
                jobs.append((wout_raw[:, c, g * P:(g + 1) * P], woutT[:, g, c * P:(c + 1) * P]))
        GROUPS = len(jobs) // 4
        dve = Steps(nc.vector, s_dve)

        with nc.Block() as block:
            @block.sync
            def _(sp):
                sp.wait_ge(s_fill, 2)
                for j, e in enumerate((src, dst)):
                    sp.dma_start(raw_e[:, j, 0:FULL_B, :], e[0:FULL_B * P * P].rearrange("(b p c) -> p b c", p=P, c=P)).then_inc(s_edges, 16)
                    sp.dma_start(raw_e[0:FULL_T, j, FULL_B, :], e[FULL_B * P * P:FULL_B * P * P + FULL_T * P].rearrange("(p c) -> p c", c=P)).then_inc(s_edges, 16)
                    sp.dma_start(raw_e[FULL_T:FULL_T + 1, j, FULL_B, 0:REST], e[E - REST:E].rearrange("(p c) -> p c", p=1)).then_inc(s_edges, 16)
                sp.dma_start(x_all[:, 0:NT - 1, :], x[0:(NT - 1) * P, :].rearrange("(t p) c -> p t c", p=P)).then_inc(s_x, 16)
                sp.dma_start(x_all[0:TAIL, NT - 1, :], x[(NT - 1) * P:N, :]).then_inc(s_x, 16)
                for i, w in enumerate((W_s, W_t, W_fc)):
                    sp.dma_start(w3_raw[:, 2 * i:2 * i + 2, :], w.rearrange("(o p) c -> p o c", p=P)).then_inc(s_w, 16)
                sp.dma_start(kv_raw, w_qkv[INNER:3 * INNER, :].rearrange("(o p) c -> p o c", p=P)).then_inc(s_w, 16)
                sp.dma_start(wout_raw, w_out.rearrange("(o p) c -> p o c", p=P)).then_inc(s_w, 16)
                sp.dma_start(b1_raw[0:NE * FT, :], b1.rearrange("e (f p) -> (e f) p", p=P)).then_inc(s_w, 16)
                sp.dma_start(wq[:, :, :], w_qkv[0:INNER, :].rearrange("(o p) c -> p o c", p=P)).then_inc(s_w, 16)
                sp.dma_start(attn[:, 0:D], W_attn[0, :].partition_broadcast(P)).then_inc(s_w, 16)
                sp.dma_start(gw[:, :, :], gate_w.rearrange("(c p) e -> p c e", p=P)).then_inc(s_w, 16)
                sp.dma_start(gb[:, :], gate_b.partition_broadcast(P)).then_inc(s_w, 16)
                sp.dma_start(bias_row[:, 0, :], b_fc.rearrange("(a c) -> a c", a=1)).then_inc(s_w, 16)
                sp.dma_start(bias_row[:, 1, :], b_out.rearrange("(a c) -> a c", a=1)).then_inc(s_w, 16)

                def store(t, slot):
                    wait(sp, s_pc, 2 * t + 2)
                    wait(sp, s_lin, 4 * t + 4)
                    rows = span(t * P, P)
                    sp.dma_start(proj_s[rows, :], proj[:, slot, 0, :]).then_inc(s_st[slot], 16)
                    sp.dma_start(proj_t[rows, :], proj[:, slot, 1, :]).then_inc(s_st[slot], 16)
                    sp.dma_start(node_rows[rows, 0:D], proj[:, slot, 2, 0:D]).then_inc(s_st[slot], 16)

                with sp.Fori(0, NT // 2) as i:
                    store(2 * i, 0)
                    store(2 * i + 1, 1)
                store(NT - 1, 0)
                sp.wait_ge(s_rf, 1)
                for j in range(2):
                    sp.dma_start(edge_rows[j, 0:FULL_B * P * P].rearrange("(b p c) -> p b c", p=P, c=P), raw_f[:, j, 0:FULL_B, :]).then_inc(s_edges, 16)
                    sp.dma_start(edge_rows[j, FULL_B * P * P:ET * P].rearrange("(p c) -> p c", c=P), raw_f[0:ET - FULL_B * P, j, FULL_B, :]).then_inc(s_edges, 16)
                sp.wait_ge(s_edges, 16 * 10)
                sp.wait_ge(s_st[0], 48 * (NT // 2 + 1))
                sp.wait_ge(s_st[1], 48 * (NT // 2))

            @block.gpsimd
            def _(g):
                st = Steps(g, s_pool)
                st.done(g.memset(ident[:, :], 0.0))
                st.done(g.memset(below[:, :], 0.0))
                st.done(g.memset(above[:, :], 0.0))
                st.done(g.iota(count_i[:, :], [[1, P]], base=0, channel_multiplier=0))
                st.then(g.iota(trash_i[:, :], [[0, 1]], base=0, channel_multiplier=1))
                g.affine_select(out=ident[:, :], in_=ident[:, :], compare_op=ALU.not_equal, fill=1.0, base=0,
                                pattern=[[-1, P]], channel_multiplier=1).then_inc(s_const, 1)
                g.affine_select(out=below[:, :], in_=below[:, :], compare_op=ALU.is_ge, fill=1.0, base=0,
                                pattern=[[1, P]], channel_multiplier=-1).then_inc(s_const, 1)
                g.affine_select(out=above[:, :], in_=above[:, :], compare_op=ALU.is_ge, fill=1.0, base=0,
                                pattern=[[-1, P]], channel_multiplier=1).then_inc(s_const, 1)

            @block.vector
            def _(v):
                v.memset(x_all[96:P, NT - 1, :], 0.0).then_inc(s_fill, 1)
                v.memset(raw_e, PAD_NODE).then_inc(s_fill, 1)
                dve.done(v.memset(ones[:, :], 1.0))
                dve.done(v.memset(attn[:, D:D + 1], 1.0))
                dve.done(v.memset(attn[:, D + 1:ZW], -1.0))
                dve.done(v.memset(zeros[:, :], 0.0))
                dve.done(v.memset(score_all[:, :], 0.0))
                dve.done(v.memset(tab_max[:, :], -BIG))
                dve.done(v.memset(tab_sum[:, :], 0.0))
                v.wait_ge(s_edges, 96)
                v.tensor_copy(raw_f, raw_e).then_inc(s_rf, 1)
                v.wait_ge(s_x, 32)

                def measure(t, slot):
                    dve.done(v.bn_stats(stats[:, slot, :], at(x_all, t)))
                    dve.hold(s_held)
                    dve.then(v.bn_aggr(pair[:, slot, :], stats[:, slot, :]))
                    dve.done(v.tensor_copy(at(mean_var, t), pair[:, slot, :]))

                measure(0, 0)
                with v.Fori(0, NT // 2) as i:
                    dve.enter(i, 0, 6)
                    measure(2 * i + 1, 1)
                    measure(2 * i + 2, 0)
                dve.leave(NT // 2)
                dve.wait()
                dve.then(v.tensor_scalar(variance, mean_var[:, :, 1], LN_EPS, None, ALU.add))
                rsqrt(v, dve, rstd, variance, scratch)

                def norm(t, slot):
                    wait(v, s_tp, t - 1)
                    v.tensor_scalar(xn[:, slot, :], at(x_all, t), at(mean_var, t)[:, 0:1], rstd[:, span(t, 1)],
                                    ALU.subtract, ALU.mult).then_inc(s_xn, 1)

                def linear(t, slot):
                    wait(v, s_pc, 2 * t + 1)
                    wait(v, s_lin, 4 * t)
                    for w in range(2):
                        for k, sign in ((0, 1.0), (1, -1.0)):
                            v.tensor_tensor_reduce(lin_out[:, 2 * w + k, :], proj[:, slot, w, 0:D], attn[:, 0:D],
                                                   sign * SLOPE / (1.0 - SLOPE), 0.0, ALU.mult, ALU.add,
                                                   proj[:, slot, w, D + k:D + k + 1]).then_inc(s_lin, 1)

                norm(0, 0)
                norm(1, 1)
                norm(2, 0)
                linear(0, 0)
                norm(3, 1)
                linear(1, 1)
                with v.Fori(1, NT // 2 - 1) as i:
                    norm(2 * i + 2, 0)
                    linear(2 * i, 0)
                    norm(2 * i + 3, 1)
                    linear(2 * i + 1, 1)
                norm(NT - 1, 0)
                linear(NT - 3, 0)
                linear(NT - 2, 1)
                linear(NT - 1, 0)

                v.wait_ge(s_pool, 5)
                dve.done(v.tensor_copy(count[:, :], count_i[:, :]))
                dve.done(v.tensor_copy(row_id[:, :], trash_i[:, :]))
                dve.done(v.memset(attr[:, 0, ET:EC], PAD_NODE))
                dve.done(v.memset(dst_f[:, ET:EC], PAD_NODE))
                for b in range(FULL_B + 1):
                    n = min(P, ET - b * P)
                    v.wait_ge(s_et, b + 1)
                    dve.done(v.tensor_copy(attr[:, 0, b * P:b * P + n], psum[:, b % 2, 0:n]))
                    dve.then(v.tensor_copy(dst_f[:, b * P:b * P + n], psum[:, b % 2, P:P + n]))
                    v.sem_inc(s_ec, 1)
                dve.done(v.tensor_copy(edges[:, 0, :], attr[:, 0, :]))
                dve.then(v.tensor_copy(edges[:, 1, :], dst_f[:, :]))
                dve.then(v.tensor_scalar(hi_i, edges[:, 0, :], P.bit_length() - 1, None, ALU.arith_shift_right))
                dve.then(v.tensor_copy(attr[:, 1, :], hi_i))
                dve.then(v.scalar_tensor_tensor(out=attr[:, 2, :], in0=attr[:, 1, :], scalar=-float(P), in1=attr[:, 0, :],
                                                op0=ALU.mult, op1=ALU.add))
                by_half = dst_f[:, 0:ET].rearrange("p (k t) -> p k t", t=HALF)
                v.tensor_reduce(dst_range[:, 0, :], by_half, AX.X, ALU.min).then_inc(s_range, 1)
                v.tensor_reduce(dst_range[:, 1, :], by_half, AX.X, ALU.max).then_inc(s_range, 1)
                v.wait_ge(s_rangeT, 1)
                dve.done(v.tensor_reduce(extremes[0:HALVES, 0:1], psum[0:HALVES, 2, 0:P], AX.X, ALU.min))
                dve.then(v.tensor_reduce(extremes[0:HALVES, 1:2], psum[0:HALVES, 2, P:2 * P], AX.X, ALU.max))
                dve.then(v.tensor_tensor(misfit[0:HALVES, :], extremes[0:HALVES, 1:2], extremes[0:HALVES, 0:1], ALU.subtract))
                v.tensor_scalar(misfit[0:HALVES, :], misfit[0:HALVES, :], P - 0.5, None, ALU.is_gt).then_inc(s_ends, 1)
                v.tensor_scalar(diagonal[0:HALVES, :], ident[0:HALVES, 0:HALVES], extremes[0:HALVES, 0:1], None, ALU.mult).then_inc(s_ends, 1)
                v.wait_ge(s_base, 1)
                dve.done(v.memset(win_rows[:, HALVES:], 0))
                dve.done(v.memset(win_base[:, HALVES:], 0.0))
                dve.done(v.memset(big[:, :], BIG))
                dve.then(v.tensor_copy(win_base[:, 0:HALVES], psum[:, 3, 0:HALVES]))
                dve.done(v.tensor_copy(attn_col[:, :], psum[:, 3, HALVES + 1:HALVES + 1 + DC]))
                dve.done(v.tensor_scalar(fits[:, :], psum[:, 3, HALVES:HALVES + 1], 0.5, None, ALU.is_lt))
                dve.then(v.tensor_scalar(window_f, win_base[:, 0:HALVES], row_id[:, :], None, ALU.add))
                dve.done(v.tensor_copy(win_nodes[:, :], window_f))
                dve.then(v.tensor_scalar(window_f, window_f, float(NP - 1), None, ALU.min))
                dve.done(v.tensor_copy(win_rows[:, 0:HALVES], window_f))
                v.wait_ge(s_wc, GROUPS + 1)
                for c in range(DC):
                    w = wkvT[:, c, :].rearrange("p (h d) -> p h d", d=DH)
                    dve.then(v.tensor_reduce(headmean[:, c, :], w, AX.X, ALU.add))
                    dve.then(v.tensor_scalar(headmean[:, c, :], headmean[:, c, :], 1.0 / DH, None, ALU.mult))
                    dve.then(v.tensor_tensor(w, w, headmean[:, c, :].unsqueeze(2).to_broadcast([P, 2 * HEADS, DH]),
                                             ALU.subtract))

            @block.tensor
            def _(pe):
                pe.wait_ge(s_const, 3)
                pe.wait_ge(s_w, 16 * LOADS)

                def transposes(a, b):
                    for q in range(a, b):
                        wait(pe, s_wc, q - 1)
                        for k in range(4):
                            mm = pe.transpose(psum[:, q % 2, k * P:(k + 1) * P], jobs[4 * q + k][0], ident[:, :])
                        mm.then_inc(s_wt, 1)

                transposes(0, FIRST // 4)

                def turn(t, slot):
                    wait(pe, s_xn, t + 1)
                    wait(pe, s_xt, t - 1)
                    for c in range(DC):
                        mm = pe.transpose(psum[:, 6 + slot, c * P:(c + 1) * P], xn[:, slot, c * P:(c + 1) * P], ident[:, :])
                    mm.then_inc(s_tp, 1)

                def project(t, slot):
                    wait(pe, s_xt, t + 1)
                    wait(pe, s_pc, 2 * t - 2)
                    for a, b, bank in ((0, 512, 2 + 2 * slot), (512, 3 * D, 3 + 2 * slot)):
                        for c in range(DC):
                            mm = pe.matmul(psum[:, bank, 0:b - a], xnT[:, slot, c * P:(c + 1) * P], w3T[:, c, a:b],
                                           start=(c == 0), stop=(c == DC - 1))
                    mm.then_inc(s_pj, 1)

                pe.wait_ge(s_wc, FIRST // 4)
                turn(0, 0)
                turn(1, 1)
                project(0, 0)
                turn(2, 0)
                project(1, 1)
                with pe.Fori(1, NT // 2) as i:
                    turn(2 * i + 1, 1)
                    project(2 * i, 0)
                    turn(2 * i + 2, 0)
                    project(2 * i + 1, 1)
                project(NT - 1, 0)
                transposes(FIRST // 4, GROUPS)
                pe.wait_ge(s_wc, GROUPS - 1)
                mm = pe.transpose(psum[:, GROUPS % 2, 0:NE * FT], b1_raw[0:NE * FT, :], ident[0:NE * FT, 0:NE * FT])
                mm.then_inc(s_wt, 1)
                pe.wait_ge(s_wc, GROUPS + 1)
                pe.wait_ge(s_rf, 1)
                for b in range(FULL_B + 1):
                    n = min(P, ET - b * P)
                    wait(pe, s_ec, b - 1)
                    for j in range(2):
                        mm = pe.transpose(psum[:, b % 2, j * P:j * P + n], raw_f[0:n, j, b, :], ident[0:n, 0:n])
                    mm.then_inc(s_et, 1)
                pe.wait_ge(s_range, 2)
                for j in range(2):
                    mm = pe.transpose(psum[0:HALVES, 2, j * P:(j + 1) * P], dst_range[:, j, :], ident[:, :])
                mm.then_inc(s_rangeT, 1)
                pe.wait_ge(s_ends, 2)
                pe.matmul(psum[:, 3, 0:HALVES], ones[0:HALVES, :], diagonal[0:HALVES, :], start=True, stop=True)
                for c in range(DC):
                    pe.matmul(psum[:, 3, HALVES + 1 + c:HALVES + 2 + c], attn[0:1, c * P:(c + 1) * P], ones[0:1, 0:1], start=True, stop=True)
                pe.matmul(psum[:, 3, HALVES:HALVES + 1], ones[0:HALVES, :], misfit[0:HALVES, :], start=True, stop=True).then_inc(s_base, 1)

            @block.scalar
            def _(act):
                def copies(a, b):
                    for q in range(a, b):
                        act.wait_ge(s_wt, q + 1)
                        d0, d2 = jobs[4 * q][1], jobs[4 * q + 2][1]
                        for k in range(4):
                            ins = act.copy(jobs[4 * q + k][1], psum[:, q % 2, k * P:(k + 1) * P])
                        ins.then_inc(s_wc, 1)

                def take(t, slot):
                    wait(act, s_tp, t + 1)
                    wait(act, s_pj, t - 1)
                    act.copy(at(xn_all, t), psum[:, 6 + slot, 0:D])
                    act.copy(xnT[:, slot, :], psum[:, 6 + slot, 0:D]).then_inc(s_xt, 1)

                def give(t, slot):
                    wait(act, s_pj, t + 1)
                    wait(act, s_st[slot], 24 * t - 24 * slot)
                    act.copy(proj[:, slot, 0:2, 0:D], psum[:, 2 + 2 * slot, :].rearrange("p (w c) -> p w c", c=D)).then_inc(s_pc, 1)
                    act.copy(proj[:, slot, 2, 0:D], psum[:, 3 + 2 * slot, 0:D]).then_inc(s_pc, 1)

                copies(0, FIRST // 4)
                take(0, 0)
                take(1, 1)
                give(0, 0)
                take(2, 0)
                give(1, 1)
                with act.Fori(1, NT // 2) as i:
                    take(2 * i + 1, 1)
                    give(2 * i, 0)
                    take(2 * i + 2, 0)
                    give(2 * i + 1, 1)
                give(NT - 1, 0)
                copies(FIRST // 4, GROUPS)
                act.wait_ge(s_wt, GROUPS + 1)
                act.copy(b1T[:, :], psum[:, GROUPS % 2, 0:NE * FT]).then_inc(s_wc, 1)

        m = Arena()
        idx = [m.take(2, HALF).bitcast(I32) for _ in range(2)]
        at3 = [m.take(3, HALF) for _ in range(2)]
        z = m.take(PASS, ZW)
        lk = m.take(4, ZW)
        ttr_out = m.take(2, ZW)
        score = [m.take(HALF) for _ in range(2)]
        pen = m.take(2, P)
        top = m.take(HALF)
        expo = m.take(HALF)
        lo_hot = [m.take(HALF, P) for _ in range(2)]
        hi_hot = [m.take(HALF, TABW) for _ in range(2)]
        tabs = m.take(HALF, TABW)
        cnt = m.take(HALF, NT)
        new_max = m.take(NT)
        scale_old = m.take(NT)
        part = m.take(NT)

        s_idx, s_zin1, s_zin = sem("indices_ready"), [sem(f"proj_s_in{i}") for i in range(HALF // 2)], [sem(f"z_in{i}") for i in range(PASS)]
        s_lk, s_sc, s_row, s_top = sem("leaky_done"), sem("score_done"), sem("rows_broadcast"), sem("top_done")
        s_dif, s_exp, s_hot = sem("top_difference"), sem("exp_done"), sem("hot_ready")
        s_tab, s_ev, s_mrg, s_df2, s_ex2 = sem("tables_ready"), sem("tables_copied"), sem("merge_done"), sem("merge_differences"), sem("merge_exps")

        s_zero = sem("zeros_stored")

        m = Arena()
        w_idx = [m.take(HALF).bitcast(I32) for _ in range(2)]
        w_win = [m.take(1).bitcast(I32) for _ in range(2)]
        s_rows_w = m.take(PASS, ZW)
        t_win = m.take(2, ZW)
        dot_w = m.take(4, ZW)
        attn_w = m.take(ZW)
        pen_w = m.take(HALF, P)
        same_w = m.take(2, P)
        ttr_w = m.take(HALF, P)
        vals = [m.take(HALF, 2 * NT) for _ in range(2)]
        m = Arena(x_all[:, :, :].rearrange("p t c -> p (t c)"), NT * D)
        dst_row = m.take(HALF * P)
        src_row = m.take(HALF * P)
        hot_T = m.take(HALF * P)
        lo_w = [m.take(HALF, P) for _ in range(2)]
        hi_w = m.take(HALF, NT)
        gone = m.take(HALF, NT)
        run = m.take(HALF, NT)
        wsum = m.take(HALF, NT)
        new_max_w = m.take(NT)
        scale_w = m.take(NT)
        part_w = m.take(NT)
        score_w = [m.take(HALF) for _ in range(2)]
        neg_src = [m.take(HALF) for _ in range(2)]
        same_count = m.take(HALF)
        inv_count = m.take(HALF)
        top_w = m.take(HALF)
        top_share = m.take(HALF)
        expo_w = m.take(HALF)
        Z_BANK = (0, 1, 2, 7)
        APART = 2.0 ** 100

        s_in = s_zin[0:2]
        s_dstr, s_srcr = s_zin1[0:2]
        s_gone, s_tread = s_ev, s_mrg
        s_hotT, s_z = sem("window_hot_ready"), sem("z_ready")
        s_neg, s_pen, s_cnt = sem("neg_src_ready"), sem("pen_ready"), sem("counts_ready")
        s_path2, s_last2 = sem("path_steps2"), sem("last_steps2")

        with nc.Block() as block:
            @block.gpsimd
            def _(g):
                with g.If(windowed(g) > 0):
                    def fetch(i, h):
                        k = 2 * i + h
                        hold(g, s_idx, k + 1, s_held)
                        hold(g, s_z, HALF * (k - 1), s_held)
                        for u in range(HALF):
                            g.indirect_dma_start(s_rows_w[:, HALF * h + u, :], None, proj_s, bass.IndirectOffsetOnAxis(
                                ap=w_idx[h][:, u:u + 1], axis=0)).then_inc(s_in[h], 16)
                        g.indirect_dma_start(t_win[:, h, :], None, proj_t, bass.IndirectOffsetOnAxis(
                            ap=w_win[h], axis=0)).then_inc(s_in[h], 16)

                    fetch(0, 0)
                    fetch(0, 1)
                    with g.Fori(1, PASSES) as i:
                        fetch(i, 0)
                        fetch(i, 1)
                with g.Else():
                    def half(i, h):
                        k = 2 * i + h
                        hold(g, s_idx, k + 1, s_held)

                        LAG = HALF // 2

                        def first(u):
                            g.indirect_dma_start(z[:, HALF * h + u, :], None, proj_s, bass.IndirectOffsetOnAxis(
                                ap=idx[h][:, 0, u:u + 1], axis=0)).then_inc(s_zin1[u % LAG], 16)

                        def second(u):
                            hold(g, s_zin1[u % LAG], 16 * (2 * k + u // LAG + 1), s_held)
                            g.indirect_dma_start(z[:, HALF * h + u, :], None, proj_t, bass.IndirectOffsetOnAxis(
                                ap=idx[h][:, 1, u:u + 1], axis=0), compute_op=ALU.add).then_inc(s_zin[HALF * h + u], 16)

                        for u in range(LAG):
                            first(u)
                        for u in range(LAG):
                            second(u)
                            first(u + LAG)
                        for u in range(LAG, HALF):
                            second(u)

                    with g.Fori(0, PASSES) as i:
                        half(i, 0)
                        half(i, 1)

            @block.scalar
            def _(act):
                with act.If(windowed(act) > 0):
                    def penalties(i, h):
                        k = 2 * i + h
                        wait(act, s_neg, k + 1)
                        wait(act, s_srcr, 16 * k + 16)
                        for u in range(HALF):
                            wait(act, s_top, HALF * (k - 1) + u + 1)
                            act.activation(pen_w[:, u, :], src_row[:, u * P:(u + 1) * P], ACT.Abs, scale=APART,
                                           bias=neg_src[h][:, u:u + 1]).then_inc(s_pen, 1)
                        for u in range(HALF):
                            wait(act, s_pen, HALF * k + u + 1)
                            wait(act, s_cnt, HALF * k + u - 1)
                            act.activation(same_w[:, u % 2, :], pen_w[:, u, :], ACT.Relu, scale=-1.0, bias=ones[:, 0:1],
                                           accum_out=same_count[:, u:u + 1]).then_inc(s_cnt, 1)

                    def absent(k):
                        wait(act, s_df2, 2 * k)
                        for b in range(2):
                            wait(act, s_tab, 2 * k + b + 1)
                            act.activation(gone[:, 4 * b:4 * b + 4, :], psum[:, 5 + b, 0:8 * NT].rearrange("p (t c) -> p t c", c=2 * NT)[:, :, NT:2 * NT],
                                           ACT.Relu, scale=-2.0 * BIG, bias=big[:, :]).then_inc(s_gone, 1)

                    def merge_exps_w(k):
                        wait(act, s_df2, 2 * k + 2)
                        act.activation(run, run, ACT.Exp).then_inc(s_ex2, 1)
                        act.activation(scale_w, scale_w, ACT.Exp).then_inc(s_ex2, 1)

                    def step(i, h, first=False, last=False):
                        k = 2 * i + h
                        if not first:
                            absent(k - 1)
                        wait(act, s_dif, k + 1)
                        act.activation(expo_w, expo_w, ACT.Exp).then_inc(s_exp, 1)
                        if not first:
                            merge_exps_w(k - 1)
                        if not last:
                            penalties(*((i, 1) if h == 0 else (i + 1, 0)))

                    penalties(0, 0)
                    step(0, 0, first=True)
                    step(0, 1)
                    with act.Fori(1, PASSES - 1) as i:
                        step(i, 0)
                        step(i, 1)
                    step(PASSES - 1, 0)
                    step(PASSES - 1, 1, last=True)
                    absent(HALVES - 1)
                    merge_exps_w(HALVES - 1)
                with act.Else():
                    def leaky(i, h, u):
                        T = PASS * i + HALF * h + u
                        wait(act, s_zin[HALF * h + u], 16 * (i + 1))
                        wait(act, s_sc, T - 3)
                        act.activation(lk[:, u % 4, :], z[:, HALF * h + u, :], ACT.Relu, scale=1.0 - SLOPE).then_inc(s_lk, 1)

                    def copy_tables(i, h, b):
                        k = 2 * i + h
                        wait(act, s_tab, 4 * k + b + 1)
                        wait(act, s_mrg, k)
                        act.copy(tabs[:, 2 * b:2 * b + 2, :], psum[:, 4 + b, 0:2 * TABW].rearrange("p (t c) -> p t c", c=TABW)).then_inc(s_ev, 1)

                    def merge_exps(k):
                        wait(act, s_df2, k + 1)
                        act.activation(tabs[:, :, 0:NT], tabs[:, :, 0:NT], ACT.Exp).then_inc(s_ex2, 1)
                        act.activation(scale_old, scale_old, ACT.Exp).then_inc(s_ex2, 1)

                    def half(i, h):
                        k = 2 * i + h
                        for u in range(6):
                            leaky(i, h, u)
                        for b in range(4):
                            copy_tables(i, h, b)
                        leaky(i, h, 6)
                        leaky(i, h, 7)
                        merge_exps(k)
                        wait(act, s_dif, k + 1)
                        act.activation(expo, expo, ACT.Exp).then_inc(s_exp, 1)

                    half(0, 0)
                    half(0, 1)
                    with act.Fori(1, PASSES) as i:
                        half(i, 0)
                        half(i, 1)
                    for b in range(4):
                        copy_tables(PASSES, 0, b)
                    merge_exps(2 * PASSES)

            @block.tensor
            def _(pe):
                with pe.If(windowed(pe) > 0):
                    def sum_z(i, h):
                        k = 2 * i + h
                        wait(pe, s_hotT, k + 1)
                        wait(pe, s_in[h], 16 * (HALF + 1) * (i + 1))
                        for u in range(HALF):
                            wait(pe, s_sc, HALF * k + u - 3)
                            pe.matmul(psum[:, Z_BANK[u % 4], 0:ZW], hot_T[:, u * P:(u + 1) * P], t_win[:, h, :], start=True, stop=False)
                            pe.matmul(psum[:, Z_BANK[u % 4], 0:ZW], ident[:, :], s_rows_w[:, HALF * h + u, :], start=False, stop=True).then_inc(s_z, 1)

                    def spread(i, h):
                        k = 2 * i + h
                        wait(pe, s_sc, HALF * k + HALF)
                        wait(pe, s_top, HALF * k)
                        for u in range(HALF):
                            mm = pe.matmul(psum[:, 3 + u // 4, (u % 4) * P:(u % 4 + 1) * P], score_w[h][:, u:u + 1].to_broadcast([P, P]),
                                           ident[:, :], start=True, stop=True)
                            if u % 4 == 3:
                                mm.then_inc(s_row, 1)

                    def tables(i, h):
                        k = 2 * i + h
                        wait(pe, s_hot, k + 1)
                        wait(pe, s_gone, 2 * k)
                        wait(pe, s_tread, k)
                        for u in range(HALF):
                            mm = pe.matmul(psum[:, 5 + u // 4, (u % 4) * 2 * NT:(u % 4 + 1) * 2 * NT], lo_w[h][:, u, :], vals[h][:, u, :],
                                           start=True, stop=True)
                            if u % 4 == 3:
                                mm.then_inc(s_tab, 1)

                    def step(i, h):
                        nxt = (i, 1) if h == 0 else (i + 1, 0)
                        sum_z(*nxt)
                        tables(i, h)
                        spread(*nxt)

                    sum_z(0, 0)
                    spread(0, 0)
                    step(0, 0)
                    step(0, 1)
                    with pe.Fori(1, PASSES - 1) as i:
                        step(i, 0)
                        step(i, 1)
                    step(PASSES - 1, 0)
                    tables(PASSES - 1, 1)
                with pe.Else():
                    for b in range(4):
                        pe.matmul(psum[:, 4 + b, 0:2 * TABW], zeros[:, 0:P], zeros[:, 0:2 * TABW], start=True, stop=True).then_inc(s_tab, 1)

                    def half(i, h):
                        k = 2 * i + h
                        for u in range(HALF):
                            T = HALF * k + u
                            wait(pe, s_sc, T + 1)
                            if u % 2 == 0:
                                wait(pe, s_top, T - HALF + 2)
                            row = psum[:, u // 2, (u % 2) * 2 * P:(u % 2) * 2 * P + 2 * P]
                            pe.matmul(row[:, 0:P], at3[h][:, 0, u:u + 1].to_broadcast([P, P]), ident[:, :], start=True, stop=True)
                            mm = pe.matmul(row[:, P:2 * P], score[h][:, u:u + 1].to_broadcast([P, P]), ident[:, :], start=True,
                                           stop=True)
                            if u % 2 == 1:
                                mm.then_inc(s_row, 1)
                        wait(pe, s_hot, k + 1)
                        for b in range(4):
                            wait(pe, s_ev, 4 * k + b + 1)
                            for j in range(2):
                                u = 2 * b + j
                                mm = pe.matmul(psum[:, 4 + b, j * TABW:(j + 1) * TABW], lo_hot[h][:, u, :], hi_hot[h][:, u, :],
                                               start=True, stop=True)
                            mm.then_inc(s_tab, 1)

                    half(0, 0)
                    half(0, 1)
                    with pe.Fori(1, PASSES) as i:
                        half(i, 0)
                        half(i, 1)

            @block.vector
            def _(v):
                with v.If(windowed(v) > 0):
                    dve = Steps(v, s_path2)

                    def indices(k, h):
                        dve.done(v.tensor_copy(w_win[h], win_rows[:, span(k, 1)]))
                        v.tensor_copy(w_idx[h], edges[:, 0, span(HALF * k, HALF)]).then_inc(s_idx, 1)

                    def sources(k, h):
                        v.tensor_scalar(neg_src[h], attr[:, 0, span(HALF * k, HALF)], -APART, None, ALU.mult).then_inc(s_neg, 1)

                    def hot(k):
                        wait(v, s_dstr, 16 * k + 16)
                        v.tensor_scalar(hot_T, dst_row, win_base[:, span(k, 1)], row_id[:, :], ALU.subtract, ALU.is_equal).then_inc(s_hotT, 1)

                    def table(c):
                        return psum[:, 5:7, 0:8 * NT].rearrange("p b (t c) -> p b t c", c=2 * NT)[:, :, :, c * NT:(c + 1) * NT]

                    def quads(a):
                        return a.rearrange("p (b t) c -> p b t c", t=4)

                    def weighted_sum(k, h, u):
                        hold(v, s_z, HALF * k + u + 1, s_held)
                        v.scalar_tensor_tensor(out=dot_w[:, u % 4, :], in0=psum[:, Z_BANK[u % 4], 0:ZW], scalar=0.0, in1=attn_w, op0=ALU.max,
                                               op1=ALU.mult, accum_out=score_w[h][:, u:u + 1]).then_inc(s_sc, 1)

                    def merge(k, other):
                        wait(v, s_gone, 2 * k + 2)
                        dve.done(v.tensor_tensor(quads(run), table(0), quads(gone), ALU.subtract))
                        other(0)
                        dve.wait()
                        dve.done(v.tensor_reduce(new_max_w, run.rearrange("p t n -> p n t"), AX.X, ALU.max))
                        other(1)
                        dve.wait()
                        dve.done(v.tensor_tensor(new_max_w, new_max_w, tab_max[:, :], ALU.max))
                        other(2)
                        dve.wait()
                        v.tensor_tensor(run, run, new_max_w.unsqueeze(1).to_broadcast([P, HALF, NT]), ALU.subtract).then_inc(s_df2, 1)
                        v.tensor_tensor(scale_w, tab_max[:, :], new_max_w, ALU.subtract).then_inc(s_df2, 1)
                        other(3)
                        wait(v, s_df2, 2 * k + 2)
                        dve.done(v.tensor_copy(tab_max[:, :], new_max_w))
                        other(4)
                        other(5)
                        wait(v, s_ex2, 2 * k + 2)
                        v.tensor_tensor(quads(wsum), quads(run), table(1), ALU.mult).then_inc(s_tread, 1)
                        dve.done(v.tensor_tensor(tab_sum[:, :], tab_sum[:, :], scale_w, ALU.mult))
                        other(6)
                        wait(v, s_tread, k + 1)
                        dve.done(v.tensor_reduce(part_w, wsum.rearrange("p t n -> p n t"), AX.X, ALU.add))
                        other(7)
                        dve.wait()
                        dve.done(v.tensor_tensor(tab_sum[:, :], tab_sum[:, :], part_w, ALU.add))
                    PER_MERGE = 7

                    def step(i, h, first=False, last=False, ending=False):
                        k = 2 * i + h

                        def next_score(u):
                            if not last:
                                weighted_sum(k + 1, 1 - h, u)

                        if not last:
                            hot(k + 1)
                        wait(v, s_tab, 2 * k - 2)
                        lo = attr[:, 2, span(HALF * k, HALF)].unsqueeze(2).to_broadcast([P, HALF, P])
                        hi = attr[:, 1, span(HALF * k, HALF)].unsqueeze(2).to_broadcast([P, HALF, NT])
                        dve.done(v.tensor_tensor(lo_w[h], lo, count[:, :].unsqueeze(1).to_broadcast([P, HALF, P]), ALU.is_equal))
                        dve.done(v.tensor_tensor(hi_w, hi, count[:, 0:NT].unsqueeze(1).to_broadcast([P, HALF, NT]), ALU.is_equal))
                        wait(v, s_cnt, HALF * k + HALF)
                        dve.done(v.reciprocal(inv_count, same_count))
                        for u in range(HALF):
                            if u % 4 == 0:
                                hold(v, s_row, 2 * k + u // 4 + 1, s_held)
                            v.tensor_tensor_reduce(ttr_w[:, u, :], psum[:, 3 + u // 4, (u % 4) * P:(u % 4 + 1) * P], pen_w[:, u, :], 1.0, -3.0e38,
                                                   ALU.subtract, ALU.max, top_w[:, u:u + 1]).then_inc(s_top, 1)
                        dve.done(v.tensor_copy(score_all[:, span(HALF * k, HALF)], score_w[h]))
                        wait(v, s_top, HALF * k + HALF)
                        v.tensor_tensor(expo_w, score_w[h], top_w, ALU.subtract).then_inc(s_dif, 1)
                        dve.done(v.tensor_tensor(top_share, top_w, inv_count, ALU.mult))
                        if not ending:
                            wait(v, s_in[1 - h], 16 * (HALF + 1) * (i + 1 + h))
                            indices(k + 3, 1 - h)
                            sources(k + 2, h)
                        dve.wait()
                        dve.done(v.tensor_tensor(vals[h][:, :, 0:NT], hi_w, top_share.unsqueeze(2).to_broadcast([P, HALF, NT]), ALU.mult))
                        wait(v, s_exp, k + 1)
                        v.tensor_tensor(vals[h][:, :, NT:2 * NT], hi_w, expo_w.unsqueeze(2).to_broadcast([P, HALF, NT]), ALU.mult).then_inc(s_hot, 1)
                        if first:
                            for u in range(HALF):
                                next_score(u)
                        else:
                            merge(k - 1, next_score)
                        if not last:
                            wait(v, s_sc, HALF * k + 2 * HALF)
                        dve.wait()
                        wait(v, s_hot, k + 1)
                    PER_STEP = 3 + 1 + 1 + 1 + 1 + PER_MERGE

                    dve.then(v.tensor_scalar(attn_w, attn[:, :], 1.0 - SLOPE, None, ALU.mult))
                    indices(0, 0)
                    indices(1, 1)
                    sources(0, 0)
                    sources(1, 1)
                    hot(0)
                    wait(v, s_in[0], 16 * (HALF + 1))
                    indices(2, 0)
                    for u in range(HALF):
                        weighted_sum(0, 0, u)
                    wait(v, s_sc, HALF)
                    step(0, 0, first=True)
                    step(0, 1)
                    with v.Fori(1, PASSES - 1) as i:
                        dve.enter(i, 1, 2 * PER_STEP)
                        step(i, 0)
                        step(i, 1)
                    dve.leave(PASSES - 2)
                    step(PASSES - 1, 0, ending=True)
                    step(PASSES - 1, 1, last=True, ending=True)
                    merge(HALVES - 1, lambda u: None)
                    dve.wait()
                with v.Else():
                    dve = Steps(v, s_path2)

                    def prepare(i, h):
                        c = span(PASS * i + HALF * h, HALF)
                        dve.done(v.tensor_copy(at3[h], attr[:, :, c]))
                        v.tensor_copy(idx[h], edges[:, :, c]).then_inc(s_idx, 1)

                    def merge(k):
                        wait(v, s_ev, 4 * k + 4)
                        cn = tabs[:, :, NT:2 * NT]
                        tm = tabs[:, :, 0:NT]
                        ts = tabs[:, :, 2 * NT:3 * NT]
                        dve.then(v.tensor_scalar(cnt, cn, 1.0, None, ALU.max))
                        dve.then(v.reciprocal(cnt, cnt))
                        dve.then(v.tensor_tensor(tm, tm, cnt, ALU.mult))
                        dve.then(v.tensor_scalar(cnt, cn, 0.5, -BIG, ALU.is_lt, ALU.mult))
                        dve.then(v.tensor_tensor(tm, tm, cnt, ALU.add))
                        dve.then(v.tensor_reduce(new_max, tm.rearrange("p t n -> p n t"), AX.X, ALU.max))
                        dve.then(v.tensor_tensor(new_max, new_max, tab_max[:, :], ALU.max))
                        dve.then(v.tensor_tensor(scale_old, tab_max[:, :], new_max, ALU.subtract))
                        v.tensor_tensor(tm, tm, new_max.unsqueeze(1).to_broadcast([P, HALF, NT]), ALU.subtract).then_inc(s_df2, 1)
                        dve.done(v.tensor_copy(tab_max[:, :], new_max))
                        wait(v, s_ex2, 2 * k + 2)
                        dve.then(v.tensor_tensor(tm, tm, ts, ALU.mult))
                        dve.then(v.tensor_reduce(part, tm.rearrange("p t n -> p n t"), AX.X, ALU.add))
                        dve.then(v.tensor_tensor(tab_sum[:, :], tab_sum[:, :], scale_old, ALU.mult))
                        v.tensor_tensor(tab_sum[:, :], tab_sum[:, :], part, ALU.add).then_inc(s_mrg, 1)
                        wait(v, s_mrg, k + 1)
                    MERGE = 12

                    def half(i, h):
                        k = 2 * i + h
                        for u in range(HALF):
                            T = HALF * k + u
                            wait(v, s_sc, T - 1)
                            wait(v, s_lk, T + 1)
                            v.tensor_tensor_reduce(ttr_out[:, u % 2, :], lk[:, u % 4, :], attn[:, :], 1.0, 0.0, ALU.mult, ALU.add,
                                                   score[h][:, u:u + 1]).then_inc(s_sc, 1)
                        merge(k)
                        lo = at3[h][:, 2, :].unsqueeze(2).to_broadcast([P, HALF, P])
                        hi = at3[h][:, 1, :].unsqueeze(2).to_broadcast([P, HALF, NT])
                        dve.done(v.tensor_tensor(lo_hot[h], lo, count[:, :].unsqueeze(1).to_broadcast([P, HALF, P]), ALU.is_equal))
                        dve.done(v.tensor_tensor(hi_hot[h][:, :, NT:2 * NT], hi, count[:, 0:NT].unsqueeze(1).to_broadcast([P, HALF, NT]),
                                                 ALU.is_equal))
                        for u in range(HALF):
                            T = HALF * k + u
                            wait(v, s_top, T - 1)
                            wait(v, s_row, HALF // 2 * k + u // 2 + 1)
                            row = psum[:, u // 2, (u % 2) * 2 * P:(u % 2) * 2 * P + 2 * P]
                            dve.done(v.tensor_scalar(pen[:, u % 2, :], row[:, 0:P], at3[h][:, 0, u:u + 1], -BIG, ALU.not_equal, ALU.mult))
                            dve.hold(s_held)
                            v.tensor_tensor_reduce(ttr_out[:, u % 2, 0:P], row[:, P:2 * P], pen[:, u % 2, :], 1.0, -3.0e38, ALU.add, ALU.max,
                                                   top[:, u:u + 1]).then_inc(s_top, 1)
                        wait(v, s_top, HALF * k + HALF)
                        v.tensor_tensor(expo, score[h], top, ALU.subtract).then_inc(s_dif, 1)
                        hot = hi_hot[h][:, :, NT:2 * NT]
                        dve.done(v.tensor_tensor(hi_hot[h][:, :, 0:NT], hot, top.unsqueeze(2).to_broadcast([P, HALF, NT]), ALU.mult))
                        dve.then(v.tensor_copy(score_all[:, span(HALF * k, HALF)], score[h]))
                        wait(v, s_exp, k + 1)
                        v.tensor_tensor(hi_hot[h][:, :, 2 * NT:3 * NT], hot, expo.unsqueeze(2).to_broadcast([P, HALF, NT]),
                                        ALU.mult).then_inc(s_hot, 1)
                        wait(v, s_hot, k + 1)
                        prepare(i + 1, h)
                    PER = 2 * (MERGE + 2 + HALF + 2 + 1)

                    prepare(0, 0)
                    prepare(0, 1)
                    half(0, 0)
                    half(0, 1)
                    with v.Fori(1, PASSES) as i:
                        dve.enter(i, 1, PER)
                        half(i, 0)
                        half(i, 1)
                    dve.leave(PASSES - 1)
                    merge(2 * PASSES)
                    dve.wait()
                dve = Steps(v, s_last2)
                dve.then(v.tensor_scalar(tab_sum[:, :], tab_sum[:, :], 0.5, None, ALU.max))
                dve.then(v.reciprocal(tab_sum[:, :], tab_sum[:, :]))
                dve.done(v.tensor_copy(max_rsum[:, :, 0], tab_max[:, :]))
                dve.then(v.tensor_copy(max_rsum[:, :, 1], tab_sum[:, :]))

            @block.sync
            def _(sp):
                for a in range(ACCS):
                    sp.dma_start(acc[a].rearrange("(t p) c -> p t c", p=P),
                                 zeros[:, 0:D].unsqueeze(1).to_broadcast([P, ACC_ROWS // P, D])).then_inc(s_zero, 16)
                sp.dma_start(moe_in[0:NE * SLOTS, :].rearrange("(t p) c -> p t c", p=P),
                             zeros[:, 0:D].unsqueeze(1).to_broadcast([P, NE * CT, D])).then_inc(s_zero, 16)
                with sp.If(windowed(sp) > 0):
                    def row(j, k):
                        return edge_rows[j, span(k * HALF * P, HALF * P)].partition_broadcast(P)

                    sp.dma_start(dst_row, row(1, 0)).then_inc(s_dstr, 16)
                    sp.dma_start(src_row, row(0, 0)).then_inc(s_srcr, 16)
                    with sp.Fori(0, HALVES - 1) as k:
                        hold(sp, s_hotT, k + 1, s_held)
                        sp.dma_start(dst_row, row(1, k + 1)).then_inc(s_dstr, 16)
                        hold(sp, s_pen, HALF * k + HALF, s_held)
                        sp.dma_start(src_row, row(0, k + 1)).then_inc(s_srcr, 16)
                sp.wait_ge(s_zero, 16 * (ACCS + 1))

        m = Arena()
        idx = [m.take(HALF).bitcast(I32) for _ in range(2)]
        dst_h = [m.take(HALF) for _ in range(2)]
        score_h = [m.take(HALF) for _ in range(2)]
        out_idx = [m.take(HALF).bitcast(I32) for _ in range(2)]
        rows = m.take(PASS, ROWW)
        msg = m.take(HALF, D)
        weight = m.take(2, 1)
        alpha = m.take(2, 1)
        picked = m.take(2, P)
        skip_out = m.take(2, P)
        earlier = m.take(HALF)
        away = m.take(HALF)
        x_tile = m.take(D)
        squares = m.take(2, INNER)
        k_sb = m.take(INNER)
        v_sb = m.take(INNER)
        var = m.take(2, HEADS)
        norm_kv = m.take(HEADS)
        inv_kv = m.take(HEADS)
        scratch = m.take(HEADS)
        trash = m.take(1)
        to_window = [m.take(1).bitcast(I32) for _ in range(2)]
        rel = [m.take(HALF) for _ in range(2)]
        wide_diff = m.take(HALF)
        wide_alpha = m.take(HALF)
        wide_picked = m.take(4, P)
        window = m.take(2, D)

        s_idx, s_mr = sem("row_indices_ready"), sem("max_rsum_stored")
        s_rows = [sem(f"rows_in{i}") for i in range(PASS)]
        s_acc = [sem(f"accumulated{a}") for a in range(ACCS)]
        s_dr, s_oi, s_w3, s_pick, s_m, s_msg = sem("dst_rows_broadcast"), sem("out_indices_ready"), sem("weights_done"), sem("picks_done"), sem("messages_ready"), sem("messages_copied")
        s_xt3, s_kv, s_sq, s_kc, s_nv, s_dots = sem("mix_x_ready"), sem("kv_ready"), sem("squares_done"), sem("keys_copied"), sem("values_ready"), sem("dots_added")
        s_red = sem("squares_summed")
        s_half, s_wacc = s_rows[0:2], s_acc[0:2]
        s_to, s_diff, s_wexp, s_win = sem("to_window_ready"), sem("differences_ready"), sem("window_weights_done"), sem("window_sums_done")
        s_xz, s_xr = sem("x_padding_zero"), sem("x_loaded_again")
        s_path3 = sem("path_steps3")

        with nc.Block() as block:
            @block.sync
            def _(sp):
                sp.dma_start(node_rows.rearrange("(t p) c -> p t c", p=P)[:, :, D:ROWW], max_rsum[:, :, :]).then_inc(s_mr, 16)
                sp.wait_ge(s_xz, 1)
                sp.dma_start(x_all[:, 0:NT - 1, :], x[0:(NT - 1) * P, :].rearrange("(t p) c -> p t c", p=P)).then_inc(s_xr, 16)
                sp.dma_start(x_all[0:TAIL, NT - 1, :], x[(NT - 1) * P:N, :]).then_inc(s_xr, 16)
                sp.wait_ge(s_xr, 32)

            @block.gpsimd
            def _(g):
                g.wait_ge(s_mr, 16)
                with g.If(windowed(g) > 0):
                    def fetch_half(k, h):
                        hold(g, s_idx, k + 1, s_held)
                        for u in range(HALF):
                            g.indirect_dma_start(rows[:, HALF * h + u, :], None, node_rows,
                                                 bass.IndirectOffsetOnAxis(ap=idx[h][:, u:u + 1], axis=0)).then_inc(s_half[h], 16)

                    def add_window(i, h):
                        k = 2 * i + h
                        hold(g, s_to, k + 1, s_held)
                        hold(g, s_msg, k + 1, s_held)
                        hold(g, s_wacc[h], 16 * i, s_held)
                        g.indirect_dma_start(acc[h], bass.IndirectOffsetOnAxis(ap=to_window[h], axis=0), window[:, h, :],
                                             None, compute_op=ALU.add).then_inc(s_wacc[h], 16)

                    def step(i):
                        fetch_half(2 * i + 1, 1)
                        add_window(i, 0)
                        fetch_half(2 * i + 2, 0)
                        add_window(i, 1)

                    fetch_half(0, 0)
                    step(0)
                    with g.Fori(1, PASSES) as i:
                        step(i)
                    for h in range(2):
                        g.wait_ge(s_wacc[h], 16 * PASSES)
                    g.wait_ge(s_half[0], 16 * HALF * (PASSES + 1))
                with g.Else():
                    def gather(k, h):
                        hold(g, s_idx, k + 1, s_held)
                        return lambda u: g.indirect_dma_start(
                            rows[:, HALF * h + u, :], None, node_rows,
                            bass.IndirectOffsetOnAxis(ap=idx[h][:, u:u + 1], axis=0)).then_inc(s_rows[HALF * h + u], 16)

                    def scatter(k, h, u):
                        a = u % ACCS
                        n = (HALF // ACCS) * k + u // ACCS
                        hold(g, s_msg, HALF * k + u + 1, s_held)
                        hold(g, s_acc[a], 16 * n, s_held)
                        g.indirect_dma_start(acc[a], bass.IndirectOffsetOnAxis(ap=out_idx[h][:, u:u + 1], axis=0), msg[:, u, :],
                                             None, compute_op=ALU.add).then_inc(s_acc[a], 16)

                    def half(i, h):
                        k = 2 * i + h
                        fetch = gather(k + 1, 1 - h)
                        hold(g, s_oi, k + 1, s_held)
                        for u in range(HALF):
                            fetch(u)
                            scatter(k, h, u)

                    fetch = gather(0, 0)
                    for u in range(HALF):
                        fetch(u)
                    half(0, 0)
                    half(0, 1)
                    with g.Fori(1, PASSES) as i:
                        half(i, 0)
                        half(i, 1)
                    for a in range(ACCS):
                        g.wait_ge(s_acc[a], 16 * (ET // ACCS))
                    for u in range(HALF):
                        g.wait_ge(s_rows[u], 16 * (PASSES + 1))

            @block.scalar
            def _(act):
                def mix(i):
                    wait(act, s_kv, i)
                    act.copy(x_tile, at(xn_all, i)).then_inc(s_xt3, 1)
                    wait(act, s_kv, i + 1)
                    wait(act, s_red, i)
                    act.activation(squares[:, 0, :], psum[:, 4, :], ACT.Square).then_inc(s_sq, 1)
                    act.activation(squares[:, 1, :], psum[:, 5, :], ACT.Square).then_inc(s_sq, 1)
                    wait(act, s_dots, i)
                    act.copy(k_sb, psum[:, 4, :]).then_inc(s_kc, 1)

                with act.If(windowed(act) > 0):
                    def step(i, h):
                        k = 2 * i + h
                        wait(act, s_diff, k + 1)
                        act.activation(wide_diff, wide_diff, ACT.Exp).then_inc(s_wexp, 1)
                        wait(act, s_win, HALF * k + HALF)
                        wait(act, s_wacc[h], 16 * i)
                        act.copy(window[:, h, :], psum[:, h, 0:D]).then_inc(s_msg, 1)

                    step(0, 0)
                    mix(0)
                    step(0, 1)
                    with act.Fori(1, PASSES) as i:
                        step(i, 0)
                        mix(i)
                        step(i, 1)
                with act.Else():
                    def half(i, h):
                        k = 2 * i + h
                        for u in range(HALF):
                            T = HALF * k + u
                            wait(act, s_rows[HALF * h + u], 16 * (i + 1))
                            wait(act, s_pick, T - 1)
                            act.activation(weight[:, u % 2, :], rows[:, HALF * h + u, D:D + 1], ACT.Exp, scale=-1.0,
                                           bias=score_h[h][:, u:u + 1]).then_inc(s_w3, 1)
                            if u >= 1:
                                give(i, h, u - 1)
                        give(i, h, HALF - 1)

                    def give(i, h, u):
                        k = 2 * i + h
                        T = HALF * k + u
                        wait(act, s_m, T + 1)
                        wait(act, s_acc[u % ACCS], 16 * ((HALF // ACCS) * (k - 1) + u // ACCS + 1))
                        act.copy(msg[:, u, :], psum[:, 2 + u % 2, 0:D]).then_inc(s_msg, 1)

                    half(0, 0)
                    mix(0)
                    half(0, 1)
                    with act.Fori(1, PASSES) as i:
                        half(i, 0)
                        mix(i)
                        half(i, 1)

            @block.tensor
            def _(pe):
                pe.matmul(psum[:, 6, :], zeros[:, 0:P], zeros[:, :], start=True, stop=True)

                def keys_values(i):
                    wait(pe, s_xt3, i + 1)
                    wait(pe, s_nv, i)
                    wait(pe, s_kc, i)
                    for half_ in range(2):
                        for c in range(DC):
                            mm = pe.matmul(psum[:, 4 + half_, :], x_tile[:, c * P:(c + 1) * P],
                                           wkvT[:, c, half_ * INNER:(half_ + 1) * INNER], start=(c == 0), stop=(c == DC - 1))
                    mm.then_inc(s_kv, 1)

                def add_dots(i):
                    wait(pe, s_kc, i + 1)
                    wait(pe, s_nv, i + 1)
                    for q in range(PAIRS):
                        mm = pe.matmul(psum[:, 6, q * P:(q + 1) * P], v_sb[:, q * P:(q + 1) * P], k_sb[:, q * P:(q + 1) * P],
                                       start=False, stop=True, skip_group_check=True)
                    mm.then_inc(s_dots, 1)

                with pe.If(windowed(pe) > 0):
                    def window_sums(i, h):
                        k = 2 * i + h
                        wait(pe, s_msg, k - 1)
                        for u in range(HALF):
                            wait(pe, s_pick, HALF * k + u + 1)
                            pe.matmul(psum[:, h, 0:D], wide_picked[:, u % 4, :], rows[:, HALF * h + u, 0:D],
                                      start=(u == 0), stop=(u == HALF - 1)).then_inc(s_win, 1)

                    def step(i):
                        window_sums(i, 0)
                        keys_values(i)
                        window_sums(i, 1)
                        add_dots(i)

                    step(0)
                    with pe.Fori(1, PASSES) as i:
                        step(i)
                with pe.Else():
                    def spread(i, h):
                        k = 2 * i + h
                        wait(pe, s_idx, k + 1)
                        wait(pe, s_pick, HALF * k)
                        for u in range(HALF):
                            mm = pe.matmul(psum[:, u // 4, (u % 4) * P:(u % 4 + 1) * P], dst_h[h][:, u:u + 1].to_broadcast([P, P]), ident[:, :],
                                           start=True, stop=True)
                        mm.then_inc(s_dr, 1)

                    def sums(i, h):
                        k = 2 * i + h
                        for u in range(HALF):
                            T = HALF * k + u
                            wait(pe, s_pick, T + 1)
                            wait(pe, s_msg, T - 1)
                            pe.matmul(psum[:, 2 + u % 2, 0:D], picked[:, u % 2, :], rows[:, HALF * h + u, 0:D],
                                      start=True, stop=True).then_inc(s_m, 1)

                    def whole(i):
                        spread(i, 0)
                        sums(i, 0)
                        keys_values(i)
                        spread(i, 1)
                        sums(i, 1)
                        add_dots(i)

                    whole(0)
                    with pe.Fori(1, PASSES) as i:
                        whole(i)

            @block.vector
            def _(v):
                v.memset(x_all[96:P, NT - 1, :], 0.0).then_inc(s_xz, 1)

                def mix(i, dve):
                    wait(v, s_sq, 2 * i + 2)
                    dve.done(v.tensor_reduce(var[:, 0, :], squares[:, 0, :].rearrange("p (h d) -> p h d", d=DH), AX.X, ALU.add))
                    ins = v.tensor_reduce(var[:, 1, :], squares[:, 1, :].rearrange("p (h d) -> p h d", d=DH), AX.X, ALU.add)
                    ins.then_inc(s_red, 1)
                    wait(v, s_red, i + 1)
                    dve.wait()
                    dve.then(v.tensor_scalar(var, var, 1.0 / DH, LN_EPS, ALU.mult, ALU.add))
                    dve.then(v.tensor_tensor(norm_kv, var[:, 0, :], var[:, 1, :], ALU.mult))
                    rsqrt(v, dve, inv_kv, norm_kv, scratch)
                    wait(v, s_dots, i)
                    v.tensor_tensor(v_sb.rearrange("p (h d) -> p h d", d=DH), psum[:, 5, :].rearrange("p (h d) -> p h d", d=DH),
                                    inv_kv.unsqueeze(2).to_broadcast([P, HEADS, DH]), ALU.mult).then_inc(s_nv, 1)
                PER_MIX = 3 + RSQRT_STEPS

                with v.If(windowed(v) > 0):
                    dve = Steps(v, s_path3)

                    def prepare(i, h):
                        c = span(PASS * i + HALF * h, HALF)
                        dve.done(v.tensor_scalar(rel[h], dst_f[:, c], win_base[:, span(2 * i + h, 1)], None, ALU.subtract))
                        dve.done(v.tensor_copy(score_h[h], score_all[:, c]))
                        v.tensor_copy(idx[h], edges[:, 0, c]).then_inc(s_idx, 1)

                    def step(i, h):
                        k = 2 * i + h
                        wait(v, s_wacc[h], 16 * i)
                        v.tensor_copy(to_window[h], win_nodes[:, span(k, 1)]).then_inc(s_to, 1)
                        wait(v, s_half[h], 16 * HALF * (i + 1))
                        row = rows[:, HALF * h:HALF * h + HALF, :]
                        v.tensor_tensor(wide_diff, score_h[h], row[:, :, D], ALU.subtract).then_inc(s_diff, 1)
                        wait(v, s_wexp, k + 1)
                        dve.then(v.tensor_tensor(wide_alpha, wide_diff, row[:, :, D + 1], ALU.mult))
                        for u in range(HALF):
                            wait(v, s_win, HALF * k + u - 3)
                            v.tensor_scalar(wide_picked[:, u % 4, :], count[:, :], rel[h][:, u:u + 1], wide_alpha[:, u:u + 1],
                                            ALU.is_equal, ALU.mult).then_inc(s_pick, 1)
                        wait(v, s_win, HALF * k + HALF)
                        prepare(i + 1, h)
                    PER_STEP = 1 + 2

                    prepare(0, 0)
                    prepare(0, 1)
                    step(0, 0)
                    mix(0, dve)
                    step(0, 1)
                    with v.Fori(1, PASSES) as i:
                        dve.enter(i, 1, 2 * PER_STEP + PER_MIX)
                        step(i, 0)
                        mix(i, dve)
                        step(i, 1)
                    dve.leave(PASSES - 1)
                with v.Else():
                    dve = Steps(v, s_path3)

                    def prepare(i, h):
                        c = span(PASS * i + HALF * h, HALF)
                        dve.done(v.tensor_copy(dst_h[h], dst_f[:, c]))
                        dve.done(v.tensor_copy(score_h[h], score_all[:, c]))
                        v.tensor_copy(idx[h], edges[:, 0, c]).then_inc(s_idx, 1)

                    def half(i, h):
                        k = 2 * i + h
                        wait(v, s_dr, k + 1)
                        row = [psum[:, u // 4, (u % 4) * P:(u % 4 + 1) * P] for u in range(HALF)]
                        for u in range(HALF):
                            dve.wait(1)
                            dve.done(v.scalar_tensor_tensor(out=skip_out[:, u % 2, :], in0=row[u], scalar=dst_h[h][:, u:u + 1], in1=below[:, :],
                                                                  op0=ALU.is_equal, op1=ALU.mult, accum_out=earlier[:, u:u + 1]))
                        dve.wait()
                        dve.then(v.tensor_scalar(away, dst_h[h], trash, -1.0, ALU.subtract, ALU.mult))
                        dve.then(v.scalar_tensor_tensor(out=away, in0=earlier, scalar=1.0, in1=away, op0=ALU.min, op1=ALU.mult))
                        wait(v, s_acc[ACCS - 1], 16 * (HALF // ACCS) * (k - 1))
                        v.tensor_tensor(out_idx[h], away, dst_h[h], ALU.add).then_inc(s_oi, 1)
                        for u in range(HALF):
                            T = HALF * k + u
                            wait(v, s_w3, T + 1)
                            dve.then(v.tensor_tensor(alpha[:, u % 2, :], weight[:, u % 2, :], rows[:, HALF * h + u, D + 1:D + 2], ALU.mult))
                            wait(v, s_m, T - 1)
                            v.tensor_scalar(picked[:, u % 2, :], row[u], dst_h[h][:, u:u + 1], alpha[:, u % 2, :], ALU.is_equal,
                                            ALU.mult).then_inc(s_pick, 1)
                        wait(v, s_m, HALF * k + HALF)
                        wait(v, s_pick, HALF * k + HALF)
                        prepare(i + 1, h)
                    PER_HALF = HALF + 2 + HALF + 2

                    dve.then(v.tensor_scalar(trash, row_id[:, :], float(NP), None, ALU.add))
                    prepare(0, 0)
                    prepare(0, 1)
                    half(0, 0)
                    mix(0, dve)
                    half(0, 1)
                    with v.Fori(1, PASSES) as i:
                        dve.enter(i, 1, 2 * PER_HALF + PER_MIX)
                        half(i, 0)
                        mix(i, dve)
                        half(i, 1)
                    dve.leave(PASSES - 1)

        m = Arena()
        parts = m.take(2, ACCS, D)
        summed = m.take(2, 2, D)
        logits = m.take(NT, NE)
        x_tile = m.take(2, D)
        hT = m.take(2, D)
        h_sb = m.take(2, D)
        s_hs = sem("h_copied")
        stats = m.take(6)
        mean_var = m.take(NT, 2)
        pair = m.take(2, 2)
        variance = m.take(NT)
        rstd = m.take(NT)
        scratch = m.take(NT)
        dotsT = m.take(PAIRS, P)
        fold = m.take(PAIRS, D)
        mixed = m.take(DC, D)
        same_head = m.take(P)
        dots_all = m.take(PAIRS, P)
        s_fold, s_foldc = sem("fold_ready"), sem("fold_copied")
        s_pin = [sem(f"parts_in{i}") for i in range(2)]
        s_sum, s_x4, s_mm, s_xa, s_x1, s_h, s_ht, s_htc, s_lg, s_lgc = (sem("parts_summed"), sem("x_tile_ready"), sem("mixed_ready"), sem("mixed_read"),
            sem("x1_ready"), sem("h_ready"), sem("h_transposed"), sem("hT_ready"), sem("logits_ready"), sem("logits_copied"))
        s_gp = sem("sum_steps")

        with nc.Block() as block:
            @block.sync
            def _(sp):
                def load(t, slot):
                    wait(sp, s_sum, t - 1)
                    for a in range(ACCS):
                        sp.dma_start(parts[:, slot, a, :], acc[a][span(t * P, P), :]).then_inc(s_pin[slot], 16)
                load(0, 0)
                load(1, 1)
                with sp.Fori(1, NT // 2) as i:
                    load(2 * i, 0)
                    load(2 * i + 1, 1)
                load(NT - 1, 0)

            @block.gpsimd
            def _(g):
                st = Steps(g, s_gp)

                def add(t, slot):
                    wait(g, s_pin[slot], 32 * ACCS // 2 * ((t - slot) // 2 + 1) if isinstance(t, int) else 8 * ACCS * (t - slot) + 16 * ACCS)
                    wait(g, s_xa, t - 1)
                    st.done(g.tensor_tensor(summed[:, slot, 1, :], parts[:, slot, 2, :], parts[:, slot, 3, :], ALU.add))
                    st.then(g.tensor_tensor(summed[:, slot, 0, :], parts[:, slot, 0, :], parts[:, slot, 1, :], ALU.add))
                    g.tensor_tensor(summed[:, slot, 0, :], summed[:, slot, 0, :], summed[:, slot, 1, :], ALU.add).then_inc(s_sum, 1)
                add(0, 0)
                add(1, 1)
                with g.Fori(1, NT // 2) as i:
                    st.enter(i, 1, 4)
                    add(2 * i, 0)
                    add(2 * i + 1, 1)
                st.leave(NT // 2 - 1)
                add(NT - 1, 0)

            @block.tensor
            def _(pe):
                pe.wait_ge(s_foldc, 1)
                for q in range(PAIRS):
                    mm = pe.matmul(psum[:, q // 2, (q % 2) * D:(q % 2 + 1) * D], dotsT[:, q, :], woutT[:, q, :], start=True, stop=True)
                mm.then_inc(s_fold, 1)
                pe.wait_ge(s_foldc, 2)
                for c in range(DC):
                    for q in range(PAIRS):
                        mm = pe.matmul(psum[:, 2 + c, 0:D], wq[:, q, c * P:(c + 1) * P], fold[:, q, :], start=(q == 0), stop=(q == PAIRS - 1))
                mm.then_inc(s_fold, 1)
                pe.wait_ge(s_foldc, 3)

                def mix(t, slot):
                    wait(pe, s_x4, t + 1)
                    wait(pe, s_xa, t - 1)
                    for j in range(2):
                        pe.matmul(psum[:, slot, 0:D], ones[0:1, :], bias_row[:, j, :], start=(j == 0), stop=False)
                    for c in range(DC):
                        mm = pe.matmul(psum[:, slot, 0:D], x_tile[:, slot, c * P:(c + 1) * P], mixed[:, c, :], start=False, stop=(c == DC - 1))
                    mm.then_inc(s_mm, 1)

                def gate(t, slot):
                    wait(pe, s_h, t + 1)
                    wait(pe, s_htc, t - 1)
                    for c in range(DC):
                        mm = pe.transpose(psum[:, 4 + slot, c * P:(c + 1) * P], h_sb[:, slot, c * P:(c + 1) * P], ident[:, :])
                    mm.then_inc(s_ht, 1)
                    wait(pe, s_htc, t + 1)
                    wait(pe, s_lgc, t - 1)
                    for c in range(DC):
                        mm = pe.matmul(psum[:, 6 + slot, 0:NE], hT[:, slot, c * P:(c + 1) * P], gw[:, c, :], start=(c == 0), stop=(c == DC - 1))
                    mm.then_inc(s_lg, 1)

                for step in (mix, gate):
                    step(0, 0)
                    step(1, 1)
                    with pe.Fori(1, NT // 2) as i:
                        step(2 * i, 0)
                        step(2 * i + 1, 1)
                    step(NT - 1, 0)

            @block.scalar
            def _(act):
                def take(t, slot):
                    wait(act, s_mm, t - 1)
                    act.copy(x_tile[:, slot, :], at(xn_all, t)).then_inc(s_x4, 1)

                def turn(t, slot):
                    wait(act, s_h, t + 1)
                    act.copy(at(xn_all, t), h_sb[:, slot, :]).then_inc(s_hs, 1)
                    wait(act, s_ht, t + 1)
                    wait(act, s_lg, t - 1)
                    act.copy(hT[:, slot, :], psum[:, 4 + slot, 0:D]).then_inc(s_htc, 1)
                    wait(act, s_lg, t + 1)
                    act.copy(at(logits, t), psum[:, 6 + slot, 0:NE]).then_inc(s_lgc, 1)
                for step in (take, turn):
                    step(0, 0)
                    step(1, 1)
                    with act.Fori(1, NT // 2) as i:
                        step(2 * i, 0)
                        step(2 * i + 1, 1)
                    step(NT - 1, 0)

            @block.vector
            def _(v):
                dve.done(v.memset(same_head, 0.0))
                dve.wait()
                for h in range(P // DH):
                    dve.done(v.memset(same_head[h * DH:(h + 1) * DH, h * DH:(h + 1) * DH], 1.0 / N))
                dve.wait()
                v.tensor_tensor(dotsT, psum[:, 6, :].rearrange("p (q j) -> p q j", j=P), same_head.unsqueeze(1).to_broadcast([P, PAIRS, P]),
                                ALU.mult).then_inc(s_foldc, 1)
                v.wait_ge(s_fold, 1)
                dve.done(v.tensor_copy(fold[:, 0:2, :], psum[:, 0, :].rearrange("p (q j) -> p q j", j=D)))
                dve.wait()
                v.tensor_copy(fold[:, 2:4, :], psum[:, 1, :].rearrange("p (q j) -> p q j", j=D)).then_inc(s_foldc, 1)
                v.wait_ge(s_fold, 2)
                v.tensor_copy(mixed, psum[:, 2:4, 0:D]).then_inc(s_foldc, 1)

                def residual(t, slot):
                    xt = at(x_all, t)
                    wait(v, s_mm, t + 1)
                    dve.then(v.tensor_tensor(xt, xt, psum[:, slot, 0:D], ALU.add))
                    wait(v, s_sum, t + 1)
                    v.tensor_tensor(xt, xt, summed[:, slot, 0, :], ALU.add).then_inc(s_xa, 1)
                    hold(v, s_xa, t + 1, s_held)
                    dve.done(v.bn_stats(stats, xt))
                    dve.hold(s_held)
                    dve.then(v.bn_aggr(pair[:, slot, :], stats))
                    dve.done(v.tensor_copy(at(mean_var, t), pair[:, slot, :]))

                def normalise(t, slot):
                    wait(v, s_ht, t - 1)
                    wait(v, s_hs, t - 1)
                    v.tensor_scalar(h_sb[:, slot, :], at(x_all, t), at(mean_var, t)[:, 0:1], rstd[:, span(t, 1)],
                                    ALU.subtract, ALU.mult).then_inc(s_h, 1)

                residual(0, 0)
                residual(1, 1)
                with v.Fori(1, NT // 2) as i:
                    dve.enter(i, 1, 8)
                    residual(2 * i, 0)
                    residual(2 * i + 1, 1)
                dve.leave(NT // 2 - 1)
                residual(NT - 1, 0)
                dve.wait()
                dve.then(v.tensor_scalar(variance, mean_var[:, :, 1], LN_EPS, None, ALU.add))
                rsqrt(v, dve, rstd, variance, scratch)
                normalise(0, 0)
                normalise(1, 1)
                with v.Fori(1, NT // 2) as i:
                    normalise(2 * i, 0)
                    normalise(2 * i + 1, 1)
                normalise(NT - 1, 0)

        m = Arena()
        m.take(2, ACCS, D)
        m.take(2, 2, D)
        m.take(NT, NE)
        expos = m.take(NT, NE)
        probs = m.take(NT, NE)
        chosen = m.take(NT, NE)
        tmp = m.take(NT, NE)
        place_e = m.take(NT, NE)
        totals = m.take(NE, NT)
        upto = m.take(NE, NT)
        red = m.take(NT)
        prob = m.take(NT)
        expert = m.take(NT)
        pos = m.take(NT)
        kept = m.take(NT)
        trash = m.take(NT)
        s_r, s_rm, s_re, s_sent = sem("routed"), sem("ranks_ready"), sem("route_exp"), sem("rows_sent")

        with nc.Block() as block:
            @block.vector
            def _(v):
                def wide(a):
                    return a.unsqueeze(2).to_broadcast([P, NT, NE])
                ids = count[:, 0:NE].unsqueeze(1).to_broadcast([P, NT, NE])
                dve.then(v.tensor_scalar(trash, count[:, 0:NT], float(P), row_id[:, :], ALU.mult, ALU.add))
                dve.then(v.tensor_scalar(trash, trash, float(NE * SLOTS), None, ALU.add))
                dve.then(v.tensor_tensor(logits, logits, gb[:, :].unsqueeze(1).to_broadcast([P, NT, NE]), ALU.add))
                dve.then(v.tensor_reduce(red, logits, AX.X, ALU.max))
                v.tensor_tensor(expos, logits, wide(red), ALU.subtract).then_inc(s_r, 1)
                v.wait_ge(s_re, 1)
                dve.then(v.tensor_reduce(red, expos, AX.X, ALU.add))
                dve.then(v.reciprocal(red, red))
                dve.then(v.tensor_tensor(probs, expos, wide(red), ALU.mult))
                dve.then(v.tensor_reduce(prob, probs, AX.X, ALU.max))
                dve.then(v.tensor_tensor(tmp, probs, wide(prob), ALU.not_equal))
                dve.then(v.scalar_tensor_tensor(out=tmp, in0=tmp, scalar=float(NE), in1=ids, op0=ALU.mult, op1=ALU.add))
                dve.then(v.tensor_reduce(expert, tmp, AX.X, ALU.min))
                v.tensor_tensor(chosen, wide(expert), ids, ALU.is_equal).then_inc(s_r, 1)
                v.wait_ge(s_rm, 1)
                dve.then(v.tensor_copy(totals, psum[:, 1, 0:NT * NE].rearrange("p (t e) -> p e t", e=NE)))
                for e in range(NE):
                    dve.done(v.tensor_tensor_scan(upto[:, e, :], totals[:, e, :], zeros[:, 0:NT], 0.0, ALU.add, ALU.add))
                dve.wait()
                dve.then(v.tensor_tensor(upto, upto, totals, ALU.subtract))
                dve.then(v.tensor_tensor(place_e, upto.rearrange("p e t -> p t e"), psum[:, 0, 0:NT * NE].rearrange("p (t e) -> p t e", e=NE), ALU.add))
                dve.then(v.tensor_tensor(place_e, place_e, chosen, ALU.mult))
                dve.then(v.tensor_reduce(pos, place_e, AX.X, ALU.add))
                dve.then(v.tensor_scalar(kept, pos, float(CAP), None, ALU.is_lt))
                dve.then(v.tensor_tensor(gate_prob[:, :], prob, kept, ALU.mult))
                dve.then(v.tensor_scalar(expert, expert, float(SLOTS), None, ALU.mult))
                dve.then(v.scalar_tensor_tensor(out=red, in0=pos, scalar=float(CAP - 1), in1=expert, op0=ALU.min, op1=ALU.add))
                dve.done(v.tensor_copy(slot_in[:, :], red))
                dve.then(v.tensor_tensor(red, red, trash, ALU.subtract))
                dve.then(v.tensor_tensor(red, red, kept, ALU.mult))
                v.tensor_tensor(slot_out[:, :], red, trash, ALU.add).then_inc(s_r, 1)
                v.wait_ge(s_r, 3)

            @block.scalar
            def _(act):
                act.wait_ge(s_r, 1)
                act.activation(expos, expos, ACT.Exp).then_inc(s_re, 1)

            @block.tensor
            def _(pe):
                pe.wait_ge(s_r, 2)
                pe.matmul(psum[:, 0, 0:NT * NE], above[:, :], chosen.rearrange("p t e -> p (t e)"), start=True, stop=True)
                pe.matmul(psum[:, 1, 0:NT * NE], ones[:, :], chosen.rearrange("p t e -> p (t e)"), start=True, stop=True).then_inc(s_rm, 1)

            @block.gpsimd
            def _(g):
                g.wait_ge(s_r, 3)
                for t in range(NT):
                    g.indirect_dma_start(moe_in, bass.IndirectOffsetOnAxis(ap=slot_out[:, t:t + 1], axis=0), xn_all[:, t, :], None).then_inc(s_sent, 16)
                g.wait_ge(s_sent, 16 * NT)

        m = Arena()
        w1_sb = m.take(2, DC, F)
        w2_sb = m.take(2, FT * D)
        rows_in = m.take(2, CT * D)
        y_sb = m.take(2, D)
        big = xn_all[:, :, :].rearrange("p t c -> p (t c)")
        hid = big[:, 0:FT * SLOTS].rearrange("p (f s) -> p f s", s=SLOTS)
        inT = big[:, FT * SLOTS:FT * SLOTS + DC * SLOTS].rearrange("p (c s) -> p c s", s=SLOTS)
        b2_all = big[:, (FT + DC) * SLOTS:(FT + DC) * SLOTS + NE * D].rearrange("p (e c) -> p e c", c=D)
        s_win = [sem(f"expert_loaded{i}") for i in range(2)]
        s_b2, s_it, s_itc, s_hid, s_hc, s_y, s_yc = sem("b2_loaded"), sem("inputs_transposed"), sem("inputs_copied"), sem("hidden_ready"), sem("hidden_done"), sem("y_ready"), sem("y_done")
        s_ys = [sem(f"y_stored{i}") for i in range(2)]
        HG = 2 * FT
        IG = DC * CT // 4

        with nc.Block() as block:
            @block.sync
            def _(sp):
                sp.dma_start(b2_all, b2.partition_broadcast(P)).then_inc(s_b2, 16)

                def load(e, s):
                    wait(sp, s_y, CT * (e - 1))
                    ei = span(e, 1)
                    sp.dma_start(w1_sb[:, s, :, :], w1[ei, :, :].rearrange("a (c p) f -> p (a c) f", p=P)).then_inc(s_win[s], 16)
                    sp.dma_start(w2_sb[:, s, :].rearrange("p (f d) -> p f d", d=D), w2[ei, :, :].rearrange("a (f p) d -> p (a f) d", p=P)).then_inc(s_win[s], 16)
                    sp.dma_start(rows_in[:, s, :].rearrange("p (t c) -> p t c", c=D),
                                 moe_in[span(e * SLOTS, SLOTS), :].rearrange("(t p) c -> p t c", p=P)).then_inc(s_win[s], 16)

                def store(e, s):
                    for j in range(CT):
                        wait(sp, s_yc, CT * e + j + 1)
                        sp.dma_start(moe_out[span(e * SLOTS + j * P, P), :], y_sb[:, j % 2, :]).then_inc(s_ys[j % 2], 16)
                load(0, 0)
                load(1, 1)
                store(0, 0)
                with sp.Fori(1, NE // 2) as i:
                    load(2 * i, 0)
                    store(2 * i - 1, 1)
                    load(2 * i + 1, 1)
                    store(2 * i, 0)
                store(NE - 1, 1)
                for q in range(2):
                    sp.wait_ge(s_ys[q], 16 * NE * CT // 2)

            @block.tensor
            def _(pe):
                def expert_(e, s):
                    wait(pe, s_win[s], 48 * ((e - s) // 2 + 1) if isinstance(e, int) else 24 * (e - s) + 48)
                    for q in range(IG):
                        wait(pe, s_itc, IG * e + q - 1)
                        for k in range(4):
                            c, j = (4 * q + k) // CT, (4 * q + k) % CT
                            mm = pe.transpose(psum[:, q % 2, k * P:(k + 1) * P], rows_in[:, s, j * D + c * P:j * D + (c + 1) * P], ident[:, :])
                        mm.then_inc(s_it, 1)
                    wait(pe, s_itc, IG * e + IG)
                    for f in range(FT):
                        for n in range(2):
                            G = HG * e + 2 * f + n
                            bank = 2 + (2 * f + n) % 4
                            wait(pe, s_hc, G - 3)
                            for c in range(DC):
                                mm = pe.matmul(psum[:, bank, :], w1_sb[:, s, c, f * P:(f + 1) * P], inT[:, c, n * 512:(n + 1) * 512],
                                               start=(c == 0), stop=(c == DC - 1))
                            mm.then_inc(s_hid, 1)
                    wait(pe, s_hc, HG * e + HG)
                    for j in range(CT):
                        wait(pe, s_yc, CT * e + j - 1)
                        for f in range(FT):
                            mm = pe.matmul(psum[:, 6 + j % 2, 0:D], hid[:, f, j * P:(j + 1) * P], w2_sb[:, s, f * D:(f + 1) * D],
                                           start=(f == 0), stop=(f == FT - 1))
                        mm.then_inc(s_y, 1)
                expert_(0, 0)
                expert_(1, 1)
                with pe.Fori(1, NE // 2) as i:
                    expert_(2 * i, 0)
                    expert_(2 * i + 1, 1)

            @block.scalar
            def _(act):
                def expert_(e):
                    for q in range(IG):
                        wait(act, s_it, IG * e + q + 1)
                        wait(act, s_hid, HG * e)
                        c, j = 4 * q // CT, 4 * q % CT
                        act.copy(inT[:, c, j * P:(j + 4) * P], psum[:, q % 2, :]).then_inc(s_itc, 1)
                    for f in range(FT):
                        for n in range(2):
                            G = HG * e + 2 * f + n
                            bank = 2 + (2 * f + n) % 4
                            hold(act, s_hid, G + 1, s_held)
                            hold(act, s_y, CT * e, s_held)
                            act.activation(hid[:, f, n * 512:(n + 1) * 512], psum[:, bank, :], ACT.Relu,
                                           bias=b1T[:, span(e * FT + f, 1)]).then_inc(s_hc, 1)
                expert_(0)
                with act.Fori(1, NE) as i:
                    expert_(i)

            @block.vector
            def _(v):
                def expert_(e):
                    for j in range(CT):
                        wait(v, s_y, CT * e + j + 1)
                        wait(v, s_ys[j % 2], 16 * (CT // 2 * e + j // 2))
                        v.tensor_tensor(y_sb[:, j % 2, :], psum[:, 6 + j % 2, 0:D], at(b2_all, e), ALU.add).then_inc(s_yc, 1)
                v.wait_ge(s_b2, 16)
                expert_(0)
                with v.Fori(1, NE) as i:
                    expert_(i)

        RING = 7
        m = Arena()
        got = m.take(RING, D)
        y = m.take(RING, D)
        high = m.take(D)
        bad = m.take(D)
        fine = m.take(D)
        s_got = [sem(f"result_in{i}") for i in range(RING)]
        s_rd, s_o = sem("result_read"), sem("out_ready")
        s_os = [sem(f"out_stored{i}") for i in range(RING)]

        with nc.Block() as block:
            @block.gpsimd
            def _(g):
                for t in range(NT):
                    wait(g, s_rd, t - RING + 1)
                    g.indirect_dma_start(got[:, t % RING, :], None, moe_out,
                                         bass.IndirectOffsetOnAxis(ap=slot_in[:, t:t + 1], axis=0)).then_inc(s_got[t % RING], 16)

            @block.vector
            def _(v):
                def tile(i, u):
                    t = RING * i + u
                    wait(v, s_got[u], 16 * (i + 1))
                    wait(v, s_os[u], 16 * i)
                    yu = y[:, u, :]
                    v.tensor_scalar(yu, got[:, u, :], gate_prob[:, span(t, 1)], None, ALU.mult).then_inc(s_rd, 1)
                    wait(v, s_rd, t + 1)
                    dve.done(v.tensor_scalar(high, yu, FLOAT_MAX, None, ALU.is_gt))
                    dve.then(v.tensor_scalar(fine, yu, 0.0, 0.0, ALU.mult, ALU.is_equal))
                    dve.then(v.scalar_tensor_tensor(out=bad, in0=yu, scalar=-FLOAT_MAX, in1=high, op0=ALU.is_lt, op1=ALU.subtract))
                    dve.done(v.tensor_scalar(bad, bad, -1.0e4, None, ALU.mult))
                    dve.hold(s_held)
                    dve.then(v.copy_predicated(bad, fine.bitcast(I32), yu))
                    v.tensor_tensor(yu, bad, at(x_all, t), ALU.add).then_inc(s_o, 1)
                    wait(v, s_o, t + 1)
                for u in range(RING):
                    tile(0, u)
                with v.Fori(1, NT // RING) as i:
                    dve.enter(i, 1, 5 * RING)
                    for u in range(RING):
                        tile(i, u)
                dve.leave(NT // RING - 1)

            @block.sync
            def _(sp):
                def store(t, u):
                    wait(sp, s_o, t + 1)
                    sp.dma_start(out[span(t * P, P), :], y[:, u, :]).then_inc(s_os[u], 16)
                with sp.Fori(0, NT // RING - 1) as i:
                    for u in range(RING):
                        store(RING * i + u, u)
                for t in range(NT - RING, NT - 1):
                    store(t, t % RING)
                sp.wait_ge(s_o, NT)
                sp.dma_start(out[(NT - 1) * P:N, :], y[0:TAIL, RING - 1, :]).then_inc(s_os[RING - 1], 16)
                for u in range(RING):
                    sp.wait_ge(s_os[u], 16 * (NT // RING))


_INS = ['x', 'src', 'dst', 'L0_gnn_W_s', 'L0_gnn_W_t', 'L0_gnn_W_attn', 'L0_gnn_W_fc', 'L0_gnn_b_fc', 'L0_mix_w_qkv',
        'L0_mix_w_out', 'L0_mix_b_out', 'L0_ffn_gate_w', 'L0_ffn_gate_b', 'L0_ffn_w1', 'L0_ffn_b1', 'L0_ffn_w2',
        'L0_ffn_b2']


def kernel(**inputs):
    import numpy as _np
    import concourse.bacc as _bacc
    from concourse import mybir as _mybir
    from concourse.bass_utils import run_bass_kernel_spmd as _run

    nc = _bacc.Bacc("TRN2", target_bir_lowering=False, num_devices=1)
    arrays, args = {}, []
    for name in _INS:
        a = _np.ascontiguousarray(inputs[name])
        arrays[f"in_{name}_dram"] = a
        args.append(nc.dram_tensor(f"in_{name}_dram", a.shape, _mybir.dt.from_np(a.dtype), kind="ExternalInput").ap())
    args.append(nc.dram_tensor("out_0_dram", tuple(inputs['x'].shape), _mybir.dt.float32, kind="ExternalOutput").ap())
    graph_transformer_kernel(nc, *args)
    r = _run(nc, [arrays], core_ids=[0])
    return r.results[0]["out_0_dram"]
```

```python
import concourse.bass as bass
from concourse import mybir
from contextlib import ExitStack

F32 = mybir.dt.float32
I32 = mybir.dt.int32
ALU = mybir.AluOpType
ACT = mybir.ActivationFunctionType
AX = mybir.AxisListType

P = 128
FLOAT_MAX = 3.4028234663852886e38
BIG = 1.0e30
LN_EPS = 1e-5
SLOPE = 0.2


class Steps:

    def __init__(self, eng, sem):
        self.eng, self.sem, self.base, self.n = eng, sem, 0, 0

    def enter(self, i, first, per_pass):
        self.start, self.per_pass = self.base + self.n, per_pass
        self.base, self.n = self.start + (i - first) * per_pass, 0

    def leave(self, passes):
        assert self.n == self.per_pass, (self.n, self.per_pass)
        self.base, self.n = self.start + passes * self.per_pass, 0

    def done(self, ins):
        self.n += 1
        return ins.then_inc(self.sem, 1)

    def wait(self, but=0):
        self.eng.wait_ge(self.sem, self.base + self.n - but)

    def hold(self, past):
        hold(self.eng, self.sem, self.base + self.n, past)

    def then(self, ins):
        self.done(ins)
        self.wait()


def rsqrt_step(v, steps, n, out, value, scratch):
    if n == 0:
        steps.done(v.tensor_scalar(out.bitcast(I32), value.bitcast(I32), -0.5, float(0x5f3759df), ALU.mult, ALU.add))
    elif n % 3 == 1:
        steps.done(v.tensor_tensor(scratch, out, out, ALU.mult))
    elif n % 3 == 2:
        steps.done(v.scalar_tensor_tensor(out=scratch, in0=scratch, scalar=-0.5, in1=value, op0=ALU.mult, op1=ALU.mult))
    else:
        steps.done(v.scalar_tensor_tensor(out=out, in0=scratch, scalar=1.5, in1=out, op0=ALU.add, op1=ALU.mult))


def rsqrt(v, steps, out, value, scratch):
    for n in range(RSQRT_STEPS):
        rsqrt_step(v, steps, n, out, value, scratch)
        steps.wait()


RSQRT_STEPS = 10


def wait(eng, sem, value):
    if not isinstance(value, int) or value > 0:
        eng.wait_ge(sem, value)


def hold(eng, sem, value, held):
    if not isinstance(value, int) or value > 0:
        eng.wait_ge(sem, value)
        eng.sem_inc(held, 1)


def at(v, t):
    if isinstance(t, int):
        return v[:, t, :]
    return v[:, bass.ds(t, 1), :].rearrange("p a c -> p (a c)")


def span(t, n):
    return slice(t, t + n) if isinstance(t, int) else bass.ds(t, n)


def graph_transformer_kernel(nc, x, src, dst, W_s, W_t, W_attn, W_fc, b_fc, w_qkv, w_out, b_out,
                             gate_w, gate_b, w1, b1, w2, b2, out):
    N, D = x.shape
    E = src.shape[0]
    NT = (N + P - 1) // P
    NP = NT * P
    TAIL = N - (NT - 1) * P
    PAD_NODE = NP - 1
    HALF = 8
    PASS = 2 * HALF
    PASSES = (E + P * PASS - 1) // (P * PASS)
    ET = PASSES * PASS
    HALVES = 2 * PASSES
    EC = ET + PASS
    FULL_B = E // (P * P)
    FULL_T = E // P - FULL_B * P
    REST = E % P
    ZW = D + 2
    HEADS, DH = 8, 64
    INNER = HEADS * DH
    PAIRS = INNER // P
    NE, _, F = w1.shape
    FT = F // P
    CAP = max(1, -(-5 * N // (4 * NE)))
    CT = (CAP + P - 1) // P
    SLOTS = CT * P
    DC = D // P
    TABW = 3 * NT
    ROWW = D + 2
    ACCS = 4
    ACC_ROWS = NP + P
    assert DC == 2 and NT == PASSES

    proj_s = nc.dram_tensor("proj_s", (NP, ZW), F32, kind="Internal").ap()
    proj_t = nc.dram_tensor("proj_t", (NP, ZW), F32, kind="Internal").ap()
    node_rows = nc.dram_tensor("node_rows", (NP, ROWW), F32, kind="Internal").ap()
    edge_rows = nc.dram_tensor("edge_rows", (2, ET * P), F32, kind="Internal").ap()
    acc = [nc.dram_tensor(f"acc{a}", (ACC_ROWS, D), F32, kind="Internal").ap() for a in range(ACCS)]
    moe_in = nc.dram_tensor("moe_in", (NE * SLOTS + NP, D), F32, kind="Internal").ap()
    moe_out = nc.dram_tensor("moe_out", (NE * SLOTS, D), F32, kind="Internal").ap()

    with ExitStack() as ctx:
        def sb(name, shape, dt=F32):
            return ctx.enter_context(nc.sbuf_tensor(name, shape, dt))

        def sem(name):
            return ctx.enter_context(nc.semaphore(name))

        s_held = sem("held")
        psum = ctx.enter_context(nc.psum_tensor("psum", [P, 8, 512], F32))

        x_all = sb("x_all", [P, NT, D])
        xn_all = sb("xn_all", [P, NT, D])
        edges = sb("edges", [P, 2, EC], I32)
        attr = sb("attr", [P, 3, EC])
        dst_f = sb("dst_f", [P, EC])
        score_all = sb("score_all", [P, EC])
        ident = sb("ident", [P, P])
        below = sb("below", [P, P])
        above = sb("above", [P, P])
        ones = sb("ones", [P, P])
        count_i = sb("count_i", [P, P], I32)
        count = sb("count", [P, P])
        trash_i = sb("trash_i", [P, 1], I32)
        row_id = sb("row_id", [P, 1])
        attn = sb("attn", [P, ZW])
        attn_col = sb("attn_col", [P, DC])
        win_base = sb("win_base", [P, HALVES + 2])
        win_nodes = sb("win_nodes", [P, HALVES], I32)
        big = sb("big", [P, 1])
        win_rows = sb("win_rows", [P, HALVES + 2], I32)
        fits = sb("fits", [P, 1], I32)
        bias_row = sb("bias_row", [1, 2, D])
        w3T = sb("w3T", [P, DC, 3 * D])
        wkvT = sb("wkvT", [P, DC, 2 * INNER])
        woutT = sb("woutT", [P, PAIRS, D])
        wq = sb("wq", [P, PAIRS, D])
        gw = sb("gw", [P, DC, NE])
        gb = sb("gb", [P, NE])
        b1T = sb("b1T", [P, NE * FT])
        tab_max = sb("tab_max", [P, NT])
        tab_sum = sb("tab_sum", [P, NT])
        max_rsum = sb("max_rsum", [P, NT, 2])
        zeros = sb("zeros", [P, 512])
        gate_prob = sb("gate_prob", [P, NT])
        slot_in = sb("slot_in", [P, NT], I32)
        slot_out = sb("slot_out", [P, NT], I32)
        pool_mem = sb("pool_mem", [P, 13800])

        def windowed(eng):
            return eng.value_load(fits[0:1, 0:1], min_val=0, max_val=1)

        class Arena:
            def __init__(self, memory=pool_mem, size=13800):
                self.at, self.memory, self.size = 0, memory, size

            def take(self, *shape):
                n = 1
                for s in shape:
                    n *= s
                v = self.memory[:, self.at:self.at + n]
                self.at += n
                assert self.at <= self.size, self.at
                if len(shape) == 2:
                    v = v.rearrange("p (a b) -> p a b", b=shape[1])
                if len(shape) == 3:
                    v = v.rearrange("p (a b c) -> p a b c", b=shape[1], c=shape[2])
                return v

        m = Arena()
        w3_raw = m.take(3 * DC, D)
        kv_raw = m.take(2 * INNER // P, D)
        wout_raw = m.take(DC, INNER)
        b1_raw = m.take(P)
        stats = m.take(4, 6)
        mean_var = m.take(NT, 2)
        pair = m.take(4, 2)
        variance = m.take(NT)
        rstd = m.take(NT)
        scratch = m.take(NT)
        xn = m.take(2, D)
        xnT = m.take(2, D)
        proj = m.take(2, 3, ZW)
        lin_out = m.take(4, D)
        headmean = m.take(DC, 2 * HEADS)
        hi_i = m.take(EC).bitcast(I32)
        raw_e = m.take(2, FULL_B + 1, P).bitcast(I32)
        raw_f = m.take(2, FULL_B + 1, P)
        dst_range = m.take(2, HALVES)
        extremes = m.take(2)
        misfit = m.take(1)
        diagonal = m.take(HALVES)
        window_f = m.take(HALVES)

        s_fill, s_x, s_edges, s_w = sem("fills_done"), sem("x_loaded"), sem("edges_loaded"), sem("weights_loaded")
        s_const, s_pool, s_dve = sem("constants_made"), sem("pool_steps"), sem("dve_steps")
        s_wt, s_wc = sem("weights_transposed"), sem("weights_copied")
        s_xn, s_tp, s_xt = sem("xn_ready"), sem("xn_transposed"), sem("xnT_ready")
        s_pj, s_pc, s_lin = sem("proj_ready"), sem("proj_copied"), sem("linear_terms_done")
        s_st = [sem(f"proj_stored{i}") for i in range(2)]
        s_rf, s_et, s_ec = sem("raw_edges_float"), sem("edges_transposed"), sem("edges_copied")
        s_range, s_rangeT, s_ends, s_base = sem("ranges_ready"), sem("ranges_transposed"), sem("extremes_ready"), sem("bases_broadcast")
        LOADS = 12

        jobs = []
        for c in range(DC):
            for w in range(3 * DC):
                jobs.append((w3_raw[:, w, c * P:(c + 1) * P], w3T[:, c, w * P:(w + 1) * P]))
        FIRST = len(jobs)
        for c in range(DC):
            for w in range(2 * INNER // P):
                jobs.append((kv_raw[:, w, c * P:(c + 1) * P], wkvT[:, c, w * P:(w + 1) * P]))
        for g in range(PAIRS):
            for c in range(DC):
                jobs.append((wout_raw[:, c, g * P:(g + 1) * P], woutT[:, g, c * P:(c + 1) * P]))
        GROUPS = len(jobs) // 4
        dve = Steps(nc.vector, s_dve)

        with nc.Block() as block:
            @block.sync
            def _(sp):
                sp.wait_ge(s_fill, 2)
                for j, e in enumerate((src, dst)):
                    sp.dma_start(raw_e[:, j, 0:FULL_B, :], e[0:FULL_B * P * P].rearrange("(b p c) -> p b c", p=P, c=P)).then_inc(s_edges, 16)
                    sp.dma_start(raw_e[0:FULL_T, j, FULL_B, :], e[FULL_B * P * P:FULL_B * P * P + FULL_T * P].rearrange("(p c) -> p c", c=P)).then_inc(s_edges, 16)
                    sp.dma_start(raw_e[FULL_T:FULL_T + 1, j, FULL_B, 0:REST], e[E - REST:E].rearrange("(p c) -> p c", p=1)).then_inc(s_edges, 16)
                sp.dma_start(x_all[:, 0:NT - 1, :], x[0:(NT - 1) * P, :].rearrange("(t p) c -> p t c", p=P)).then_inc(s_x, 16)
                sp.dma_start(x_all[0:TAIL, NT - 1, :], x[(NT - 1) * P:N, :]).then_inc(s_x, 16)
                for i, w in enumerate((W_s, W_t, W_fc)):
                    sp.dma_start(w3_raw[:, 2 * i:2 * i + 2, :], w.rearrange("(o p) c -> p o c", p=P)).then_inc(s_w, 16)
                sp.dma_start(kv_raw, w_qkv[INNER:3 * INNER, :].rearrange("(o p) c -> p o c", p=P)).then_inc(s_w, 16)
                sp.dma_start(wout_raw, w_out.rearrange("(o p) c -> p o c", p=P)).then_inc(s_w, 16)
                sp.dma_start(b1_raw[0:NE * FT, :], b1.rearrange("e (f p) -> (e f) p", p=P)).then_inc(s_w, 16)
                sp.dma_start(wq[:, :, :], w_qkv[0:INNER, :].rearrange("(o p) c -> p o c", p=P)).then_inc(s_w, 16)
                sp.dma_start(attn[:, 0:D], W_attn[0, :].partition_broadcast(P)).then_inc(s_w, 16)
                sp.dma_start(gw[:, :, :], gate_w.rearrange("(c p) e -> p c e", p=P)).then_inc(s_w, 16)
                sp.dma_start(gb[:, :], gate_b.partition_broadcast(P)).then_inc(s_w, 16)
                sp.dma_start(bias_row[:, 0, :], b_fc.rearrange("(a c) -> a c", a=1)).then_inc(s_w, 16)
                sp.dma_start(bias_row[:, 1, :], b_out.rearrange("(a c) -> a c", a=1)).then_inc(s_w, 16)

                def store(t, slot):
                    wait(sp, s_pc, 2 * t + 2)
                    wait(sp, s_lin, 4 * t + 4)
                    rows = span(t * P, P)
                    sp.dma_start(proj_s[rows, :], proj[:, slot, 0, :]).then_inc(s_st[slot], 16)
                    sp.dma_start(proj_t[rows, :], proj[:, slot, 1, :]).then_inc(s_st[slot], 16)
                    sp.dma_start(node_rows[rows, 0:D], proj[:, slot, 2, 0:D]).then_inc(s_st[slot], 16)

                with sp.Fori(0, NT // 2) as i:
                    store(2 * i, 0)
                    store(2 * i + 1, 1)
                store(NT - 1, 0)
                sp.wait_ge(s_rf, 1)
                for j in range(2):
                    sp.dma_start(edge_rows[j, 0:FULL_B * P * P].rearrange("(b p c) -> p b c", p=P, c=P), raw_f[:, j, 0:FULL_B, :]).then_inc(s_edges, 16)
                    sp.dma_start(edge_rows[j, FULL_B * P * P:ET * P].rearrange("(p c) -> p c", c=P), raw_f[0:ET - FULL_B * P, j, FULL_B, :]).then_inc(s_edges, 16)
                sp.wait_ge(s_edges, 16 * 10)
                sp.wait_ge(s_st[0], 48 * (NT // 2 + 1))
                sp.wait_ge(s_st[1], 48 * (NT // 2))

            @block.gpsimd
            def _(g):
                st = Steps(g, s_pool)
                st.done(g.memset(ident[:, :], 0.0))
                st.done(g.memset(below[:, :], 0.0))
                st.done(g.memset(above[:, :], 0.0))
                st.done(g.iota(count_i[:, :], [[1, P]], base=0, channel_multiplier=0))
                st.then(g.iota(trash_i[:, :], [[0, 1]], base=0, channel_multiplier=1))
                g.affine_select(out=ident[:, :], in_=ident[:, :], compare_op=ALU.not_equal, fill=1.0, base=0,
                                pattern=[[-1, P]], channel_multiplier=1).then_inc(s_const, 1)
                g.affine_select(out=below[:, :], in_=below[:, :], compare_op=ALU.is_ge, fill=1.0, base=0,
                                pattern=[[1, P]], channel_multiplier=-1).then_inc(s_const, 1)
                g.affine_select(out=above[:, :], in_=above[:, :], compare_op=ALU.is_ge, fill=1.0, base=0,
                                pattern=[[-1, P]], channel_multiplier=1).then_inc(s_const, 1)

            @block.vector
            def _(v):
                v.memset(x_all[96:P, NT - 1, :], 0.0).then_inc(s_fill, 1)
                v.memset(raw_e, PAD_NODE).then_inc(s_fill, 1)
                dve.done(v.memset(ones[:, :], 1.0))
                dve.done(v.memset(attn[:, D:D + 1], 1.0))
                dve.done(v.memset(attn[:, D + 1:ZW], -1.0))
                dve.done(v.memset(zeros[:, :], 0.0))
                dve.done(v.memset(score_all[:, :], 0.0))
                dve.done(v.memset(tab_max[:, :], -BIG))
                dve.done(v.memset(tab_sum[:, :], 0.0))
                v.wait_ge(s_edges, 96)
                v.tensor_copy(raw_f, raw_e).then_inc(s_rf, 1)
                v.wait_ge(s_x, 32)

                def measure(t, n):
                    for k in range(n):
                        dve.done(v.bn_stats(stats[:, k, :], at(x_all, t + k)))
                    dve.hold(s_held)
                    for k in range(n):
                        dve.done(v.bn_aggr(pair[:, k, :], stats[:, k, :]))
                    dve.wait()
                    dve.done(v.tensor_copy(mean_var[:, span(t, n), :], pair[:, 0:n, :]))

                measure(0, 1)
                with v.Fori(0, (NT - 1) // 4) as i:
                    dve.enter(i, 0, 9)
                    measure(4 * i + 1, 4)
                dve.leave((NT - 1) // 4)
                dve.wait()
                dve.then(v.tensor_scalar(variance, mean_var[:, :, 1], LN_EPS, None, ALU.add))
                rsqrt(v, dve, rstd, variance, scratch)

                def norm(t, slot):
                    wait(v, s_tp, t - 1)
                    v.tensor_scalar(xn[:, slot, :], at(x_all, t), at(mean_var, t)[:, 0:1], rstd[:, span(t, 1)],
                                    ALU.subtract, ALU.mult).then_inc(s_xn, 1)

                def linear(t, slot):
                    wait(v, s_pc, 2 * t + 1)
                    wait(v, s_lin, 4 * t)
                    for w in range(2):
                        for k, sign in ((0, 1.0), (1, -1.0)):
                            v.tensor_tensor_reduce(lin_out[:, 2 * w + k, :], proj[:, slot, w, 0:D], attn[:, 0:D],
                                                   sign * SLOPE / (1.0 - SLOPE), 0.0, ALU.mult, ALU.add,
                                                   proj[:, slot, w, D + k:D + k + 1]).then_inc(s_lin, 1)

                norm(0, 0)
                norm(1, 1)
                norm(2, 0)
                linear(0, 0)
                norm(3, 1)
                linear(1, 1)
                with v.Fori(1, NT // 2 - 1) as i:
                    norm(2 * i + 2, 0)
                    linear(2 * i, 0)
                    norm(2 * i + 3, 1)
                    linear(2 * i + 1, 1)
                norm(NT - 1, 0)
                linear(NT - 3, 0)
                linear(NT - 2, 1)
                linear(NT - 1, 0)

                v.wait_ge(s_pool, 5)
                dve.done(v.tensor_copy(count[:, :], count_i[:, :]))
                dve.done(v.tensor_copy(row_id[:, :], trash_i[:, :]))
                dve.done(v.memset(attr[:, 0, ET:EC], PAD_NODE))
                dve.done(v.memset(dst_f[:, ET:EC], PAD_NODE))
                for b in range(FULL_B + 1):
                    n = min(P, ET - b * P)
                    v.wait_ge(s_et, b + 1)
                    dve.done(v.tensor_copy(attr[:, 0, b * P:b * P + n], psum[:, b % 2, 0:n]))
                    dve.then(v.tensor_copy(dst_f[:, b * P:b * P + n], psum[:, b % 2, P:P + n]))
                    v.sem_inc(s_ec, 1)
                dve.done(v.tensor_copy(edges[:, 0, :], attr[:, 0, :]))
                dve.then(v.tensor_copy(edges[:, 1, :], dst_f[:, :]))
                dve.then(v.tensor_scalar(hi_i, edges[:, 0, :], P.bit_length() - 1, None, ALU.arith_shift_right))
                dve.then(v.tensor_copy(attr[:, 1, :], hi_i))
                dve.then(v.scalar_tensor_tensor(out=attr[:, 2, :], in0=attr[:, 1, :], scalar=-float(P), in1=attr[:, 0, :],
                                                op0=ALU.mult, op1=ALU.add))
                by_half = dst_f[:, 0:ET].rearrange("p (k t) -> p k t", t=HALF)
                v.tensor_reduce(dst_range[:, 0, :], by_half, AX.X, ALU.min).then_inc(s_range, 1)
                v.tensor_reduce(dst_range[:, 1, :], by_half, AX.X, ALU.max).then_inc(s_range, 1)
                v.wait_ge(s_rangeT, 1)
                dve.done(v.tensor_reduce(extremes[0:HALVES, 0:1], psum[0:HALVES, 2, 0:P], AX.X, ALU.min))
                dve.then(v.tensor_reduce(extremes[0:HALVES, 1:2], psum[0:HALVES, 2, P:2 * P], AX.X, ALU.max))
                dve.then(v.tensor_tensor(misfit[0:HALVES, :], extremes[0:HALVES, 1:2], extremes[0:HALVES, 0:1], ALU.subtract))
                v.tensor_scalar(misfit[0:HALVES, :], misfit[0:HALVES, :], P - 0.5, None, ALU.is_gt).then_inc(s_ends, 1)
                v.tensor_scalar(diagonal[0:HALVES, :], ident[0:HALVES, 0:HALVES], extremes[0:HALVES, 0:1], None, ALU.mult).then_inc(s_ends, 1)
                v.wait_ge(s_base, 1)
                dve.done(v.memset(win_rows[:, HALVES:], 0))
                dve.done(v.memset(win_base[:, HALVES:], 0.0))
                dve.done(v.memset(big[:, :], BIG))
                dve.then(v.tensor_copy(win_base[:, 0:HALVES], psum[:, 3, 0:HALVES]))
                dve.done(v.tensor_copy(attn_col[:, :], psum[:, 3, HALVES + 1:HALVES + 1 + DC]))
                dve.done(v.tensor_scalar(fits[:, :], psum[:, 3, HALVES:HALVES + 1], 0.5, None, ALU.is_lt))
                dve.then(v.tensor_scalar(window_f, win_base[:, 0:HALVES], row_id[:, :], None, ALU.add))
                dve.done(v.tensor_copy(win_nodes[:, :], window_f))
                dve.then(v.tensor_scalar(window_f, window_f, float(NP - 1), None, ALU.min))
                dve.done(v.tensor_copy(win_rows[:, 0:HALVES], window_f))
                v.wait_ge(s_wc, GROUPS + 1)
                for c in range(DC):
                    w = wkvT[:, c, :].rearrange("p (h d) -> p h d", d=DH)
                    dve.then(v.tensor_reduce(headmean[:, c, :], w, AX.X, ALU.add))
                    dve.then(v.tensor_scalar(headmean[:, c, :], headmean[:, c, :], 1.0 / DH, None, ALU.mult))
                    dve.then(v.tensor_tensor(w, w, headmean[:, c, :].unsqueeze(2).to_broadcast([P, 2 * HEADS, DH]),
                                             ALU.subtract))

            @block.tensor
            def _(pe):
                pe.wait_ge(s_const, 3)
                pe.wait_ge(s_w, 16 * LOADS)

                def transposes(a, b):
                    for q in range(a, b):
                        wait(pe, s_wc, q - 1)
                        for k in range(4):
                            mm = pe.transpose(psum[:, q % 2, k * P:(k + 1) * P], jobs[4 * q + k][0], ident[:, :])
                        mm.then_inc(s_wt, 1)

                transposes(0, FIRST // 4)

                def turn(t, slot):
                    wait(pe, s_xn, t + 1)
                    wait(pe, s_xt, t - 1)
                    for c in range(DC):
                        mm = pe.transpose(psum[:, 6 + slot, c * P:(c + 1) * P], xn[:, slot, c * P:(c + 1) * P], ident[:, :])
                    mm.then_inc(s_tp, 1)

                def project(t, slot):
                    wait(pe, s_xt, t + 1)
                    wait(pe, s_pc, 2 * t - 2)
                    for a, b, bank in ((0, 512, 2 + 2 * slot), (512, 3 * D, 3 + 2 * slot)):
                        for c in range(DC):
                            mm = pe.matmul(psum[:, bank, 0:b - a], xnT[:, slot, c * P:(c + 1) * P], w3T[:, c, a:b],
                                           start=(c == 0), stop=(c == DC - 1))
                    mm.then_inc(s_pj, 1)

                pe.wait_ge(s_wc, FIRST // 4)
                turn(0, 0)
                turn(1, 1)
                project(0, 0)
                turn(2, 0)
                project(1, 1)
                with pe.Fori(1, NT // 2) as i:
                    turn(2 * i + 1, 1)
                    project(2 * i, 0)
                    turn(2 * i + 2, 0)
                    project(2 * i + 1, 1)
                project(NT - 1, 0)
                transposes(FIRST // 4, GROUPS)
                pe.wait_ge(s_wc, GROUPS - 1)
                mm = pe.transpose(psum[:, GROUPS % 2, 0:NE * FT], b1_raw[0:NE * FT, :], ident[0:NE * FT, 0:NE * FT])
                mm.then_inc(s_wt, 1)
                pe.wait_ge(s_wc, GROUPS + 1)
                pe.wait_ge(s_rf, 1)
                for b in range(FULL_B + 1):
                    n = min(P, ET - b * P)
                    wait(pe, s_ec, b - 1)
                    for j in range(2):
                        mm = pe.transpose(psum[:, b % 2, j * P:j * P + n], raw_f[0:n, j, b, :], ident[0:n, 0:n])
                    mm.then_inc(s_et, 1)
                pe.wait_ge(s_range, 2)
                for j in range(2):
                    mm = pe.transpose(psum[0:HALVES, 2, j * P:(j + 1) * P], dst_range[:, j, :], ident[:, :])
                mm.then_inc(s_rangeT, 1)
                pe.wait_ge(s_ends, 2)
                pe.matmul(psum[:, 3, 0:HALVES], ones[0:HALVES, :], diagonal[0:HALVES, :], start=True, stop=True)
                for c in range(DC):
                    pe.matmul(psum[:, 3, HALVES + 1 + c:HALVES + 2 + c], attn[0:1, c * P:(c + 1) * P], ones[0:1, 0:1], start=True, stop=True)
                pe.matmul(psum[:, 3, HALVES:HALVES + 1], ones[0:HALVES, :], misfit[0:HALVES, :], start=True, stop=True).then_inc(s_base, 1)

            @block.scalar
            def _(act):
                def copies(a, b):
                    for q in range(a, b):
                        act.wait_ge(s_wt, q + 1)
                        for k in range(4):
                            ins = act.copy(jobs[4 * q + k][1], psum[:, q % 2, k * P:(k + 1) * P])
                        ins.then_inc(s_wc, 1)

                def take(t, slot):
                    wait(act, s_tp, t + 1)
                    wait(act, s_pj, t - 1)
                    act.copy(at(xn_all, t), psum[:, 6 + slot, 0:D])
                    act.copy(xnT[:, slot, :], psum[:, 6 + slot, 0:D]).then_inc(s_xt, 1)

                def give(t, slot):
                    wait(act, s_pj, t + 1)
                    wait(act, s_st[slot], 24 * t - 24 * slot)
                    act.copy(proj[:, slot, 0:2, 0:D], psum[:, 2 + 2 * slot, :].rearrange("p (w c) -> p w c", c=D)).then_inc(s_pc, 1)
                    act.copy(proj[:, slot, 2, 0:D], psum[:, 3 + 2 * slot, 0:D]).then_inc(s_pc, 1)

                copies(0, FIRST // 4)
                take(0, 0)
                take(1, 1)
                give(0, 0)
                take(2, 0)
                give(1, 1)
                with act.Fori(1, NT // 2) as i:
                    take(2 * i + 1, 1)
                    give(2 * i, 0)
                    take(2 * i + 2, 0)
                    give(2 * i + 1, 1)
                give(NT - 1, 0)
                copies(FIRST // 4, GROUPS)
                act.wait_ge(s_wt, GROUPS + 1)
                act.copy(b1T[:, :], psum[:, GROUPS % 2, 0:NE * FT]).then_inc(s_wc, 1)

        m = Arena()
        idx = [m.take(2, HALF).bitcast(I32) for _ in range(2)]
        at3 = [m.take(3, HALF) for _ in range(2)]
        z = m.take(PASS, ZW)
        lk = m.take(4, ZW)
        ttr_out = m.take(2, ZW)
        score = [m.take(HALF) for _ in range(2)]
        pen = m.take(2, P)
        top = m.take(HALF)
        expo = m.take(HALF)
        lo_hot = [m.take(HALF, P) for _ in range(2)]
        hi_hot = [m.take(HALF, TABW) for _ in range(2)]
        tabs = m.take(HALF, TABW)
        cnt = m.take(HALF, NT)
        new_max = m.take(NT)
        scale_old = m.take(NT)
        part = m.take(NT)

        s_idx, s_zin1, s_zin = sem("indices_ready"), [sem(f"proj_s_in{i}") for i in range(HALF // 2)], [sem(f"z_in{i}") for i in range(PASS)]
        s_lk, s_sc, s_row, s_top = sem("leaky_done"), sem("score_done"), sem("rows_broadcast"), sem("top_done")
        s_dif, s_exp, s_hot = sem("top_difference"), sem("exp_done"), sem("hot_ready")
        s_tab, s_ev, s_mrg, s_df2, s_ex2 = sem("tables_ready"), sem("tables_copied"), sem("merge_done"), sem("merge_differences"), sem("merge_exps")

        s_zero = sem("zeros_stored")

        m = Arena()
        w_idx = [m.take(HALF).bitcast(I32) for _ in range(2)]
        w_win = [m.take(1).bitcast(I32) for _ in range(2)]
        s_rows_w = m.take(PASS, ZW)
        t_win = m.take(2, ZW)
        dot_w = m.take(4, ZW)
        attn_w = m.take(ZW)
        pen_w = m.take(HALF, P)
        same_w = m.take(2, P)
        ttr_w = m.take(HALF, P)
        vals = [m.take(HALF, 2 * NT) for _ in range(2)]
        m = Arena(x_all[:, :, :].rearrange("p t c -> p (t c)"), NT * D)
        dst_row = m.take(HALF * P)
        src_row = m.take(HALF * P)
        hot_T = m.take(HALF * P)
        lo_w = [m.take(HALF, P) for _ in range(2)]
        hi_w = m.take(HALF, NT)
        gone = m.take(HALF, NT)
        run = m.take(HALF, NT)
        wsum = m.take(HALF, NT)
        new_max_w = m.take(NT)
        scale_w = m.take(NT)
        part_w = m.take(NT)
        score_w = [m.take(HALF) for _ in range(2)]
        neg_src = [m.take(HALF) for _ in range(2)]
        same_count = m.take(HALF)
        inv_count = m.take(HALF)
        top_w = m.take(HALF)
        top_share = m.take(HALF)
        expo_w = m.take(HALF)
        Z_BANK = (0, 1, 2, 7)
        APART = 2.0 ** 100

        s_in = s_zin[0:2]
        s_dstr, s_srcr = s_zin1[0:2]
        s_gone, s_tread = s_ev, s_mrg
        s_hotT, s_z = sem("window_hot_ready"), sem("z_ready")
        s_vexp = sem("exp_values_ready")
        s_neg, s_pen, s_cnt = sem("neg_src_ready"), sem("pen_ready"), sem("counts_ready")
        s_path2, s_last2 = sem("path_steps2"), sem("last_steps2")

        with nc.Block() as block:
            @block.gpsimd
            def _(g):
                with g.If(windowed(g) > 0):
                    def fetch(i, h):
                        k = 2 * i + h
                        hold(g, s_idx, k + 1, s_held)
                        hold(g, s_z, HALF * (k - 1), s_held)
                        for u in range(HALF):
                            g.indirect_dma_start(s_rows_w[:, HALF * h + u, :], None, proj_s, bass.IndirectOffsetOnAxis(
                                ap=w_idx[h][:, u:u + 1], axis=0)).then_inc(s_in[h], 16)
                        g.indirect_dma_start(t_win[:, h, :], None, proj_t, bass.IndirectOffsetOnAxis(
                            ap=w_win[h], axis=0)).then_inc(s_in[h], 16)

                    fetch(0, 0)
                    fetch(0, 1)
                    with g.Fori(1, PASSES) as i:
                        fetch(i, 0)
                        fetch(i, 1)
                with g.Else():
                    def half(i, h):
                        k = 2 * i + h
                        hold(g, s_idx, k + 1, s_held)

                        LAG = HALF // 2

                        def first(u):
                            g.indirect_dma_start(z[:, HALF * h + u, :], None, proj_s, bass.IndirectOffsetOnAxis(
                                ap=idx[h][:, 0, u:u + 1], axis=0)).then_inc(s_zin1[u % LAG], 16)

                        def second(u):
                            hold(g, s_zin1[u % LAG], 16 * (2 * k + u // LAG + 1), s_held)
                            g.indirect_dma_start(z[:, HALF * h + u, :], None, proj_t, bass.IndirectOffsetOnAxis(
                                ap=idx[h][:, 1, u:u + 1], axis=0), compute_op=ALU.add).then_inc(s_zin[HALF * h + u], 16)

                        for u in range(LAG):
                            first(u)
                        for u in range(LAG):
                            second(u)
                            first(u + LAG)
                        for u in range(LAG, HALF):
                            second(u)

                    with g.Fori(0, PASSES) as i:
                        half(i, 0)
                        half(i, 1)

            @block.scalar
            def _(act):
                with act.If(windowed(act) > 0):
                    def fetch_sources(k):
                        hold(act, s_pen, HALF * k, s_held)
                        act.dma_start(src_row, edge_rows[0, span(k * HALF * P, HALF * P)].partition_broadcast(P)).then_inc(s_srcr, 16)

                    def penalties(i, h):
                        k = 2 * i + h
                        wait(act, s_neg, k + 1)
                        wait(act, s_srcr, 16 * k + 16)
                        for u in range(HALF):
                            wait(act, s_top, HALF * (k - 1) + u + 1)
                            act.activation(pen_w[:, u, :], src_row[:, u * P:(u + 1) * P], ACT.Abs, scale=APART,
                                           bias=neg_src[h][:, u:u + 1]).then_inc(s_pen, 1)
                        for u in range(HALF):
                            wait(act, s_pen, HALF * k + u + 1)
                            wait(act, s_cnt, HALF * k + u - 1)
                            act.activation(same_w[:, u % 2, :], pen_w[:, u, :], ACT.Relu, scale=-1.0, bias=ones[:, 0:1],
                                           accum_out=same_count[:, u:u + 1]).then_inc(s_cnt, 1)

                    def absent(k):
                        wait(act, s_df2, 2 * k)
                        for b in range(2):
                            wait(act, s_tab, 2 * k + b + 1)
                            act.activation(gone[:, 4 * b:4 * b + 4, :], psum[:, 5 + b, 0:8 * NT].rearrange("p (t c) -> p t c", c=2 * NT)[:, :, NT:2 * NT],
                                           ACT.Relu, scale=-2.0 * BIG, bias=big[:, :]).then_inc(s_gone, 1)

                    def merge_exps_w(k):
                        wait(act, s_df2, 2 * k + 2)
                        act.activation(run, run, ACT.Exp).then_inc(s_ex2, 1)
                        act.activation(scale_w, scale_w, ACT.Exp).then_inc(s_ex2, 1)

                    def step(i, h, first=False, last=False):
                        k = 2 * i + h
                        if not last:
                            fetch_sources(k + 1)
                        if not first:
                            absent(k - 1)
                        wait(act, s_dif, k + 1)
                        act.activation(expo_w, expo_w, ACT.Exp).then_inc(s_exp, 1)
                        hold(act, s_exp, k + 1, s_held)
                        for u in range(HALF):
                            act.activation(vals[h][:, u, NT:2 * NT], hi_w[:, u, :], ACT.Copy, scale=expo_w[:, u:u + 1]).then_inc(s_vexp, 1)
                        if not first:
                            merge_exps_w(k - 1)
                        if not last:
                            penalties(*((i, 1) if h == 0 else (i + 1, 0)))

                    fetch_sources(0)
                    penalties(0, 0)
                    step(0, 0, first=True)
                    step(0, 1)
                    with act.Fori(1, PASSES - 1) as i:
                        step(i, 0)
                        step(i, 1)
                    step(PASSES - 1, 0)
                    step(PASSES - 1, 1, last=True)
                    absent(HALVES - 1)
                    merge_exps_w(HALVES - 1)
                with act.Else():
                    def leaky(i, h, u):
                        T = PASS * i + HALF * h + u
                        wait(act, s_zin[HALF * h + u], 16 * (i + 1))
                        wait(act, s_sc, T - 3)
                        act.activation(lk[:, u % 4, :], z[:, HALF * h + u, :], ACT.Relu, scale=1.0 - SLOPE).then_inc(s_lk, 1)

                    def copy_tables(i, h, b):
                        k = 2 * i + h
                        wait(act, s_tab, 4 * k + b + 1)
                        wait(act, s_mrg, k)
                        act.copy(tabs[:, 2 * b:2 * b + 2, :], psum[:, 4 + b, 0:2 * TABW].rearrange("p (t c) -> p t c", c=TABW)).then_inc(s_ev, 1)

                    def merge_exps(k):
                        wait(act, s_df2, k + 1)
                        act.activation(tabs[:, :, 0:NT], tabs[:, :, 0:NT], ACT.Exp).then_inc(s_ex2, 1)
                        act.activation(scale_old, scale_old, ACT.Exp).then_inc(s_ex2, 1)

                    def half(i, h):
                        k = 2 * i + h
                        for u in range(6):
                            leaky(i, h, u)
                        for b in range(4):
                            copy_tables(i, h, b)
                        leaky(i, h, 6)
                        leaky(i, h, 7)
                        merge_exps(k)
                        wait(act, s_dif, k + 1)
                        act.activation(expo, expo, ACT.Exp).then_inc(s_exp, 1)

                    half(0, 0)
                    half(0, 1)
                    with act.Fori(1, PASSES) as i:
                        half(i, 0)
                        half(i, 1)
                    for b in range(4):
                        copy_tables(PASSES, 0, b)
                    merge_exps(2 * PASSES)

            @block.tensor
            def _(pe):
                with pe.If(windowed(pe) > 0):
                    def sum_z(i, h):
                        k = 2 * i + h
                        wait(pe, s_hotT, k + 1)
                        wait(pe, s_in[h], 16 * (HALF + 1) * (i + 1))
                        for u in range(HALF):
                            wait(pe, s_sc, HALF * k + u - 3)
                            pe.matmul(psum[:, Z_BANK[u % 4], 0:ZW], hot_T[:, u * P:(u + 1) * P], t_win[:, h, :], start=True, stop=False)
                            pe.matmul(psum[:, Z_BANK[u % 4], 0:ZW], ident[:, :], s_rows_w[:, HALF * h + u, :], start=False, stop=True).then_inc(s_z, 1)

                    def spread(i, h):
                        k = 2 * i + h
                        wait(pe, s_sc, HALF * k + HALF)
                        wait(pe, s_top, HALF * k)
                        for u in range(HALF):
                            mm = pe.matmul(psum[:, 3 + u // 4, (u % 4) * P:(u % 4 + 1) * P], score_w[h][:, u:u + 1].to_broadcast([P, P]),
                                           ident[:, :], start=True, stop=True)
                            if u % 4 == 3:
                                mm.then_inc(s_row, 1)

                    def tables(i, h):
                        k = 2 * i + h
                        wait(pe, s_hot, k + 1)
                        wait(pe, s_vexp, HALF * k + HALF)
                        wait(pe, s_gone, 2 * k)
                        wait(pe, s_tread, k)
                        for u in range(HALF):
                            mm = pe.matmul(psum[:, 5 + u // 4, (u % 4) * 2 * NT:(u % 4 + 1) * 2 * NT], lo_w[h][:, u, :], vals[h][:, u, :],
                                           start=True, stop=True)
                            if u % 4 == 3:
                                mm.then_inc(s_tab, 1)

                    def step(i, h):
                        nxt = (i, 1) if h == 0 else (i + 1, 0)
                        sum_z(*nxt)
                        tables(i, h)
                        spread(*nxt)

                    sum_z(0, 0)
                    spread(0, 0)
                    step(0, 0)
                    step(0, 1)
                    with pe.Fori(1, PASSES - 1) as i:
                        step(i, 0)
                        step(i, 1)
                    step(PASSES - 1, 0)
                    tables(PASSES - 1, 1)
                with pe.Else():
                    for b in range(4):
                        pe.matmul(psum[:, 4 + b, 0:2 * TABW], zeros[:, 0:P], zeros[:, 0:2 * TABW], start=True, stop=True).then_inc(s_tab, 1)

                    def half(i, h):
                        k = 2 * i + h
                        for u in range(HALF):
                            T = HALF * k + u
                            wait(pe, s_sc, T + 1)
                            if u % 2 == 0:
                                wait(pe, s_top, T - HALF + 2)
                            row = psum[:, u // 2, (u % 2) * 2 * P:(u % 2) * 2 * P + 2 * P]
                            pe.matmul(row[:, 0:P], at3[h][:, 0, u:u + 1].to_broadcast([P, P]), ident[:, :], start=True, stop=True)
                            mm = pe.matmul(row[:, P:2 * P], score[h][:, u:u + 1].to_broadcast([P, P]), ident[:, :], start=True,
                                           stop=True)
                            if u % 2 == 1:
                                mm.then_inc(s_row, 1)
                        wait(pe, s_hot, k + 1)
                        for b in range(4):
                            wait(pe, s_ev, 4 * k + b + 1)
                            for j in range(2):
                                u = 2 * b + j
                                mm = pe.matmul(psum[:, 4 + b, j * TABW:(j + 1) * TABW], lo_hot[h][:, u, :], hi_hot[h][:, u, :],
                                               start=True, stop=True)
                            mm.then_inc(s_tab, 1)

                    half(0, 0)
                    half(0, 1)
                    with pe.Fori(1, PASSES) as i:
                        half(i, 0)
                        half(i, 1)

            @block.vector
            def _(v):
                with v.If(windowed(v) > 0):
                    dve = Steps(v, s_path2)

                    def indices(k, h):
                        dve.done(v.tensor_copy(w_win[h], win_rows[:, span(k, 1)]))
                        v.tensor_copy(w_idx[h], edges[:, 0, span(HALF * k, HALF)]).then_inc(s_idx, 1)

                    def sources(k, h):
                        v.tensor_scalar(neg_src[h], attr[:, 0, span(HALF * k, HALF)], -APART, None, ALU.mult).then_inc(s_neg, 1)

                    def hot(k):
                        wait(v, s_dstr, 16 * k + 16)
                        v.tensor_scalar(hot_T, dst_row, win_base[:, span(k, 1)], row_id[:, :], ALU.subtract, ALU.is_equal).then_inc(s_hotT, 1)

                    def table(c):
                        return psum[:, 5:7, 0:8 * NT].rearrange("p b (t c) -> p b t c", c=2 * NT)[:, :, :, c * NT:(c + 1) * NT]

                    def quads(a):
                        return a.rearrange("p (b t) c -> p b t c", t=4)

                    def weighted_sum(k, h, u):
                        hold(v, s_z, HALF * k + u + 1, s_held)
                        v.scalar_tensor_tensor(out=dot_w[:, u % 4, :], in0=psum[:, Z_BANK[u % 4], 0:ZW], scalar=0.0, in1=attn_w, op0=ALU.max,
                                               op1=ALU.mult, accum_out=score_w[h][:, u:u + 1]).then_inc(s_sc, 1)

                    def merge(k, other):
                        wait(v, s_gone, 2 * k + 2)
                        dve.done(v.tensor_tensor(quads(run), table(0), quads(gone), ALU.subtract))
                        other(0)
                        dve.wait()
                        dve.done(v.tensor_reduce(new_max_w, run.rearrange("p t n -> p n t"), AX.X, ALU.max))
                        other(1)
                        dve.wait()
                        dve.done(v.tensor_tensor(new_max_w, new_max_w, tab_max[:, :], ALU.max))
                        other(2)
                        dve.wait()
                        v.tensor_tensor(run, run, new_max_w.unsqueeze(1).to_broadcast([P, HALF, NT]), ALU.subtract).then_inc(s_df2, 1)
                        v.tensor_tensor(scale_w, tab_max[:, :], new_max_w, ALU.subtract).then_inc(s_df2, 1)
                        other(3)
                        wait(v, s_df2, 2 * k + 2)
                        dve.done(v.tensor_copy(tab_max[:, :], new_max_w))
                        other(4)
                        other(5)
                        wait(v, s_ex2, 2 * k + 2)
                        v.tensor_tensor(quads(wsum), quads(run), table(1), ALU.mult).then_inc(s_tread, 1)
                        dve.done(v.tensor_tensor(tab_sum[:, :], tab_sum[:, :], scale_w, ALU.mult))
                        other(6)
                        wait(v, s_tread, k + 1)
                        dve.done(v.tensor_reduce(part_w, wsum.rearrange("p t n -> p n t"), AX.X, ALU.add))
                        other(7)
                        dve.wait()
                        dve.done(v.tensor_tensor(tab_sum[:, :], tab_sum[:, :], part_w, ALU.add))
                    PER_MERGE = 7

                    def step(i, h, first=False, last=False, ending=False):
                        k = 2 * i + h

                        def next_score(u):
                            if not last:
                                weighted_sum(k + 1, 1 - h, u)

                        if not last:
                            hot(k + 1)
                        wait(v, s_tab, 2 * k - 2)
                        lo = attr[:, 2, span(HALF * k, HALF)].unsqueeze(2).to_broadcast([P, HALF, P])
                        hi = attr[:, 1, span(HALF * k, HALF)].unsqueeze(2).to_broadcast([P, HALF, NT])
                        dve.done(v.tensor_tensor(lo_w[h], lo, count[:, :].unsqueeze(1).to_broadcast([P, HALF, P]), ALU.is_equal))
                        wait(v, s_vexp, HALF * k)
                        dve.done(v.tensor_tensor(hi_w, hi, count[:, 0:NT].unsqueeze(1).to_broadcast([P, HALF, NT]), ALU.is_equal))
                        wait(v, s_cnt, HALF * k + HALF)
                        dve.done(v.reciprocal(inv_count, same_count))
                        for u in range(HALF):
                            if u % 4 == 0:
                                hold(v, s_row, 2 * k + u // 4 + 1, s_held)
                            v.tensor_tensor_reduce(ttr_w[:, u, :], psum[:, 3 + u // 4, (u % 4) * P:(u % 4 + 1) * P], pen_w[:, u, :], 1.0, -3.0e38,
                                                   ALU.subtract, ALU.max, top_w[:, u:u + 1]).then_inc(s_top, 1)
                        dve.done(v.tensor_copy(score_all[:, span(HALF * k, HALF)], score_w[h]))
                        wait(v, s_top, HALF * k + HALF)
                        v.tensor_tensor(expo_w, score_w[h], top_w, ALU.subtract).then_inc(s_dif, 1)
                        dve.done(v.tensor_tensor(top_share, top_w, inv_count, ALU.mult))
                        if not ending:
                            wait(v, s_in[1 - h], 16 * (HALF + 1) * (i + 1 + h))
                            indices(k + 3, 1 - h)
                            sources(k + 2, h)
                        dve.wait()
                        v.tensor_tensor(vals[h][:, :, 0:NT], hi_w, top_share.unsqueeze(2).to_broadcast([P, HALF, NT]), ALU.mult).then_inc(s_hot, 1)
                        if first:
                            for u in range(HALF):
                                next_score(u)
                        else:
                            merge(k - 1, next_score)
                        if not last:
                            wait(v, s_sc, HALF * k + 2 * HALF)
                        dve.wait()
                        wait(v, s_hot, k + 1)
                    PER_STEP = 3 + 1 + 1 + 1 + PER_MERGE

                    dve.then(v.tensor_scalar(attn_w, attn[:, :], 1.0 - SLOPE, None, ALU.mult))
                    indices(0, 0)
                    indices(1, 1)
                    sources(0, 0)
                    sources(1, 1)
                    hot(0)
                    wait(v, s_in[0], 16 * (HALF + 1))
                    indices(2, 0)
                    for u in range(HALF):
                        weighted_sum(0, 0, u)
                    wait(v, s_sc, HALF)
                    step(0, 0, first=True)
                    step(0, 1)
                    with v.Fori(1, PASSES - 1) as i:
                        dve.enter(i, 1, 2 * PER_STEP)
                        step(i, 0)
                        step(i, 1)
                    dve.leave(PASSES - 2)
                    step(PASSES - 1, 0, ending=True)
                    step(PASSES - 1, 1, last=True, ending=True)
                    merge(HALVES - 1, lambda u: None)
                    dve.wait()
                with v.Else():
                    dve = Steps(v, s_path2)

                    def prepare(i, h):
                        c = span(PASS * i + HALF * h, HALF)
                        dve.done(v.tensor_copy(at3[h], attr[:, :, c]))
                        v.tensor_copy(idx[h], edges[:, :, c]).then_inc(s_idx, 1)

                    def merge(k):
                        wait(v, s_ev, 4 * k + 4)
                        cn = tabs[:, :, NT:2 * NT]
                        tm = tabs[:, :, 0:NT]
                        ts = tabs[:, :, 2 * NT:3 * NT]
                        dve.then(v.tensor_scalar(cnt, cn, 1.0, None, ALU.max))
                        dve.then(v.reciprocal(cnt, cnt))
                        dve.then(v.tensor_tensor(tm, tm, cnt, ALU.mult))
                        dve.then(v.tensor_scalar(cnt, cn, 0.5, -BIG, ALU.is_lt, ALU.mult))
                        dve.then(v.tensor_tensor(tm, tm, cnt, ALU.add))
                        dve.then(v.tensor_reduce(new_max, tm.rearrange("p t n -> p n t"), AX.X, ALU.max))
                        dve.then(v.tensor_tensor(new_max, new_max, tab_max[:, :], ALU.max))
                        dve.then(v.tensor_tensor(scale_old, tab_max[:, :], new_max, ALU.subtract))
                        v.tensor_tensor(tm, tm, new_max.unsqueeze(1).to_broadcast([P, HALF, NT]), ALU.subtract).then_inc(s_df2, 1)
                        dve.done(v.tensor_copy(tab_max[:, :], new_max))
                        wait(v, s_ex2, 2 * k + 2)
                        dve.then(v.tensor_tensor(tm, tm, ts, ALU.mult))
                        dve.then(v.tensor_reduce(part, tm.rearrange("p t n -> p n t"), AX.X, ALU.add))
                        dve.then(v.tensor_tensor(tab_sum[:, :], tab_sum[:, :], scale_old, ALU.mult))
                        v.tensor_tensor(tab_sum[:, :], tab_sum[:, :], part, ALU.add).then_inc(s_mrg, 1)
                        wait(v, s_mrg, k + 1)
                    MERGE = 12

                    def half(i, h):
                        k = 2 * i + h
                        for u in range(HALF):
                            T = HALF * k + u
                            wait(v, s_sc, T - 1)
                            wait(v, s_lk, T + 1)
                            v.tensor_tensor_reduce(ttr_out[:, u % 2, :], lk[:, u % 4, :], attn[:, :], 1.0, 0.0, ALU.mult, ALU.add,
                                                   score[h][:, u:u + 1]).then_inc(s_sc, 1)
                        merge(k)
                        lo = at3[h][:, 2, :].unsqueeze(2).to_broadcast([P, HALF, P])
                        hi = at3[h][:, 1, :].unsqueeze(2).to_broadcast([P, HALF, NT])
                        dve.done(v.tensor_tensor(lo_hot[h], lo, count[:, :].unsqueeze(1).to_broadcast([P, HALF, P]), ALU.is_equal))
                        dve.done(v.tensor_tensor(hi_hot[h][:, :, NT:2 * NT], hi, count[:, 0:NT].unsqueeze(1).to_broadcast([P, HALF, NT]),
                                                 ALU.is_equal))
                        for u in range(HALF):
                            T = HALF * k + u
                            wait(v, s_top, T - 1)
                            wait(v, s_row, HALF // 2 * k + u // 2 + 1)
                            row = psum[:, u // 2, (u % 2) * 2 * P:(u % 2) * 2 * P + 2 * P]
                            dve.done(v.tensor_scalar(pen[:, u % 2, :], row[:, 0:P], at3[h][:, 0, u:u + 1], -BIG, ALU.not_equal, ALU.mult))
                            dve.hold(s_held)
                            v.tensor_tensor_reduce(ttr_out[:, u % 2, 0:P], row[:, P:2 * P], pen[:, u % 2, :], 1.0, -3.0e38, ALU.add, ALU.max,
                                                   top[:, u:u + 1]).then_inc(s_top, 1)
                        wait(v, s_top, HALF * k + HALF)
                        v.tensor_tensor(expo, score[h], top, ALU.subtract).then_inc(s_dif, 1)
                        hot = hi_hot[h][:, :, NT:2 * NT]
                        dve.done(v.tensor_tensor(hi_hot[h][:, :, 0:NT], hot, top.unsqueeze(2).to_broadcast([P, HALF, NT]), ALU.mult))
                        dve.then(v.tensor_copy(score_all[:, span(HALF * k, HALF)], score[h]))
                        wait(v, s_exp, k + 1)
                        v.tensor_tensor(hi_hot[h][:, :, 2 * NT:3 * NT], hot, expo.unsqueeze(2).to_broadcast([P, HALF, NT]),
                                        ALU.mult).then_inc(s_hot, 1)
                        wait(v, s_hot, k + 1)
                        prepare(i + 1, h)
                    PER = 2 * (MERGE + 2 + HALF + 2 + 1)

                    prepare(0, 0)
                    prepare(0, 1)
                    half(0, 0)
                    half(0, 1)
                    with v.Fori(1, PASSES) as i:
                        dve.enter(i, 1, PER)
                        half(i, 0)
                        half(i, 1)
                    dve.leave(PASSES - 1)
                    merge(2 * PASSES)
                    dve.wait()
                dve = Steps(v, s_last2)
                dve.then(v.tensor_scalar(tab_sum[:, :], tab_sum[:, :], 0.5, None, ALU.max))
                dve.then(v.reciprocal(tab_sum[:, :], tab_sum[:, :]))
                dve.done(v.tensor_copy(max_rsum[:, :, 0], tab_max[:, :]))
                dve.then(v.tensor_copy(max_rsum[:, :, 1], tab_sum[:, :]))

            @block.sync
            def _(sp):
                def clear(rows):
                    sp.dma_start(rows.rearrange("(t p) c -> p t c", p=P),
                                 zeros[:, 0:D].unsqueeze(1).to_broadcast([P, rows.shape[0] // P, D])).then_inc(s_zero, 16)

                with sp.If(windowed(sp) > 0):
                    def fetch(k):
                        sp.dma_start(dst_row, edge_rows[1, span(k * HALF * P, HALF * P)].partition_broadcast(P)).then_inc(s_dstr, 16)

                    fetch(0)
                    clear(acc[0][NT * P:ACC_ROWS, :])
                    clear(moe_in[NT * P:NE * SLOTS, :])
                    with sp.Fori(0, NT) as k:
                        hold(sp, s_hotT, k + 1, s_held)
                        fetch(k + 1)
                        clear(acc[0][span(k * P, P), :])
                        clear(moe_in[span(k * P, P), :])
                    with sp.Fori(0, HALVES - 1 - NT) as k:
                        hold(sp, s_hotT, k + NT + 1, s_held)
                        fetch(k + NT + 1)
                    sp.wait_ge(s_zero, 16 * (2 + 2 * NT))
                with sp.Else():
                    for a in range(ACCS):
                        clear(acc[a])
                    clear(moe_in[0:NE * SLOTS, :])
                    sp.wait_ge(s_zero, 16 * (ACCS + 1))

        m = Arena()
        idx = [m.take(HALF).bitcast(I32) for _ in range(2)]
        dst_h = [m.take(HALF) for _ in range(2)]
        score_h = [m.take(HALF) for _ in range(2)]
        out_idx = [m.take(HALF).bitcast(I32) for _ in range(2)]
        rows = m.take(PASS, ROWW)
        msg = m.take(HALF, D)
        weight = m.take(2, 1)
        alpha = m.take(2, 1)
        picked = m.take(2, P)
        skip_out = m.take(2, P)
        earlier = m.take(HALF)
        away = m.take(HALF)
        x_tile = m.take(D)
        squares = m.take(2, INNER)
        k_sb = m.take(INNER)
        v_sb = m.take(INNER)
        var = m.take(2, HEADS)
        norm_kv = m.take(HEADS)
        inv_kv = m.take(HEADS)
        scratch = m.take(HEADS)
        trash = m.take(1)
        to_window = [m.take(1).bitcast(I32) for _ in range(2)]
        rel = [m.take(HALF) for _ in range(2)]
        wide_diff = m.take(HALF)
        wide_alpha = m.take(HALF)
        wide_picked = m.take(HALF, P)
        window = m.take(2, D)

        s_idx, s_mr = sem("row_indices_ready"), sem("max_rsum_stored")
        s_rows = [sem(f"rows_in{i}") for i in range(PASS)]
        s_acc = [sem(f"accumulated{a}") for a in range(ACCS)]
        s_dr, s_oi, s_w3, s_pick, s_m, s_msg = sem("dst_rows_broadcast"), sem("out_indices_ready"), sem("weights_done"), sem("picks_done"), sem("messages_ready"), sem("messages_copied")
        s_xt3, s_kv, s_sq, s_kc, s_nv, s_dots = sem("mix_x_ready"), sem("kv_ready"), sem("squares_done"), sem("keys_copied"), sem("values_ready"), sem("dots_added")
        s_red = sem("squares_summed")
        s_half, s_wacc = s_rows[0:2], s_acc[0]
        s_to, s_diff, s_wexp, s_win = sem("to_window_ready"), sem("differences_ready"), sem("window_weights_done"), sem("window_sums_done")
        s_xz, s_xr = sem("x_padding_zero"), sem("x_loaded_again")
        s_path3 = sem("path_steps3")

        with nc.Block() as block:
            @block.sync
            def _(sp):
                sp.dma_start(node_rows.rearrange("(t p) c -> p t c", p=P)[:, :, D:ROWW], max_rsum[:, :, :]).then_inc(s_mr, 16)
                sp.wait_ge(s_xz, 1)
                sp.dma_start(x_all[:, 0:NT - 1, :], x[0:(NT - 1) * P, :].rearrange("(t p) c -> p t c", p=P)).then_inc(s_xr, 16)
                sp.dma_start(x_all[0:TAIL, NT - 1, :], x[(NT - 1) * P:N, :]).then_inc(s_xr, 16)
                sp.wait_ge(s_xr, 32)

            @block.gpsimd
            def _(g):
                g.wait_ge(s_mr, 16)
                with g.If(windowed(g) > 0):
                    def fetch_half(k, h):
                        hold(g, s_idx, k + 1, s_held)
                        for u in range(HALF):
                            hold(g, s_win, HALF * (k - 2) + u + 1, s_held)
                            g.indirect_dma_start(rows[:, HALF * h + u, :], None, node_rows,
                                                 bass.IndirectOffsetOnAxis(ap=idx[h][:, u:u + 1], axis=0)).then_inc(s_half[h], 16)
                            if u == HALF // 2 - 1 and not (isinstance(k, int) and k < 2):
                                add_window(k - 2, h)

                    def add_window(k, h):
                        hold(g, s_to, k + 1, s_held)
                        hold(g, s_msg, k + 1, s_held)
                        hold(g, s_wacc, 16 * k, s_held)
                        g.indirect_dma_start(acc[0], bass.IndirectOffsetOnAxis(ap=to_window[h], axis=0), window[:, h, :],
                                             None, compute_op=ALU.add).then_inc(s_wacc, 16)

                    fetch_half(0, 0)
                    fetch_half(1, 1)
                    fetch_half(2, 0)
                    with g.Fori(1, PASSES) as i:
                        fetch_half(2 * i + 1, 1)
                        fetch_half(2 * i + 2, 0)
                    add_window(HALVES - 1, 1)
                    g.wait_ge(s_wacc, 16 * HALVES)
                    g.wait_ge(s_half[0], 16 * HALF * (PASSES + 1))
                with g.Else():
                    def gather(k, h):
                        hold(g, s_idx, k + 1, s_held)
                        return lambda u: g.indirect_dma_start(
                            rows[:, HALF * h + u, :], None, node_rows,
                            bass.IndirectOffsetOnAxis(ap=idx[h][:, u:u + 1], axis=0)).then_inc(s_rows[HALF * h + u], 16)

                    def scatter(k, h, u):
                        a = u % ACCS
                        n = (HALF // ACCS) * k + u // ACCS
                        hold(g, s_msg, HALF * k + u + 1, s_held)
                        hold(g, s_acc[a], 16 * n, s_held)
                        g.indirect_dma_start(acc[a], bass.IndirectOffsetOnAxis(ap=out_idx[h][:, u:u + 1], axis=0), msg[:, u, :],
                                             None, compute_op=ALU.add).then_inc(s_acc[a], 16)

                    def half(i, h):
                        k = 2 * i + h
                        fetch = gather(k + 1, 1 - h)
                        hold(g, s_oi, k + 1, s_held)
                        for u in range(HALF):
                            fetch(u)
                            scatter(k, h, u)

                    fetch = gather(0, 0)
                    for u in range(HALF):
                        fetch(u)
                    half(0, 0)
                    half(0, 1)
                    with g.Fori(1, PASSES) as i:
                        half(i, 0)
                        half(i, 1)
                    for a in range(ACCS):
                        g.wait_ge(s_acc[a], 16 * (ET // ACCS))
                    for u in range(HALF):
                        g.wait_ge(s_rows[u], 16 * (PASSES + 1))

            @block.scalar
            def _(act):
                def mix(i):
                    wait(act, s_kv, i)
                    act.copy(x_tile, at(xn_all, i)).then_inc(s_xt3, 1)
                    wait(act, s_kv, i + 1)
                    wait(act, s_red, i)
                    act.activation(squares[:, 0, :], psum[:, 4, :], ACT.Square).then_inc(s_sq, 1)
                    act.activation(squares[:, 1, :], psum[:, 5, :], ACT.Square).then_inc(s_sq, 1)
                    wait(act, s_dots, i)
                    act.copy(k_sb, psum[:, 4, :]).then_inc(s_kc, 1)

                with act.If(windowed(act) > 0):
                    def step(i, h):
                        k = 2 * i + h
                        wait(act, s_diff, k + 1)
                        act.activation(wide_diff, wide_diff, ACT.Exp).then_inc(s_wexp, 1)
                        wait(act, s_win, HALF * k + HALF)
                        wait(act, s_wacc, 16 * (k - 1))
                        act.copy(window[:, h, :], psum[:, h, 0:D]).then_inc(s_msg, 1)

                    step(0, 0)
                    mix(0)
                    step(0, 1)
                    with act.Fori(1, PASSES) as i:
                        step(i, 0)
                        mix(i)
                        step(i, 1)
                with act.Else():
                    def half(i, h):
                        k = 2 * i + h
                        for u in range(HALF):
                            T = HALF * k + u
                            wait(act, s_rows[HALF * h + u], 16 * (i + 1))
                            wait(act, s_pick, T - 1)
                            act.activation(weight[:, u % 2, :], rows[:, HALF * h + u, D:D + 1], ACT.Exp, scale=-1.0,
                                           bias=score_h[h][:, u:u + 1]).then_inc(s_w3, 1)
                            if u >= 1:
                                give(i, h, u - 1)
                        give(i, h, HALF - 1)

                    def give(i, h, u):
                        k = 2 * i + h
                        T = HALF * k + u
                        wait(act, s_m, T + 1)
                        wait(act, s_acc[u % ACCS], 16 * ((HALF // ACCS) * (k - 1) + u // ACCS + 1))
                        act.copy(msg[:, u, :], psum[:, 2 + u % 2, 0:D]).then_inc(s_msg, 1)

                    half(0, 0)
                    mix(0)
                    half(0, 1)
                    with act.Fori(1, PASSES) as i:
                        half(i, 0)
                        mix(i)
                        half(i, 1)

            @block.tensor
            def _(pe):
                pe.matmul(psum[:, 6, :], zeros[:, 0:P], zeros[:, :], start=True, stop=True)

                def keys_values(i):
                    wait(pe, s_xt3, i + 1)
                    wait(pe, s_nv, i)
                    wait(pe, s_kc, i)
                    for half_ in range(2):
                        for c in range(DC):
                            mm = pe.matmul(psum[:, 4 + half_, :], x_tile[:, c * P:(c + 1) * P],
                                           wkvT[:, c, half_ * INNER:(half_ + 1) * INNER], start=(c == 0), stop=(c == DC - 1))
                    mm.then_inc(s_kv, 1)

                def add_dots(i):
                    wait(pe, s_kc, i + 1)
                    wait(pe, s_nv, i + 1)
                    for q in range(PAIRS):
                        mm = pe.matmul(psum[:, 6, q * P:(q + 1) * P], v_sb[:, q * P:(q + 1) * P], k_sb[:, q * P:(q + 1) * P],
                                       start=False, stop=True, skip_group_check=True)
                    mm.then_inc(s_dots, 1)

                with pe.If(windowed(pe) > 0):
                    def window_sums(i, h):
                        k = 2 * i + h
                        wait(pe, s_msg, k - 1)
                        for u in range(HALF):
                            wait(pe, s_pick, HALF * k + u + 1)
                            pe.matmul(psum[:, h, 0:D], wide_picked[:, u, :], rows[:, HALF * h + u, 0:D],
                                      start=(u == 0), stop=(u == HALF - 1)).then_inc(s_win, 1)

                    def step(i, first=False):
                        window_sums(i, 0)
                        if not first:
                            add_dots(i - 1)
                        keys_values(i)
                        window_sums(i, 1)

                    step(0, first=True)
                    with pe.Fori(1, PASSES) as i:
                        step(i)
                    add_dots(PASSES - 1)
                with pe.Else():
                    def spread(i, h):
                        k = 2 * i + h
                        wait(pe, s_idx, k + 1)
                        wait(pe, s_pick, HALF * k)
                        for u in range(HALF):
                            mm = pe.matmul(psum[:, u // 4, (u % 4) * P:(u % 4 + 1) * P], dst_h[h][:, u:u + 1].to_broadcast([P, P]), ident[:, :],
                                           start=True, stop=True)
                        mm.then_inc(s_dr, 1)

                    def sums(i, h):
                        k = 2 * i + h
                        for u in range(HALF):
                            T = HALF * k + u
                            wait(pe, s_pick, T + 1)
                            wait(pe, s_msg, T - 1)
                            pe.matmul(psum[:, 2 + u % 2, 0:D], picked[:, u % 2, :], rows[:, HALF * h + u, 0:D],
                                      start=True, stop=True).then_inc(s_m, 1)

                    def whole(i):
                        spread(i, 0)
                        sums(i, 0)
                        keys_values(i)
                        spread(i, 1)
                        sums(i, 1)
                        add_dots(i)

                    whole(0)
                    with pe.Fori(1, PASSES) as i:
                        whole(i)

            @block.vector
            def _(v):
                v.memset(x_all[96:P, NT - 1, :], 0.0).then_inc(s_xz, 1)

                def mix_squares(i, dve):
                    wait(v, s_sq, 2 * i + 2)
                    dve.done(v.tensor_reduce(var[:, 0, :], squares[:, 0, :].rearrange("p (h d) -> p h d", d=DH), AX.X, ALU.add))
                    ins = v.tensor_reduce(var[:, 1, :], squares[:, 1, :].rearrange("p (h d) -> p h d", d=DH), AX.X, ALU.add)
                    ins.then_inc(s_red, 1)
                    wait(v, s_red, i + 1)
                    dve.wait()
                    dve.done(v.tensor_scalar(var, var, 1.0 / DH, LN_EPS, ALU.mult, ALU.add))

                def mix_norms(n, dve):
                    dve.wait()
                    if n == 0:
                        dve.done(v.tensor_tensor(norm_kv, var[:, 0, :], var[:, 1, :], ALU.mult))
                    else:
                        rsqrt_step(v, dve, n - 1, inv_kv, norm_kv, scratch)

                def mix_values(i, dve):
                    dve.wait()
                    wait(v, s_dots, i)
                    v.tensor_tensor(v_sb.rearrange("p (h d) -> p h d", d=DH), psum[:, 5, :].rearrange("p (h d) -> p h d", d=DH),
                                    inv_kv.unsqueeze(2).to_broadcast([P, HEADS, DH]), ALU.mult).then_inc(s_nv, 1)

                def mix(i, dve):
                    mix_squares(i, dve)
                    for n in range(RSQRT_STEPS + 1):
                        mix_norms(n, dve)
                    mix_values(i, dve)
                PER_MIX = 3 + RSQRT_STEPS

                with v.If(windowed(v) > 0):
                    dve = Steps(v, s_path3)

                    def prepare(i, h):
                        c = span(PASS * i + HALF * h, HALF)
                        dve.done(v.tensor_scalar(rel[h], dst_f[:, c], win_base[:, span(2 * i + h, 1)], None, ALU.subtract))
                        dve.done(v.tensor_copy(score_h[h], score_all[:, c]))

                    def indices(i, h):
                        v.tensor_copy(idx[h], edges[:, 0, span(PASS * i + HALF * h, HALF)]).then_inc(s_idx, 1)

                    def step(i, h, between=None):
                        k = 2 * i + h
                        wait(v, s_wacc, 16 * (k - 1))
                        v.tensor_copy(to_window[h], win_nodes[:, span(k, 1)]).then_inc(s_to, 1)
                        wait(v, s_half[h], 16 * HALF * (i + 1))
                        indices(i + 1, h)
                        dve.wait()
                        row = rows[:, HALF * h:HALF * h + HALF, :]
                        v.tensor_tensor(wide_diff, score_h[h], row[:, :, D], ALU.subtract).then_inc(s_diff, 1)
                        wait(v, s_wexp, k + 1)
                        dve.then(v.tensor_tensor(wide_alpha, wide_diff, row[:, :, D + 1], ALU.mult))
                        wait(v, s_win, HALF * k)
                        for u in range(HALF):
                            v.tensor_scalar(wide_picked[:, u, :], count[:, :], rel[h][:, u:u + 1], wide_alpha[:, u:u + 1],
                                            ALU.is_equal, ALU.mult).then_inc(s_pick, 1)
                            if between:
                                between(u)
                        wait(v, s_pick, HALF * k + HALF)
                        prepare(i + 1, h)
                    PER_STEP = 1 + 2

                    indices(0, 0)
                    indices(0, 1)
                    prepare(0, 0)
                    prepare(0, 1)
                    def norms_between(u):
                        mix_norms(u, dve)

                    def finish_mix(i):
                        for n in range(HALF, RSQRT_STEPS + 1):
                            mix_norms(n, dve)
                        mix_values(i, dve)

                    step(0, 0)
                    step(0, 1)
                    mix_squares(0, dve)
                    with v.Fori(1, PASSES) as i:
                        dve.enter(i, 1, 2 * PER_STEP + PER_MIX)
                        step(i, 0, norms_between)
                        finish_mix(i - 1)
                        step(i, 1)
                        mix_squares(i, dve)
                    dve.leave(PASSES - 1)
                    for n in range(HALF):
                        mix_norms(n, dve)
                    finish_mix(PASSES - 1)
                with v.Else():
                    dve = Steps(v, s_path3)

                    def prepare(i, h):
                        c = span(PASS * i + HALF * h, HALF)
                        dve.done(v.tensor_copy(dst_h[h], dst_f[:, c]))
                        dve.done(v.tensor_copy(score_h[h], score_all[:, c]))
                        v.tensor_copy(idx[h], edges[:, 0, c]).then_inc(s_idx, 1)

                    def half(i, h):
                        k = 2 * i + h
                        wait(v, s_dr, k + 1)
                        row = [psum[:, u // 4, (u % 4) * P:(u % 4 + 1) * P] for u in range(HALF)]
                        for u in range(HALF):
                            dve.wait(1)
                            dve.done(v.scalar_tensor_tensor(out=skip_out[:, u % 2, :], in0=row[u], scalar=dst_h[h][:, u:u + 1], in1=below[:, :],
                                                                  op0=ALU.is_equal, op1=ALU.mult, accum_out=earlier[:, u:u + 1]))
                        dve.wait()
                        dve.then(v.tensor_scalar(away, dst_h[h], trash, -1.0, ALU.subtract, ALU.mult))
                        dve.then(v.scalar_tensor_tensor(out=away, in0=earlier, scalar=1.0, in1=away, op0=ALU.min, op1=ALU.mult))
                        wait(v, s_acc[ACCS - 1], 16 * (HALF // ACCS) * (k - 1))
                        v.tensor_tensor(out_idx[h], away, dst_h[h], ALU.add).then_inc(s_oi, 1)
                        for u in range(HALF):
                            T = HALF * k + u
                            wait(v, s_w3, T + 1)
                            dve.then(v.tensor_tensor(alpha[:, u % 2, :], weight[:, u % 2, :], rows[:, HALF * h + u, D + 1:D + 2], ALU.mult))
                            wait(v, s_m, T - 1)
                            v.tensor_scalar(picked[:, u % 2, :], row[u], dst_h[h][:, u:u + 1], alpha[:, u % 2, :], ALU.is_equal,
                                            ALU.mult).then_inc(s_pick, 1)
                        wait(v, s_m, HALF * k + HALF)
                        wait(v, s_pick, HALF * k + HALF)
                        prepare(i + 1, h)
                    PER_HALF = HALF + 2 + HALF + 2

                    dve.then(v.tensor_scalar(trash, row_id[:, :], float(NP), None, ALU.add))
                    prepare(0, 0)
                    prepare(0, 1)
                    half(0, 0)
                    mix(0, dve)
                    half(0, 1)
                    with v.Fori(1, PASSES) as i:
                        dve.enter(i, 1, 2 * PER_HALF + PER_MIX)
                        half(i, 0)
                        mix(i, dve)
                        half(i, 1)
                    dve.leave(PASSES - 1)

        m = Arena()
        parts = m.take(2, ACCS, D)
        summed = m.take(2, 2, D)
        logits = m.take(NT, NE)
        x_tile = m.take(2, D)
        hT = m.take(2, D)
        h_sb = m.take(2, D)
        s_hs = sem("h_copied")
        stats = m.take(2, 6)
        mean_var = m.take(NT, 2)
        pair = m.take(2, 2)
        variance = m.take(NT)
        rstd = m.take(NT)
        scratch = m.take(NT)
        dotsT = m.take(PAIRS, P)
        fold = m.take(PAIRS, D)
        mixed = m.take(DC, D)
        same_head = m.take(P)
        bias_all = m.take(D)
        s_fold, s_foldc = sem("fold_ready"), sem("fold_copied")
        s_pin = [sem(f"parts_in{i}") for i in range(2)]
        s_sum, s_x4, s_mm, s_xa, s_h, s_ht, s_htc, s_lg, s_lgc = (sem("parts_summed"), sem("x_tile_ready"), sem("mixed_ready"), sem("mixed_read"),
            sem("h_ready"), sem("h_transposed"), sem("hT_ready"), sem("logits_ready"), sem("logits_copied"))
        s_gp = sem("sum_steps")

        with nc.Block() as block:
            @block.sync
            def _(sp):
                def loads(n):
                    def load(t, slot):
                        wait(sp, s_sum, t - 1)
                        for a in range(n):
                            sp.dma_start(parts[:, slot, a, :], acc[a][span(t * P, P), :]).then_inc(s_pin[slot], 16)
                    load(0, 0)
                    load(1, 1)
                    with sp.Fori(1, NT // 2) as i:
                        load(2 * i, 0)
                        load(2 * i + 1, 1)
                    load(NT - 1, 0)

                with sp.If(windowed(sp) > 0):
                    loads(1)
                with sp.Else():
                    loads(ACCS)

            @block.gpsimd
            def _(g):
                def sums(n):
                    st = Steps(g, s_gp)

                    def add(t, slot):
                        wait(g, s_pin[slot], 8 * n * (t - slot) + 16 * n)
                        wait(g, s_xa, t - 1)
                        whole, other = summed[:, slot, 0, :], summed[:, slot, 1, :]
                        if n == 1:
                            g.tensor_tensor(whole, parts[:, slot, 0, :], bias_all, ALU.add).then_inc(s_sum, 1)
                        else:
                            st.done(g.tensor_tensor(other, parts[:, slot, 1, :], bias_all, ALU.add))
                            st.then(g.tensor_tensor(whole, parts[:, slot, 2, :], parts[:, slot, 3, :], ALU.add))
                            st.then(g.tensor_tensor(whole, whole, parts[:, slot, 0, :], ALU.add))
                            g.tensor_tensor(whole, whole, other, ALU.add).then_inc(s_sum, 1)
                    add(0, 0)
                    add(1, 1)
                    with g.Fori(1, NT // 2) as i:
                        st.enter(i, 1, 0 if n == 1 else 6)
                        add(2 * i, 0)
                        add(2 * i + 1, 1)
                    st.leave(NT // 2 - 1)
                    add(NT - 1, 0)

                g.wait_ge(s_foldc, 1)
                with g.If(windowed(g) > 0):
                    sums(1)
                with g.Else():
                    sums(ACCS)

            @block.tensor
            def _(pe):
                for j in range(2):
                    mm = pe.matmul(psum[:, 4, 0:D], ones[0:1, :], bias_row[:, j, :], start=(j == 0), stop=(j == 1))
                mm.then_inc(s_fold, 1)
                pe.wait_ge(s_foldc, 2)
                for q in range(PAIRS):
                    mm = pe.matmul(psum[:, q // 2, (q % 2) * D:(q % 2 + 1) * D], dotsT[:, q, :], woutT[:, q, :], start=True, stop=True)
                mm.then_inc(s_fold, 1)
                pe.wait_ge(s_foldc, 3)
                for c in range(DC):
                    for q in range(PAIRS):
                        mm = pe.matmul(psum[:, 2 + c, 0:D], wq[:, q, c * P:(c + 1) * P], fold[:, q, :], start=(q == 0), stop=(q == PAIRS - 1))
                mm.then_inc(s_fold, 1)
                pe.wait_ge(s_foldc, 4)

                def mix(t, slot):
                    wait(pe, s_x4, t + 1)
                    wait(pe, s_xa, t - 1)
                    for c in range(DC):
                        mm = pe.matmul(psum[:, slot, 0:D], x_tile[:, slot, c * P:(c + 1) * P], mixed[:, c, :], start=(c == 0), stop=(c == DC - 1))
                    mm.then_inc(s_mm, 1)

                def gate(t, slot):
                    wait(pe, s_h, t + 1)
                    wait(pe, s_htc, t - 1)
                    for c in range(DC):
                        mm = pe.transpose(psum[:, 4 + slot, c * P:(c + 1) * P], h_sb[:, slot, c * P:(c + 1) * P], ident[:, :])
                    mm.then_inc(s_ht, 1)

                def logit(t, slot):
                    wait(pe, s_htc, t + 1)
                    wait(pe, s_lgc, t - 1)
                    for c in range(DC):
                        mm = pe.matmul(psum[:, 6 + slot, 0:NE], hT[:, slot, c * P:(c + 1) * P], gw[:, c, :], start=(c == 0), stop=(c == DC - 1))
                    mm.then_inc(s_lg, 1)

                mix(0, 0)
                mix(1, 1)
                with pe.Fori(1, NT // 2) as i:
                    mix(2 * i, 0)
                    mix(2 * i + 1, 1)
                mix(NT - 1, 0)
                gate(0, 0)
                gate(1, 1)
                logit(0, 0)
                with pe.Fori(1, NT // 2) as i:
                    gate(2 * i, 0)
                    logit(2 * i - 1, 1)
                    gate(2 * i + 1, 1)
                    logit(2 * i, 0)
                gate(NT - 1, 0)
                logit(NT - 2, 1)
                logit(NT - 1, 0)

            @block.scalar
            def _(act):
                def take(t, slot):
                    wait(act, s_mm, t - 1)
                    act.copy(x_tile[:, slot, :], at(xn_all, t)).then_inc(s_x4, 1)

                def turn(t, slot):
                    wait(act, s_h, t + 1)
                    act.copy(at(xn_all, t), h_sb[:, slot, :]).then_inc(s_hs, 1)
                    wait(act, s_ht, t + 1)
                    wait(act, s_lg, t - 1)
                    act.copy(hT[:, slot, :], psum[:, 4 + slot, 0:D]).then_inc(s_htc, 1)

                def keep(t, slot):
                    wait(act, s_lg, t + 1)
                    act.copy(at(logits, t), psum[:, 6 + slot, 0:NE]).then_inc(s_lgc, 1)
                take(0, 0)
                take(1, 1)
                with act.Fori(1, NT // 2) as i:
                    take(2 * i, 0)
                    take(2 * i + 1, 1)
                take(NT - 1, 0)
                turn(0, 0)
                turn(1, 1)
                keep(0, 0)
                with act.Fori(1, NT // 2) as i:
                    turn(2 * i, 0)
                    keep(2 * i - 1, 1)
                    turn(2 * i + 1, 1)
                    keep(2 * i, 0)
                turn(NT - 1, 0)
                keep(NT - 2, 1)
                keep(NT - 1, 0)

            @block.vector
            def _(v):
                v.wait_ge(s_fold, 1)
                v.tensor_copy(bias_all, psum[:, 4, 0:D]).then_inc(s_foldc, 1)
                dve.done(v.memset(same_head, 0.0))
                dve.wait()
                for h in range(P // DH):
                    dve.done(v.memset(same_head[h * DH:(h + 1) * DH, h * DH:(h + 1) * DH], 1.0 / N))
                dve.wait()
                v.tensor_tensor(dotsT, psum[:, 6, :].rearrange("p (q j) -> p q j", j=P), same_head.unsqueeze(1).to_broadcast([P, PAIRS, P]),
                                ALU.mult).then_inc(s_foldc, 1)
                v.wait_ge(s_fold, 2)
                dve.done(v.tensor_copy(fold[:, 0:2, :], psum[:, 0, :].rearrange("p (q j) -> p q j", j=D)))
                dve.wait()
                v.tensor_copy(fold[:, 2:4, :], psum[:, 1, :].rearrange("p (q j) -> p q j", j=D)).then_inc(s_foldc, 1)
                v.wait_ge(s_fold, 3)
                v.tensor_copy(mixed, psum[:, 2:4, 0:D]).then_inc(s_foldc, 1)

                def residual(t, n):
                    for k in range(n):
                        wait(v, s_mm, t + k + 1)
                        dve.done(v.tensor_tensor(at(x_all, t + k), at(x_all, t + k), psum[:, k, 0:D], ALU.add))
                    dve.wait()
                    for k in range(n):
                        wait(v, s_sum, t + k + 1)
                        v.tensor_tensor(at(x_all, t + k), at(x_all, t + k), summed[:, k, 0, :], ALU.add).then_inc(s_xa, 1)
                    for k in range(n):
                        hold(v, s_xa, t + k + 1, s_held)
                        dve.done(v.bn_stats(stats[:, k, :], at(x_all, t + k)))
                    dve.hold(s_held)
                    for k in range(n):
                        dve.done(v.bn_aggr(pair[:, k, :], stats[:, k, :]))
                    dve.wait()
                    dve.done(v.tensor_copy(mean_var[:, span(t, n), :], pair[:, 0:n, :]))

                def normalise(t, slot):
                    wait(v, s_ht, t - 1)
                    wait(v, s_hs, t - 1)
                    v.tensor_scalar(h_sb[:, slot, :], at(x_all, t), at(mean_var, t)[:, 0:1], rstd[:, span(t, 1)],
                                    ALU.subtract, ALU.mult).then_inc(s_h, 1)

                residual(0, 2)
                with v.Fori(1, NT // 2) as i:
                    dve.enter(i, 1, 7)
                    residual(2 * i, 2)
                dve.leave(NT // 2 - 1)
                residual(NT - 1, 1)
                dve.wait()
                dve.then(v.tensor_scalar(variance, mean_var[:, :, 1], LN_EPS, None, ALU.add))
                rsqrt(v, dve, rstd, variance, scratch)
                normalise(0, 0)
                normalise(1, 1)
                with v.Fori(1, NT // 2) as i:
                    normalise(2 * i, 0)
                    normalise(2 * i + 1, 1)
                normalise(NT - 1, 0)

        m = Arena()
        m.take(2, ACCS, D)
        m.take(2, 2, D)
        m.take(NT, NE)
        expos = m.take(NT, NE)
        probs = m.take(NT, NE)
        chosen = m.take(NT, NE)
        tmp = m.take(NT, NE)
        place_e = m.take(NT, NE)
        totals = m.take(NE, NT)
        upto = m.take(NE, NT)
        red = m.take(NT)
        prob = m.take(NT)
        expert = m.take(NT)
        pos = m.take(NT)
        kept = m.take(NT)
        trash = m.take(NT)
        s_r, s_rm, s_re, s_sent = sem("routed"), sem("ranks_ready"), sem("route_exp"), sem("rows_sent")

        with nc.Block() as block:
            @block.vector
            def _(v):
                def wide(a):
                    return a.unsqueeze(2).to_broadcast([P, NT, NE])
                ids = count[:, 0:NE].unsqueeze(1).to_broadcast([P, NT, NE])
                dve.then(v.tensor_scalar(trash, count[:, 0:NT], float(P), row_id[:, :], ALU.mult, ALU.add))
                dve.then(v.tensor_scalar(trash, trash, float(NE * SLOTS), None, ALU.add))
                dve.then(v.tensor_tensor(logits, logits, gb[:, :].unsqueeze(1).to_broadcast([P, NT, NE]), ALU.add))
                dve.then(v.tensor_reduce(red, logits, AX.X, ALU.max))
                v.tensor_tensor(expos, logits, wide(red), ALU.subtract).then_inc(s_r, 1)
                v.wait_ge(s_re, 1)
                dve.then(v.tensor_reduce(red, expos, AX.X, ALU.add))
                dve.then(v.reciprocal(red, red))
                dve.then(v.tensor_tensor(probs, expos, wide(red), ALU.mult))
                dve.then(v.tensor_reduce(prob, probs, AX.X, ALU.max))
                dve.then(v.tensor_tensor(tmp, probs, wide(prob), ALU.not_equal))
                dve.then(v.scalar_tensor_tensor(out=tmp, in0=tmp, scalar=float(NE), in1=ids, op0=ALU.mult, op1=ALU.add))
                dve.then(v.tensor_reduce(expert, tmp, AX.X, ALU.min))
                v.tensor_tensor(chosen, wide(expert), ids, ALU.is_equal).then_inc(s_r, 1)
                v.wait_ge(s_rm, 1)
                dve.then(v.tensor_copy(totals, psum[:, 1, 0:NT * NE].rearrange("p (t e) -> p e t", e=NE)))
                for e in range(NE):
                    dve.done(v.tensor_tensor_scan(upto[:, e, :], totals[:, e, :], zeros[:, 0:NT], 0.0, ALU.add, ALU.add))
                dve.wait()
                dve.then(v.tensor_tensor(upto, upto, totals, ALU.subtract))
                dve.then(v.tensor_tensor(place_e, upto.rearrange("p e t -> p t e"), psum[:, 0, 0:NT * NE].rearrange("p (t e) -> p t e", e=NE), ALU.add))
                dve.then(v.tensor_tensor(place_e, place_e, chosen, ALU.mult))
                dve.then(v.tensor_reduce(pos, place_e, AX.X, ALU.add))
                dve.then(v.tensor_scalar(kept, pos, float(CAP), None, ALU.is_lt))
                dve.then(v.tensor_tensor(gate_prob[:, :], prob, kept, ALU.mult))
                dve.then(v.tensor_scalar(expert, expert, float(SLOTS), None, ALU.mult))
                dve.then(v.scalar_tensor_tensor(out=red, in0=pos, scalar=float(CAP - 1), in1=expert, op0=ALU.min, op1=ALU.add))
                dve.done(v.tensor_copy(slot_in[:, :], red))
                dve.then(v.tensor_tensor(red, red, trash, ALU.subtract))
                dve.then(v.tensor_tensor(red, red, kept, ALU.mult))
                v.tensor_tensor(slot_out[:, :], red, trash, ALU.add).then_inc(s_r, 1)
                v.wait_ge(s_r, 3)

            @block.scalar
            def _(act):
                act.wait_ge(s_r, 1)
                act.activation(expos, expos, ACT.Exp).then_inc(s_re, 1)

            @block.tensor
            def _(pe):
                pe.wait_ge(s_r, 2)
                pe.matmul(psum[:, 0, 0:NT * NE], above[:, :], chosen.rearrange("p t e -> p (t e)"), start=True, stop=True)
                pe.matmul(psum[:, 1, 0:NT * NE], ones[:, :], chosen.rearrange("p t e -> p (t e)"), start=True, stop=True).then_inc(s_rm, 1)

            @block.gpsimd
            def _(g):
                g.wait_ge(s_r, 3)
                for t in range(NT):
                    g.indirect_dma_start(moe_in, bass.IndirectOffsetOnAxis(ap=slot_out[:, t:t + 1], axis=0), xn_all[:, t, :], None).then_inc(s_sent, 16)
                g.wait_ge(s_sent, 16 * NT)

        m = Arena()
        w1_sb = m.take(2, DC, F)
        w2_sb = m.take(2, FT * D)
        rows_in = m.take(2, CT * D)
        y_sb = m.take(2, D)
        big = xn_all[:, :, :].rearrange("p t c -> p (t c)")
        hid = big[:, 0:FT * SLOTS].rearrange("p (f s) -> p f s", s=SLOTS)
        inT = big[:, FT * SLOTS:FT * SLOTS + DC * SLOTS].rearrange("p (c s) -> p c s", s=SLOTS)
        b2_all = big[:, (FT + DC) * SLOTS:(FT + DC) * SLOTS + NE * D].rearrange("p (e c) -> p e c", c=D)
        s_win = [sem(f"expert_loaded{i}") for i in range(2)]
        s_b2, s_it, s_itc, s_hid, s_hc, s_y, s_yc = sem("b2_loaded"), sem("inputs_transposed"), sem("inputs_copied"), sem("hidden_ready"), sem("hidden_done"), sem("y_ready"), sem("y_done")
        s_ys = [sem(f"y_stored{i}") for i in range(2)]
        WIDTH = (512, CAP - 512)
        HG = 2 * FT
        IG = DC * CT // 4

        with nc.Block() as block:
            @block.sync
            def _(sp):
                sp.dma_start(b2_all, b2.partition_broadcast(P)).then_inc(s_b2, 16)

                def load(e, s):
                    wait(sp, s_y, CT * (e - 1))
                    ei = span(e, 1)
                    sp.dma_start(w1_sb[:, s, :, :], w1[ei, :, :].rearrange("a (c p) f -> p (a c) f", p=P)).then_inc(s_win[s], 16)
                    sp.dma_start(w2_sb[:, s, :].rearrange("p (f d) -> p f d", d=D), w2[ei, :, :].rearrange("a (f p) d -> p (a f) d", p=P)).then_inc(s_win[s], 16)
                    sp.dma_start(rows_in[:, s, :].rearrange("p (t c) -> p t c", c=D),
                                 moe_in[span(e * SLOTS, SLOTS), :].rearrange("(t p) c -> p t c", p=P)).then_inc(s_win[s], 16)

                def store(e, s):
                    for j in range(CT):
                        wait(sp, s_yc, CT * e + j + 1)
                        sp.dma_start(moe_out[span(e * SLOTS + j * P, P), :], y_sb[:, j % 2, :]).then_inc(s_ys[j % 2], 16)
                load(0, 0)
                load(1, 1)
                store(0, 0)
                with sp.Fori(1, NE // 2) as i:
                    load(2 * i, 0)
                    store(2 * i - 1, 1)
                    load(2 * i + 1, 1)
                    store(2 * i, 0)
                store(NE - 1, 1)
                for q in range(2):
                    sp.wait_ge(s_ys[q], 16 * NE * CT // 2)

            @block.tensor
            def _(pe):
                def expert_(e, s):
                    wait(pe, s_win[s], 48 * ((e - s) // 2 + 1) if isinstance(e, int) else 24 * (e - s) + 48)
                    for q in range(IG):
                        wait(pe, s_itc, IG * e + q - 1)
                        for k in range(4):
                            c, j = (4 * q + k) // CT, (4 * q + k) % CT
                            mm = pe.transpose(psum[:, q % 2, k * P:(k + 1) * P], rows_in[:, s, j * D + c * P:j * D + (c + 1) * P], ident[:, :])
                        mm.then_inc(s_it, 1)
                    wait(pe, s_itc, IG * e + IG)
                    for f in range(FT):
                        for n in range(2):
                            G = HG * e + 2 * f + n
                            bank = 2 + (2 * f + n) % 4
                            wait(pe, s_hc, G - 3)
                            for c in range(DC):
                                mm = pe.matmul(psum[:, bank, 0:WIDTH[n]], w1_sb[:, s, c, f * P:(f + 1) * P], inT[:, c, n * 512:n * 512 + WIDTH[n]],
                                               start=(c == 0), stop=(c == DC - 1))
                            mm.then_inc(s_hid, 1)
                    wait(pe, s_hc, HG * e + HG)
                    for j in range(CT):
                        wait(pe, s_yc, CT * e + j - 1)
                        for f in range(FT):
                            mm = pe.matmul(psum[:, 6 + j % 2, 0:D], hid[:, f, j * P:(j + 1) * P], w2_sb[:, s, f * D:(f + 1) * D],
                                           start=(f == 0), stop=(f == FT - 1))
                        mm.then_inc(s_y, 1)
                expert_(0, 0)
                expert_(1, 1)
                with pe.Fori(1, NE // 2) as i:
                    expert_(2 * i, 0)
                    expert_(2 * i + 1, 1)

            @block.scalar
            def _(act):
                def expert_(e):
                    for q in range(IG):
                        wait(act, s_it, IG * e + q + 1)
                        wait(act, s_hid, HG * e)
                        c, j = 4 * q // CT, 4 * q % CT
                        act.copy(inT[:, c, j * P:(j + 4) * P], psum[:, q % 2, :]).then_inc(s_itc, 1)
                    for f in range(FT):
                        for n in range(2):
                            G = HG * e + 2 * f + n
                            bank = 2 + (2 * f + n) % 4
                            hold(act, s_hid, G + 1, s_held)
                            hold(act, s_y, CT * e, s_held)
                            act.activation(hid[:, f, n * 512:n * 512 + WIDTH[n]], psum[:, bank, 0:WIDTH[n]], ACT.Relu,
                                           bias=b1T[:, span(e * FT + f, 1)]).then_inc(s_hc, 1)
                expert_(0)
                with act.Fori(1, NE) as i:
                    expert_(i)

            @block.vector
            def _(v):
                def expert_(e):
                    for j in range(CT):
                        wait(v, s_y, CT * e + j + 1)
                        wait(v, s_ys[j % 2], 16 * (CT // 2 * e + j // 2))
                        v.tensor_tensor(y_sb[:, j % 2, :], psum[:, 6 + j % 2, 0:D], at(b2_all, e), ALU.add).then_inc(s_yc, 1)
                v.wait_ge(s_b2, 16)
                expert_(0)
                with v.Fori(1, NE) as i:
                    expert_(i)

        GROUP = 7
        GROUPS_OUT = NT // GROUP
        assert GROUPS_OUT * GROUP == NT
        m = Arena()
        got = m.take(2, GROUP, D)
        y = m.take(2, GROUP, D)
        high = m.take(GROUP, D)
        bad = m.take(GROUP, D)
        fine = m.take(GROUP, D)
        s_got = [sem(f"results_in{p}") for p in range(2)]
        s_rd, s_o = sem("results_read"), sem("out_ready")
        s_os = [sem(f"out_stored{p}") for p in range(2)]

        with nc.Block() as block:
            @block.gpsimd
            def _(g):
                for i in range(GROUPS_OUT):
                    wait(g, s_rd, i - 1)
                    for u in range(GROUP):
                        t = GROUP * i + u
                        g.indirect_dma_start(got[:, i % 2, u, :], None, moe_out,
                                             bass.IndirectOffsetOnAxis(ap=slot_in[:, t:t + 1], axis=0)).then_inc(s_got[i % 2], 16)

            @block.vector
            def _(v):
                for i in range(GROUPS_OUT):
                    wait(v, s_got[i % 2], 16 * GROUP * (i // 2 + 1))
                    wait(v, s_os[i % 2], 16 * (i // 2))
                    yg = y[:, i % 2, :, :]
                    for u in range(GROUP):
                        t = GROUP * i + u
                        ins = v.tensor_scalar(yg[:, u, :], got[:, i % 2, u, :], gate_prob[:, t:t + 1], None, ALU.mult)
                        if u < GROUP - 1:
                            dve.done(ins)
                    ins.then_inc(s_rd, 1)
                    dve.wait()
                    wait(v, s_rd, i + 1)
                    dve.done(v.tensor_scalar(high, yg, FLOAT_MAX, None, ALU.is_gt))
                    dve.then(v.tensor_scalar(fine, yg, 0.0, 0.0, ALU.mult, ALU.is_equal))
                    dve.then(v.scalar_tensor_tensor(out=bad, in0=yg, scalar=-FLOAT_MAX, in1=high, op0=ALU.is_lt, op1=ALU.subtract))
                    dve.then(v.tensor_scalar(bad, bad, -1.0e4, None, ALU.mult))
                    dve.then(v.copy_predicated(bad, fine.bitcast(I32), yg))
                    v.tensor_tensor(yg, bad, x_all[:, GROUP * i:GROUP * (i + 1), :], ALU.add).then_inc(s_o, 1)
                    wait(v, s_o, i + 1)

            @block.sync
            def _(sp):
                for i in range(GROUPS_OUT):
                    sp.wait_ge(s_o, i + 1)
                    full = GROUP if i < GROUPS_OUT - 1 else GROUP - 1
                    first = GROUP * i * P
                    sp.dma_start(out[first:first + full * P, :].rearrange("(t p) c -> p t c", p=P), y[:, i % 2, 0:full, :]).then_inc(s_os[i % 2], 16)
                    if full < GROUP:
                        sp.dma_start(out[(NT - 1) * P:N, :], y[0:TAIL, i % 2, GROUP - 1, :]).then_inc(s_os[i % 2], 16)
                last = (GROUPS_OUT - 1) % 2
                sp.wait_ge(s_os[last], 16 * ((GROUPS_OUT + 1) // 2 + 1))
                sp.wait_ge(s_os[1 - last], 16 * (GROUPS_OUT // 2))


_INS = ['x', 'src', 'dst', 'L0_gnn_W_s', 'L0_gnn_W_t', 'L0_gnn_W_attn', 'L0_gnn_W_fc', 'L0_gnn_b_fc', 'L0_mix_w_qkv',
        'L0_mix_w_out', 'L0_mix_b_out', 'L0_ffn_gate_w', 'L0_ffn_gate_b', 'L0_ffn_w1', 'L0_ffn_b1', 'L0_ffn_w2',
        'L0_ffn_b2']


def kernel(**inputs):
    import numpy as _np
    import concourse.bacc as _bacc
    from concourse import mybir as _mybir
    from concourse.bass_utils import run_bass_kernel_spmd as _run

    nc = _bacc.Bacc("TRN2", target_bir_lowering=False, num_devices=1)
    arrays, args = {}, []
    for name in _INS:
        a = _np.ascontiguousarray(inputs[name])
        arrays[f"in_{name}_dram"] = a
        args.append(nc.dram_tensor(f"in_{name}_dram", a.shape, _mybir.dt.from_np(a.dtype), kind="ExternalInput").ap())
    args.append(nc.dram_tensor("out_0_dram", tuple(inputs['x'].shape), _mybir.dt.float32, kind="ExternalOutput").ap())
    graph_transformer_kernel(nc, *args)
    r = _run(nc, [arrays], core_ids=[0])
    return r.results[0]["out_0_dram"]
```
